# Optimizing a Trainium2 kernel written in Bass

```python
import numpy as np
import jax
import jax.numpy as jnp

def _softmax(x, axis=-1):
    return jax.nn.softmax(x, axis=axis)

def _gelu(x):
    return jax.nn.gelu(x, approximate=True)

def _silu(x):
    return jax.nn.silu(x)

def _sigmoid(x):
    return jax.nn.sigmoid(x)

def _layernorm(x, axis=-1, eps=1e-05):
    m = jnp.mean(x, axis=axis, keepdims=True)
    v = jnp.var(x, axis=axis, keepdims=True)
    return (x - m) / jnp.sqrt(v + eps)

def _scatter_add(tgt, idx, src, axis=0):
    return tgt.at[idx].add(src)

def _segment_sum(src, seg, n):
    return jax.ops.segment_sum(src, seg, n)
kernel_name = 'mk_xattn_ffn_d1_seqx_r4_2b2fab'

def setup_inputs(seed: int=0):
    np.random.seed(seed)
    _w = jnp.asarray

    def _rec_inputs():
        import jax
        import jax.numpy as jnp
        _rk = jax.random.key(seed)
        x = -0.0002928 + 1 * jax.random.normal(jax.random.fold_in(_rk, 1), (16, 128, 256), jnp.float32)
        _lenS = 128 - jax.random.randint(jax.random.fold_in(_rk, 7), (16,), 0, max(1, 128 // 4) + 1, jnp.int32)
        _lenS2 = 128 - jax.random.randint(jax.random.fold_in(_rk, 8), (16,), 0, max(1, 128 // 4) + 1, jnp.int32)
        _ctx_1024P = jax.random.normal(jax.random.fold_in(_rk, 11), (16, 16, 256), jnp.float32)
        _ctx_1024c = jax.random.dirichlet(jax.random.fold_in(_rk, 511), 0.3 * jnp.ones((16,), jnp.float32), (16, 128))
        _ctx_1024t = jnp.einsum('bsk,bkd->bsd', _ctx_1024c, _ctx_1024P)
        _ctx_1024t = _ctx_1024t * jax.lax.rsqrt(jnp.mean(jnp.square(_ctx_1024t)) + 1e-12) * 0.953939
        ctx_1024 = -1.39393e-06 + 0.999914 * (_ctx_1024t + 0.3 * jax.random.normal(jax.random.fold_in(_rk, 611), (16, 128, 256), jnp.float32))
        _validS = jnp.arange(128)[None, :] < _lenS[:, None]
        _validS2 = jnp.arange(128)[None, :] < _lenS2[:, None]
        _causal = jnp.tril(jnp.ones((128, 128), dtype=bool))
        mask_Bx1x1xS2_ik0 = jnp.where(jnp.broadcast_to(_validS2[:, None, None, :], (16, 1, 1, 128)), 0, 1).astype(jnp.int32)
        mask_1x1xSxS2_ik0 = jnp.where(jnp.broadcast_to(_validS2[0:1, None, None, :], (1, 1, 128, 128)), 0, 1).astype(jnp.int32)
        return (x, ctx_1024, mask_Bx1x1xS2_ik0, mask_1x1xSxS2_ik0)
    x, ctx_1024, mask_Bx1x1xS2_ik0, mask_1x1xSxS2_ik0 = _rec_inputs()

    def _L0_xattn_setup():
        import jax, jax.numpy as jnp
        import numpy as np
        E, H = (256, 16)
        N, S, T = (2, 512, 512)
        key = jax.random.key(seed)
        ks = jax.random.split(key, 8)
        scale = 1.0 / np.sqrt(E)
        q = jax.random.normal(ks[0], (N, S, E), dtype=jnp.float32)
        k = jax.random.normal(ks[1], (N, T, E), dtype=jnp.float32)
        v = jax.random.normal(ks[2], (N, T, E), dtype=jnp.float32)
        pad_mask = jax.random.randint(ks[3], (N, 1, 1, T), 0, 2, dtype=jnp.int32)
        subsq_mask = jnp.tril(jnp.ones((S, T), dtype=jnp.int32))[None, None]
        Wq = jax.random.normal(ks[4], (E, E), dtype=jnp.float32) * scale
        Wk = jax.random.normal(ks[5], (E, E), dtype=jnp.float32) * scale
        Wv = jax.random.normal(ks[6], (E, E), dtype=jnp.float32) * scale
        bq = jnp.zeros((E,), dtype=jnp.float32)
        bk = jnp.zeros((E,), dtype=jnp.float32)
        bv = jnp.zeros((E,), dtype=jnp.float32)
        return {'query': q, 'key': k, 'value': v, 'pad_mask': pad_mask, 'subsq_mask': subsq_mask, 'Wq': Wq, 'bq': bq, 'Wk': Wk, 'bk': bk, 'Wv': Wv, 'bv': bv}
    _L0_xattn_all = _L0_xattn_setup()
    _L0_xattn_in = {k: v for k, v in _L0_xattn_all.items() if k in ('Wq', 'bq', 'Wk', 'bk', 'Wv', 'bv')}
    del _L0_xattn_all

    def _L0_ffn_setup():
        import jax, jax.numpy as jnp
        import numpy as np
        D = 256
        E = 12
        HS = 2 * D
        HR = 3 * D
        TAU = 1.5

        def _geglu(h):
            a, g = jnp.split(h, 2, axis=-1)
            return a * jax.nn.gelu(g, approximate=False)
        key = jax.random.key(seed)
        ks = jax.random.split(key, 12)

        def xavier(k, shape):
            fan_in, fan_out = (shape[-2], shape[-1])
            lim = jnp.sqrt(6.0 / (fan_in + fan_out))
            return jax.random.uniform(k, shape, jnp.float32, -lim, lim)
        x = jax.random.normal(ks[0], (2, 256, D), jnp.float32)
        Ws1 = xavier(ks[1], (D, 2 * HS))
        bs1 = jnp.zeros((2 * HS,), jnp.float32)
        Ws2 = xavier(ks[2], (HS, D))
        bs2 = jnp.zeros((D,), jnp.float32)
        We1 = xavier(ks[3], (E, D, 2 * HR))
        be1 = jnp.zeros((E, 2 * HR), jnp.float32)
        We2 = xavier(ks[4], (E, HR, D))
        be2 = jnp.zeros((E, D), jnp.float32)
        Wr = xavier(ks[5], (D, E))
        br = jnp.zeros((E,), jnp.float32)
        return {'x': x, 'Ws1': Ws1, 'bs1': bs1, 'Ws2': Ws2, 'bs2': bs2, 'We1': We1, 'be1': be1, 'We2': We2, 'be2': be2, 'Wr': Wr, 'br': br}
    _L0_ffn_all = _L0_ffn_setup()
    _L0_ffn_in = {k: v for k, v in _L0_ffn_all.items() if k in ('Ws1', 'bs1', 'Ws2', 'bs2', 'We1', 'be1', 'We2', 'be2', 'Wr', 'br')}
    del _L0_ffn_all
    return {'x': x, 'ctx_1024': ctx_1024, 'mask_Bx1x1xS2_ik0': mask_Bx1x1xS2_ik0, 'mask_1x1xSxS2_ik0': mask_1x1xSxS2_ik0, 'L0_xattn_Wq': _L0_xattn_in['Wq'], 'L0_xattn_bq': _L0_xattn_in['bq'], 'L0_xattn_Wk': _L0_xattn_in['Wk'], 'L0_xattn_bk': _L0_xattn_in['bk'], 'L0_xattn_Wv': _L0_xattn_in['Wv'], 'L0_xattn_bv': _L0_xattn_in['bv'], 'L0_ffn_Ws1': _L0_ffn_in['Ws1'], 'L0_ffn_bs1': _L0_ffn_in['bs1'], 'L0_ffn_Ws2': _L0_ffn_in['Ws2'], 'L0_ffn_bs2': _L0_ffn_in['bs2'], 'L0_ffn_We1': _L0_ffn_in['We1'], 'L0_ffn_be1': _L0_ffn_in['be1'], 'L0_ffn_We2': _L0_ffn_in['We2'], 'L0_ffn_be2': _L0_ffn_in['be2'], 'L0_ffn_Wr': _L0_ffn_in['Wr'], 'L0_ffn_br': _L0_ffn_in['br']}

def reference(x, ctx_1024, mask_Bx1x1xS2_ik0, mask_1x1xSxS2_ik0, L0_xattn_Wq, L0_xattn_bq, L0_xattn_Wk, L0_xattn_bk, L0_xattn_Wv, L0_xattn_bv, L0_ffn_Ws1, L0_ffn_bs1, L0_ffn_Ws2, L0_ffn_bs2, L0_ffn_We1, L0_ffn_be1, L0_ffn_We2, L0_ffn_be2, L0_ffn_Wr, L0_ffn_br):
    import jax
    import jax.numpy as jnp

    def _L0_xattn_ref(query, key, value, pad_mask, subsq_mask, Wq, bq, Wk, bk, Wv, bv):
        import jax, jax.numpy as jnp
        import numpy as np
        E, H = (256, 16)
        N, S, T = (2, 512, 512)
        n, s, e = query.shape
        t = value.shape[1]
        d = e // H
        q = (query @ Wq.T + bq).reshape(n, s, H, d).transpose(0, 2, 1, 3)
        k = (key @ Wk.T + bk).reshape(n, t, H, d).transpose(0, 2, 1, 3)
        v = (value @ Wv.T + bv).reshape(n, t, H, d).transpose(0, 2, 1, 3)
        att = jnp.einsum('bhsd,bhtd->bhst', q, k) / jnp.sqrt(jnp.float32(d))
        att = jnp.where(pad_mask == 0, jnp.float32(-1000000000.0), att)
        att = jnp.where(subsq_mask == 0, jnp.float32(-1000000000.0), att)
        prob = jax.nn.softmax(att, axis=-1)
        out = jnp.einsum('bhst,bhtd->bhsd', prob, v)
        return out.transpose(0, 2, 1, 3).reshape(n, s, e)

    def _L0_ffn_ref(x, Ws1, bs1, Ws2, bs2, We1, be1, We2, be2, Wr, br):
        import jax, jax.numpy as jnp
        import numpy as np
        D = 256
        E = 12
        HS = 2 * D
        HR = 3 * D
        TAU = 1.5

        def _geglu(h):
            a, g = jnp.split(h, 2, axis=-1)
            return a * jax.nn.gelu(g, approximate=False)
        B, T, Dm = x.shape
        xf = x.reshape(-1, Dm)
        ys = _geglu(xf @ Ws1 + bs1) @ Ws2 + bs2
        logits = (xf @ Wr + br) / TAU
        top_val, top_idx = jax.lax.top_k(logits, 2)
        top_w = jax.nn.softmax(top_val, axis=-1)
        onehot = jax.nn.one_hot(top_idx, E, dtype=x.dtype)
        w = jnp.einsum('nke,nk->ne', onehot, top_w)
        h = jnp.einsum('nd,edh->enh', xf, We1) + be1[:, None, :]
        act = _geglu(h)
        yE = jnp.einsum('enh,ehd->end', act, We2) + be2[:, None, :]
        yr = jnp.einsum('end,ne->nd', yE, w)
        return (ys + yr).reshape(B, T, Dm)
    x = x + _L0_xattn_ref(_layernorm(x, axis=-1), ctx_1024, ctx_1024, mask_Bx1x1xS2_ik0, mask_1x1xSxS2_ik0, L0_xattn_Wq, L0_xattn_bq, L0_xattn_Wk, L0_xattn_bk, L0_xattn_Wv, L0_xattn_bv)
    x = x + _L0_ffn_ref(_layernorm(x, axis=-1), L0_ffn_Ws1, L0_ffn_bs1, L0_ffn_Ws2, L0_ffn_bs2, L0_ffn_We1, L0_ffn_be1, L0_ffn_We2, L0_ffn_be2, L0_ffn_Wr, L0_ffn_br)
    return x

_drawn_inputs = setup_inputs


def setup_inputs(seed=0):
    import zlib

    import numpy as np

    out = dict(_drawn_inputs(seed))
    spreads = {'L0_xattn_bq': (0.0, 0.1),
     'L0_xattn_bk': (0.0, 0.1),
     'L0_xattn_bv': (0.0, 0.1),
     'L0_ffn_bs1': (0.0, 0.1),
     'L0_ffn_bs2': (0.0, 0.1),
     'L0_ffn_be1': (0.0, 0.1),
     'L0_ffn_be2': (0.0, 0.1),
     'L0_ffn_br': (0.0, 0.1)}
    factors = {}
    for name, (base, spread) in spreads.items():
        noise = np.random.default_rng([zlib.crc32(name.encode()), seed]).standard_normal(out[name].shape)
        drawn = base * np.exp(spread * noise) if base else spread * noise
        out[name] = jnp.asarray(drawn.astype(out[name].dtype))
    for name, factor in factors.items():
        out[name] = (out[name] * factor).astype(out[name].dtype)
    return out
```

```python
import concourse.bass as bass
from concourse import mybir

P = 128
B, S, D = 16, 128, 256
H, HD = 16, 16
N = B * S
PAIRS = B // 2
E = 12
HR, HS = 3 * D, 2 * D
KC = D // P
TAU = 1.5
EPS = 1e-5
FILL = -1e30
TILES = N // P
SLOTS = (2 * N + (P - 1) * E + (E - 2)) // P
RING = 3
W1R, W2R = KC * 2 * HR, (HR // P) * D
W1S, W2S = KC * 2 * HS, (HS // P) * D
SLOT_W = 2 * (W1R + W2R)
VW = HD + 1
ROWS = E + 2
BW = 2 * HR + D
SHARED_ROW, V_ROW = E, E + 1
C_ID, C_UP = 0, P
C_LOQ = 2 * P
C_LOB = C_LOQ + 1
C_ROW = C_LOB + 1
C_RANK = C_ROW + 1
C_SLOT = C_RANK + E
C_STEP = C_SLOT + SLOTS
C_ALL = C_STEP + E - 1


def build(nc, x_d, ctx_d, pad_d, sub_d, wq_d, wk_d, wv_d, bq_d, bk_d, bias_d, ws1_d, ws2_d, w1_d,
          w2_d, wr_d, br_d, const_d, out_d):
    f32, f32r = mybir.dt.float32, mybir.dt.float32r
    bf16, i32 = mybir.dt.bfloat16, mybir.dt.int32
    ALU, ACT, AX = mybir.AluOpType, mybir.ActivationFunctionType, mybir.AxisListType
    vec, act, pool, pe_ = nc.vector, nc.scalar, nc.gpsimd, nc.tensor

    xn2_dram = nc.dram_tensor("xn2_dram", (N, D), f32, kind="Internal").ap()
    rows_in = nc.dram_tensor("rows_in", (SLOTS * P, D), f32, kind="Internal").ap()
    rows_out = nc.dram_tensor("rows_out", (SLOTS * P, D), f32, kind="Internal").ap()

    at = [((nc.sbuf_base + 63) // 64) * 64]

    def size(shape, dt):
        n = 1
        for k in shape[1:]:
            n *= k
        return n * (2 if dt == bf16 else 4)

    offset_of = {}

    def put(name, shape, dt, where=at):
        t = nc.alloc_sbuf_tensor_at(name, shape, dt, offset=where[0])
        offset_of[name] = where[0]
        where[0] += (size(shape, dt) + 31) // 32 * 32
        return t

    x_all = put("x_all", [P, TILES * D], f32)
    xn2_all = put("xn2_all", [P, TILES * D], f32)
    const = put("const", [P, C_ALL], f32)
    bias_tab = put("bias_tab", [2 * ROWS, BW], f32r)
    ident_b = put("ident_b", [P, P], bf16)
    upper_b = put("upper_b", [P, P], bf16)
    ones_b = put("ones_b", [P, P], bf16)
    sel_v = put("sel_v", [2 * ROWS, P], f32r)
    sel_s = put("sel_s", [2 * ROWS, P], f32r)
    sel_up = put("sel_up", [2 * ROWS, P], f32r)
    sel_down = put("sel_down", [2 * ROWS, P], f32r)
    wr = put("wr", [P, KC, E], f32)
    br = put("br", [P, E], f32)
    logits = put("logits", [P, TILES, E], f32)
    xrow = put("xrow", [P, D], f32)
    half = put("half", [P, 2], f32)
    eps = put("eps", [P, 2], f32)
    tick = put("tick", [P, 1], f32)
    ptick = put("ptick", [P, 1], f32)
    bn1 = put("bn1", [P, 2, 6], f32)
    mv1 = put("mv1", [P, 2, 2], f32)
    ve1 = put("ve1", [P, 2], f32)
    rs1 = put("rs1", [P, 2], f32)
    bn2 = put("bn2", [P, 2, 6], f32)
    mv2 = put("mv2", [P, 2, 2], f32)
    ve2 = put("ve2", [P, 2], f32)
    rs2 = put("rs2", [P, 2], f32)
    w_top = put("w_top", [P, 2, TILES], f32)
    idx_top = put("idx_top", [P, 2, TILES], i32)
    tab_ring = put("tab_ring", [P, SLOTS], i32)
    tab_need = put("tab_need", [P, SLOTS], i32)
    tab_cum = put("tab_cum", [P, E], i32)
    sel_ind = put("sel_ind", [2 * ROWS, SLOTS], f32)
    stage1 = put("stage1", [P, W1R], f32)
    stage2 = put("stage2", [P, W2R], f32)
    ring = put("ring", [P, RING, SLOT_W], f32r)
    ring_at = at[0] - RING * SLOT_W * 4
    work_at = [at[0]]
    xTh = put("xTh", [P, KC, P], f32r)
    xTl = put("xTl", [P, KC, P], f32r)
    gel = [put(f"gel{u}", [P, HR // 2], f32) for u in range(2)]
    hid = [put(f"hid{u}", [P, HR // 2], f32) for u in range(2)]
    hTh = [put(f"hTh{u}", [P, 3, P], f32r) for u in range(2)]
    hTl = [put(f"hTl{u}", [P, 3, P], f32r) for u in range(2)]
    y_row = put("y_row", [P, D], f32)
    own = [at[0]]
    pad_b = put("pad_b", [P, B * S], i32, own)
    mask_b = put("mask_b", [P, B, S], bf16, own)
    xn2p = put("xn2p", [P, 2, D], f32, own)
    cbuf = put("cbuf", [P, 2, D], f32, own)
    assert own[0] <= nc.sbuf_top, own[0] - nc.sbuf_top
    low = [ring_at]
    wqh = put("wqh", [P, KC, 512], f32r, low)
    wql = put("wql", [P, KC, 512], f32r, low)
    wkh = put("wkh", [P, KC, 512], f32r, low)
    wkl = put("wkl", [P, KC, 512], f32r, low)
    wvh = put("wvh", [P, KC, D], f32r, low)
    wvl = put("wvl", [P, KC, D], f32r, low)
    aTh = [put(f"aTh{i}", [P, KC, 256], f32r, low) for i in range(2)]
    aTl = [put(f"aTl{i}", [P, KC, 256], f32r, low) for i in range(2)]
    q_st = [put(f"q_st{i}", [P, 4, 256], f32r, low) for i in range(2)]
    k_hi = [put(f"k_hi{i}", [P, 4, 256], f32r, low) for i in range(2)]
    k_lo = [put(f"k_lo{i}", [P, 4, 256], f32r, low) for i in range(2)]
    q_cut = put("q_cut", [P, 2, 256], f32r, low)
    v_sb = [put(f"v_sb{i}", [P, 2, H, VW], f32, low) for i in range(2)]
    prob = [put(f"prob{i}", [P, 2, 4, P], f32, low) for i in range(2)]
    probT = put("probT", [P, 2, 4, P], f32, low)
    assert low[0] <= ring_at + 2 * SLOT_W * 4, low[0] - ring_at - 2 * SLOT_W * 4
    wk1 = [work_at[0]]
    xn1 = put("xn1", [P, 2, D], f32, wk1)
    att = put("att", [P, D], f32, wk1)
    rden = put("rden", [P, H], f32, wk1)
    nmax = put("nmax", [P, 2, 4], f32, wk1)
    bqs = put("bqs", [P, 4], f32, wk1)
    bqc = put("bqc", [P, 4], f32, wk1)
    bks = put("bks", [P, 4], f32, wk1)
    xn2T = put("xn2T", [P, KC, 256], f32, wk1)
    sub_b = put("sub_b", [P, S], i32, wk1)
    keep_s = put("keep_s", [P, S], f32, wk1)
    assert wk1[0] <= at[0]
    pro = [offset_of["stage1"]]
    wq_raw = put("wq_raw", [P, KC, 512], f32, pro)
    wk_raw = put("wk_raw", [P, KC, 512], f32, pro)
    wv_raw = put("wv_raw", [P, KC, D], f32, pro)
    pr2 = [offset_of["prob0"]]
    bias_raw = put("bias_raw", [2 * ROWS, BW], f32, pr2)
    pr3 = [offset_of["xn2_all"]]
    bias_cut = put("bias_cut", [2 * ROWS, BW], f32r, pr3)
    keep = put("keep", [P, B, S], f32, pr3)
    rt = [offset_of["pad_b"]]
    lg = put("lg", [P, TILES, E], f32, rt)
    eq = put("eq", [P, TILES, E], f32, rt)
    pick1 = put("pick1", [P, TILES, E], f32, rt)
    pick2 = put("pick2", [P, TILES, E], f32, rt)
    chosen = put("chosen", [P, TILES, E], bf16, rt)
    pos = put("pos", [P, TILES, E], f32, rt)
    top = put("top", [P, 2, TILES], f32, rt)
    best = put("best", [P, TILES], f32, rt)
    ex = put("ex", [P, TILES], f32, rt)
    cnt_i = put("cnt_i", [P, E], i32, rt)
    cnt_s = put("cnt_s", [P, E], i32, rt)
    tiles_e = put("tiles_e", [P, E], f32, rt)
    cum_e = put("cum_e", [P, E], f32, rt)
    base_e = put("base_e", [P, E], f32, rt)
    ones_e = put("ones_e", [P, E], f32, rt)
    past = put("past", [P, SLOTS, E - 1], f32, rt)
    past2 = put("past2", [P, SLOTS, E - 1], f32, rt)
    slot_e = put("slot_e", [P, SLOTS], f32, rt)
    slot_r = put("slot_r", [P, SLOTS], f32, rt)
    assert rt[0] <= nc.sbuf_top
    ga = [ring_at]
    gath = put("gath", [P, TILES, 2, D], f32, ga)

    ident = const[:, C_ID:C_ID + P]

    ps_s = nc.alloc_psum_tensor("ps_s", [P, 4, 512], f32)
    ps_t = nc.alloc_psum_tensor("ps_t", [P, 2, 512], f32)
    ps_o = nc.alloc_psum_tensor("ps_o", [P, 512], f32)
    ps_x = nc.alloc_psum_tensor("ps_x", [P, 512], f32)

    def sem(name):
        return nc.alloc_semaphore(name)

    const_in, x_in, x_rest_in, ctx_in, wq_in, wk_in, wv_in = map(sem, (
        "const_in", "x_in", "x_rest_in", "ctx_in", "wq_in", "wk_in", "wv_in"))
    bias_in, mask_in, misc_in, zero_out, shared_in = map(sem, (
        "bias_in", "mask_in", "misc_in", "zero_out", "shared_in"))
    consts_ready, masks_ready, w_hi, w_ready, bias_cut_done, bias_ready = map(sem, (
        "consts_ready", "masks_ready", "w_hi", "w_ready", "bias_cut_done", "bias_ready"))
    scores_ready, shifted, maxed, exp_done, pt_ready, pt_copied, pv_done, normed = map(sem, (
        "scores_ready", "shifted", "maxed", "exp_done", "pt_ready", "pt_copied", "pv_done", "normed"))
    xb_ready, xb_hi, xb_free, ln1_var, ln1_rs, ln2_var, ln2_rs, xn1_ready, xn2_ready, xn2_saved = map(sem, (
        "xb_ready", "xb_hi", "xb_free", "ln1_var", "ln1_rs", "ln2_var", "ln2_rs", "xn1_ready",
        "xn2_ready", "xn2_saved"))
    vstep, mstep, nstep, ln1_bn, pstep, pstep2, pconv = map(sem, (
        "vstep", "mstep", "nstep", "ln1_bn", "pstep", "pstep2", "pconv"))
    zero_ready = sem("zero_ready")
    chosen_ready, ranks_ready, tables_ready, rows_ready, scattered, ex_ready, gap_ready = map(sem, (
        "chosen_ready", "ranks_ready", "tables_ready", "rows_ready", "scattered", "ex_ready", "gap_ready"))
    xrow_in, xt_ready, xt_hi, xt_lo = map(sem, ("xrow_in", "xt_ready", "xt_hi", "xt_lo"))
    up_ready = [sem("up_ready0"), sem("up_ready1")]
    gelu_done = [sem("gelu_done0"), sem("gelu_done1")]
    hid_done = [sem("hid_done0"), sem("hid_done1")]
    ht_ready = [sem("ht_ready0"), sem("ht_ready1")]
    ht_hi = [sem("ht_hi0"), sem("ht_hi1")]
    ht_lo = [sem("ht_lo0"), sem("ht_lo1")]
    y_ready, y_done, y_out, sel_up_ready, sel_down_ready = map(sem, (
        "y_ready", "y_done", "y_out", "sel_up_ready", "sel_down_ready"))
    raw1_in, raw2_in, conv_hi, converted = map(sem, ("raw1_in", "raw2_in", "conv_hi", "converted"))
    gathered = [sem(f"gathered{t}") for t in range(TILES)]
    combined, stored = sem("combined"), sem("stored")

    PLAN = [["xT", "cT"], ["q0", "q1"], ["k0", "r"], ["k1", "l", "v"]]
    HI = ["xT", "cT", "q0", "q1", "k0", "k1"]
    PROJ = ["xT", "cT", "q0", "q1", "k0", "k1", "v"]

    def steps(n, first, last):
        return [s for s in PLAN[n] if (s not in "rl" or not first) and (s in "rl" or not last)]

    def before(p, n, k, first, last):
        base = len(PROJ) if first else 9 * p + 5
        return base + sum(len(steps(m, first, last)) for m in range(n)) + k

    def each_pair(eng, body):
        body(0, 0, True, False)
        with eng.Fori(0, (PAIRS - 4) // 2) as i:
            body(i * 2 + 1, 1, False, False)
            body(i * 2 + 2, 0, False, False)
        body(PAIRS - 3, 1, False, False)
        body(PAIRS - 2, 0, False, False)
        body(PAIRS - 1, 1, False, True)

    UNITS = 4 * PAIRS
    PAIR_STEPS_END = 9 * (PAIRS - 1) + 5 + 2

    block = nc.Block()
    with block:

        @block.sync
        def _(sp):
            sp.dma_start(const[:, :], const_d).then_inc(const_in, 16)
            sp.dma_start(x_all[:, 0:4 * D].rearrange("p (t d) -> p t d", d=D),
                         x_d[0:4 * P, :].rearrange("(t p) d -> p t d", p=P)).then_inc(x_in, 16)
            sp.dma_start(cbuf[:, :, :], ctx_d[0:2 * P, :].rearrange("(t p) d -> p t d", p=P)).then_inc(ctx_in, 16)
            sp.dma_start(wq_raw[:, :, :], wq_d.rearrange("(c p) n -> p c n", p=P)).then_inc(wq_in, 16)
            sp.dma_start(wk_raw[:, :, :], wk_d.rearrange("(c p) n -> p c n", p=P)).then_inc(wk_in, 16)
            sp.dma_start(wv_raw[:, :, :], wv_d.rearrange("(c p) n -> p c n", p=P)).then_inc(wv_in, 16)
            sp.dma_start(x_all[:, 4 * D:].rearrange("p (t d) -> p t d", d=D),
                         x_d[4 * P:, :].rearrange("(t p) d -> p t d", p=P)).then_inc(x_rest_in, 16)
            sp.wait_ge(w_ready, 3)
            sp.dma_start(stage1[:, 0:W1S].rearrange("p (c n) -> p c n", c=KC),
                         ws1_d.rearrange("(c p) n -> p c n", p=P)).then_inc(shared_in, 16)
            sp.dma_start(stage2[:, 0:W2S].rearrange("p (c n) -> p c n", n=D),
                         ws2_d.rearrange("(c p) n -> p c n", p=P)).then_inc(shared_in, 16)

            def load_ctx(pp):
                sp.dma_start(cbuf[:, :, :], ctx_d[bass.ds(pp * 2 * P, 2 * P), :]
                             .rearrange("(t p) d -> p t d", p=P)).then_inc(ctx_in, 16)

            sp.wait_ge(xb_ready, 2)
            load_ctx(1)

            def save_xn2(q):
                sp.wait_ge(xn2_ready, q + 1)
                sp.dma_start(xn2_all[:, bass.ds(q * 2 * D, 2 * D)], xn2p[:, :, :].rearrange("p t d -> p (t d)")).then_inc(xn2_saved, 16)
                sp.dma_start(xn2_dram[bass.ds(q * 2 * P, 2 * P), :].rearrange("(t p) d -> p t d", p=P),
                             xn2p[:, :, :]).then_inc(xn2_saved, 16)

            def pair(p, par, first, last):
                if not last:
                    sp.wait_ge(xb_ready, before(p, 0, 1, first, last) + 1)
                    load_ctx(p + 2)
                if not first:
                    save_xn2(p - 1)

            pair(0, 0, True, False)
            with sp.Fori(0, (PAIRS - 4) // 2) as i:
                pair(i * 2 + 1, 1, False, False)
                pair(i * 2 + 2, 0, False, False)
            pair(PAIRS - 3, 1, False, False)
            save_xn2(PAIRS - 3)
            save_xn2(PAIRS - 2)
            save_xn2(PAIRS - 1)

            def load_row(src, t, s, n):
                if not (isinstance(t, int) and t == 0):
                    sp.wait_ge(xt_ready, t)
                sp.dma_start(xrow[:, :], src[bass.ds(s * P, P), :]).then_inc(xrow_in, 16)

            sp.wait_ge(xn2_saved, 32 * PAIRS)
            load_row(xn2_dram, 0, 0, 0)
            with sp.Fori(1, TILES) as s:
                load_row(xn2_dram, s, s, 0)
            sp.wait_ge(scattered, 16 * 2 * TILES)
            load_row(rows_in, TILES, 0, 0)
            sp.wait_ge(xt_ready, TILES + 1)
            sp.dma_start(xrow[:, :], rows_in[P:2 * P, :]).then_inc(xrow_in, 16)

            def store_y(s):
                sp.wait_ge(y_done, TILES + s + 1)
                sp.dma_start(rows_out[bass.ds(s * P, P), :], y_row[:, :]).then_inc(y_out, 16)

            with sp.Fori(2, SLOTS) as s:
                load_row(rows_in, s + TILES, s, 0)
                store_y(s - 2)
            store_y(SLOTS - 2)
            store_y(SLOTS - 1)
            for t in range(TILES):
                sp.wait_ge(combined, 2 * (t + 1))
                sp.dma_start(out_d[t * P:(t + 1) * P, :], x_all[:, t * D:(t + 1) * D]).then_inc(stored, 16)
            sp.wait_ge(stored, 16 * TILES)

        @block.tensor
        def _(pe):
            def transposes(dst, src, n):
                for c in range(KC):
                    for b in range(n):
                        last = pe_.transpose(dst[:, (c * n + b) * P:(c * n + b + 1) * P],
                                             src[:, b, c * P:(c + 1) * P], ident)
                return last

            def step(s, pp, par, idx):
                pe.wait_ge(xb_free, idx)
                if s == "xT":
                    pe.wait_ge(xn1_ready, pp + 1)
                    last = transposes(ps_x, xn1, 2)
                elif s == "cT":
                    pe.wait_ge(ctx_in, 16 * (pp + 1))
                    last = transposes(ps_x, cbuf, 2)
                elif s[0] in "qk":
                    wh, wl, a = (wqh, wql, 0) if s[0] == "q" else (wkh, wkl, 1)
                    for gg in range(2):
                        cols = slice((2 * int(s[1]) + gg) * P, (2 * int(s[1]) + gg + 1) * P)
                        n = 0
                        for w, t in ((wh, aTh), (wh, aTl), (wl, aTh)):
                            for c in range(KC):
                                last = pe_.matmul(ps_x[:, gg * 256:(gg + 1) * 256], w[:, c, cols], t[a][:, c, :],
                                                  start=n == 0, stop=n == 5)
                                n += 1
                else:
                    for b in range(2):
                        n = 0
                        for t, w in ((aTh, wvh), (aTh, wvl), (aTl, wvh)):
                            for c in range(KC):
                                pe_.matmul(ps_x[:, b * D:(b + 1) * D], t[1][:, c, b * P:(b + 1) * P], w[:, c, :],
                                           start=n == 0, stop=False)
                                n += 1
                        last = pe_.matmul(ps_x[:, b * D:(b + 1) * D], sel_v[:, :], bias_tab[:, 0:D],
                                          start=False, stop=True)
                last.then_inc(xb_ready, 1)

            def router(s, q, idx):
                pe.wait_ge(xb_free, idx)
                if s == "r":
                    pe.wait_ge(xn2_ready, q + 1)
                    last = transposes(ps_x, xn2p, 2)
                else:
                    for b in range(2):
                        for c in range(KC):
                            last = pe_.matmul(ps_x[:, b * E:(b + 1) * E], xn2T[:, c, b * P:(b + 1) * P], wr[:, c, :],
                                              start=c == 0, stop=c == KC - 1)
                last.then_inc(xb_ready, 1)

            def scores(p, par, n):
                b, u = n // 2, n % 2
                U = p * 4 + n
                if not (isinstance(p, int) and p == 0 and n < 2):
                    pe.wait_ge(shifted, U - 1)
                for jj in range(2):
                    j = 2 * u + jj
                    pe_.matmul(ps_s[:, j, :].rearrange("p (g t) -> p g t", g=4), ident_b[:, :],
                               mask_b[:, bass.ds(p * 2 + b, 1), :].broadcast_to([P, 4, P]), start=True, stop=False)
                for jj in range(2):
                    j = 2 * u + jj
                    for g in range(4):
                        for k in (k_hi, k_lo):
                            last = pe_.matmul(ps_s[:, j, g * P:(g + 1) * P],
                                              q_st[par][32 * j:32 * j + 32, g, b * P:(b + 1) * P],
                                              k[par][32 * j:32 * j + 32, g, b * P:(b + 1) * P],
                                              start=False, stop=g == 3 and k is k_lo)
                last.then_inc(scores_ready, 1)

            def prob_transposes(U, n):
                pe.wait_ge(exp_done, U + 1)
                if not (isinstance(U, int) and U == 0):
                    pe.wait_ge(pt_copied, U)
                for jj in range(2):
                    for g in range(4):
                        last = pe_.transpose(ps_t[:, jj, g * P:(g + 1) * P], prob[n % 2][:, jj, g, :], ident)
                last.then_inc(pt_ready, 1)

            def values(U, n, par, batch):
                b, u = n // 2, n % 2
                pe.wait_ge(pt_copied, U + 1)
                if u == 0 and not (isinstance(batch, int) and batch == 0):
                    pe.wait_ge(normed, batch)
                for jj in range(2):
                    for g in range(4):
                        h = 4 * g + 2 * u + jj
                        last = pe_.matmul(ps_o[:, h * VW:(h + 1) * VW], probT[:, jj, g, :], v_sb[par][:, b, h, :],
                                          start=True, stop=True)
                last.then_inc(pv_done, 1)

            pe.wait_ge(consts_ready, 1)
            pe.wait_ge(w_ready, 3)
            pe.wait_ge(bias_ready, 1)
            for k, s in enumerate(PROJ):
                step(s, 0, 0, k)
            pe.wait_ge(masks_ready, 1)
            pe.wait_ge(misc_in, 16 * 4)

            def pair(p, par, first, last):
                for n in range(4):
                    if n == 0:
                        pe.wait_ge(xb_free, before(p, 0, 0, first, last))
                    scores(p, par, n)
                    if not (first and n == 0):
                        prob_transposes(p * 4 + n - 1, (n - 1) % 4)
                    todo = steps(n, first, last)
                    for k, s in enumerate(todo):
                        idx = before(p, n, k, first, last)
                        if s in "rl":
                            router(s, p - 1, idx)
                        else:
                            step(s, p + 1, 1 - par, idx)
                        if k == 0 and not (first and n == 0):
                            values(p * 4 + n - 1, (n - 1) % 4, par if n else 1 - par, p * 2 + n // 2)
                    if not todo and not (first and n == 0):
                        values(p * 4 + n - 1, (n - 1) % 4, par if n else 1 - par, p * 2 + n // 2)

            each_pair(pe, pair)
            prob_transposes(UNITS - 1, 3)
            values(UNITS - 1, 3, 1, B - 1)
            router("r", PAIRS - 1, PAIR_STEPS_END)
            router("l", PAIRS - 1, PAIR_STEPS_END + 1)

            def up(t, s, u, routed, place):
                half_w = (HR if routed else HS) // 2
                w1 = W1R if routed else W1S
                full = 2 * (HR if routed else HS)
                if u == 0:
                    pe.wait_ge(xt_lo, t + 1)
                    if routed:
                        pe.wait_ge(sel_up_ready, s + 1)
                if not (isinstance(t, int) and t == 0):
                    pe.wait_ge(hid_done[u], t)
                for part in range(2):
                    out = ps_s[:, 2 * u + part, 0:half_w]
                    lo_col = part * (full // 2) + u * half_w
                    n = 0
                    for x, off in ((xTh, 0), (xTh, w1), (xTl, 0)):
                        for c in range(KC):
                            a = off + c * full + lo_col
                            pe_.matmul(out, x[:, c, :], weights(place, a, half_w), start=n == 0, stop=False)
                            n += 1
                    sel = sel_up if routed else sel_s
                    last = pe_.matmul(out, sel[:, :], bias_tab[:, lo_col:lo_col + half_w], start=False, stop=True)
                last.then_inc(up_ready[u], 1)

            def weights(place, a, width):
                return ring[:, bass.ds(place, 1), a:a + width].rearrange("p o n -> p (o n)")

            def hid_transposes(t, u, routed):
                nch = (HR if routed else HS) // 2 // P
                pe.wait_ge(hid_done[u], t + 1)
                if not (isinstance(t, int) and t == 0):
                    pe.wait_ge(ht_lo[u], t)
                for c in range(nch):
                    last = pe_.transpose(ps_t[:, u, c * P:(c + 1) * P], hid[u][:, c * P:(c + 1) * P], ident)
                last.then_inc(ht_ready[u], 1)

            def x_transposes(t):
                pe.wait_ge(xrow_in, (t + 1) * 16)
                if not (isinstance(t, int) and t == 0):
                    pe.wait_ge(xt_lo, t)
                for c in range(KC):
                    last = pe_.transpose(ps_x[:, c * P:(c + 1) * P], xrow[:, c * P:(c + 1) * P], ident)
                last.then_inc(xt_ready, 1)

            def down(t, s, routed, place):
                nch = (HR if routed else HS) // 2 // P
                w1 = W1R if routed else W1S
                w2 = W2R if routed else W2S
                pe.wait_ge(ht_lo[0], t + 1)
                pe.wait_ge(ht_lo[1], t + 1)
                if routed:
                    pe.wait_ge(sel_down_ready, s + 1)
                if not (isinstance(t, int) and t == 0):
                    pe.wait_ge(y_done, t)
                n = 0
                for u in range(2):
                    for c in range(nch):
                        for h, off in ((hTh, 2 * w1), (hTh, 2 * w1 + w2), (hTl, 2 * w1)):
                            a = off + (u * nch + c) * D
                            pe_.matmul(ps_o[:, 0:D], h[u][:, c, :], weights(place, a, D), start=n == 0, stop=False)
                            n += 1
                sel = sel_down if routed else sel_s
                lo_col = 2 * HR if routed else 2 * HS
                pe_.matmul(ps_o[:, 0:D], sel[:, :], bias_tab[:, lo_col:lo_col + D], start=False, stop=True)\
                    .then_inc(y_ready, 1)

            pe.wait_ge(chosen_ready, 1)
            pe_.matmul(ps_o[:, 0:TILES * E], upper_b[:, :], chosen[:, :, :].rearrange("p t e -> p (t e)"),
                       start=True, stop=False)
            for j in range(TILES - 1):
                k = TILES - 1 - j
                pe_.matmul(ps_o[:, (j + 1) * E:TILES * E].rearrange("p (t e) -> p t e", e=E), ones_b[:, :],
                           chosen[:, j:j + 1, :].broadcast_to([P, k, E]), start=False, stop=j == TILES - 2)
            for j in range(TILES):
                last = pe_.matmul(ps_o[:, TILES * E:(TILES + 1) * E], ones_b[:, :], chosen[:, j, :],
                                  start=j == 0, stop=j == TILES - 1)
            last.then_inc(ranks_ready, 1)
            pe.wait_ge(rows_ready, 1)

            pe.wait_ge(xb_free, PAIR_STEPS_END + 2)
            pe.wait_ge(conv_hi, 1)
            pe.wait_ge(converted, 1)
            x_transposes(0)

            def tile(t, s, routed, first, place, prev, last):
                up(t, s, 0, routed, place)
                if not first:
                    hid_transposes(t - 1, 1, routed)
                up(t, s, 1, routed, place)
                if not last:
                    x_transposes(t + 1)
                if not first:
                    down(t - 1, s - 1, routed, prev)
                hid_transposes(t, 0, routed)

            SH = RING - 1
            tile(0, 0, False, True, SH, SH, False)
            with pe.Fori(1, TILES - 1) as s:
                tile(s, s, False, False, SH, SH, False)
            tile(TILES - 1, TILES - 1, False, False, SH, SH, True)
            hid_transposes(TILES - 1, 1, False)
            down(TILES - 1, TILES - 1, False, SH)

            def look(s):
                place = pe.value_load(tab_ring[0:1, bass.ds(s, 1)], min_val=0, max_val=RING - 1)
                need = pe.value_load(tab_need[0:1, bass.ds(s, 1)], min_val=2, max_val=E + 1)
                pe.wait_ge(converted, need)
                return place

            x_transposes(TILES)
            pe.wait_ge(tables_ready, 1)
            place = look(0)
            tile(TILES, 0, True, True, place, place, False)
            with pe.Fori(1, SLOTS - 1) as s:
                prev = pe.value_load(tab_ring[0:1, bass.ds(s - 1, 1)], min_val=0, max_val=RING - 1)
                place = look(s)
                tile(s + TILES, s, True, False, place, prev, False)
            prev = pe.value_load(tab_ring[0:1, SLOTS - 2:SLOTS - 1], min_val=0, max_val=RING - 1)
            place = look(SLOTS - 1)
            tile(TILES + SLOTS - 1, SLOTS - 1, True, False, place, prev, True)
            hid_transposes(TILES + SLOTS - 1, 1, True)
            down(TILES + SLOTS - 1, SLOTS - 1, True, place)

        @block.scalar
        def _(sc):
            sc.dma_start(bias_raw[:, :], bias_d).then_inc(bias_in, 16)
            sc.dma_start(pad_b[:, :], pad_d.partition_broadcast(P)).then_inc(mask_in, 16)
            sc.dma_start(sub_b[:, :], sub_d).then_inc(mask_in, 16)
            sc.dma_start(bqs[:, :], bq_d).then_inc(misc_in, 16)
            sc.dma_start(bks[:, :], bk_d).then_inc(misc_in, 16)
            sc.dma_start(wr[:, :, :], wr_d.rearrange("(c p) n -> p c n", p=P)).then_inc(misc_in, 16)
            sc.dma_start(br[:, :], br_d.partition_broadcast(P)).then_inc(misc_in, 16)
            sc.wait_ge(zero_ready, 1)
            sc.dma_start(rows_in.rearrange("(s p) d -> p s d", p=P),
                         y_row[:, :].rearrange("p (o d) -> p o d", o=1).broadcast_to([P, SLOTS, D])).then_inc(zero_out, 16)
            sc.wait_ge(wq_in, 16)
            act.activation(wqh[:, :, :], wq_raw[:, :, :], ACT.Identity).then_inc(w_hi, 1)
            sc.wait_ge(wk_in, 16)
            act.activation(wkh[:, :, :], wk_raw[:, :, :], ACT.Identity).then_inc(w_hi, 1)
            sc.wait_ge(wv_in, 16)
            act.activation(wvh[:, :, :], wv_raw[:, :, :], ACT.Identity).then_inc(w_hi, 1)
            sc.wait_ge(consts_ready, 1)
            sc.wait_ge(misc_in, 64)

            def step(s, pp, par, idx):
                sc.wait_ge(xb_ready, idx + 1)
                if s in ("xT", "cT"):
                    act.activation(aTh[s == "cT"][:, :, :], ps_x[:, :].rearrange("p (c n) -> p c n", c=KC),
                                   ACT.Identity).then_inc(xb_hi, 1)
                elif s[0] in "qk":
                    for gg in range(2):
                        g = 2 * int(s[1]) + gg
                        src = ps_x[:, gg * 256:(gg + 1) * 256]
                        if s[0] == "q":
                            last = act.activation(q_cut[:, gg, :], src, ACT.Identity, bias=bqc[:, g:g + 1],
                                                  scale=const[:, C_LOQ:C_LOQ + 1])
                        else:
                            last = act.activation(k_hi[par][:, g, :], src, ACT.Identity, bias=bks[:, g:g + 1])
                    last.then_inc(xb_hi, 1)
                else:
                    act.activation(v_sb[par][:, :, :, 0:HD],
                                   ps_x[:, :].rearrange("p (b h d) -> p b h d", b=2, h=H), ACT.Identity)\
                        .then_inc(xb_free, 1)

            def prob_copy(U):
                sc.wait_ge(pt_ready, U + 1)
                if not (isinstance(U, int) and U == 0):
                    sc.wait_ge(pv_done, U)
                act.activation(probT[:, :, :, :], ps_t[:, :, :].rearrange("p j (g t) -> p j g t", g=4),
                               ACT.Identity).then_inc(pt_copied, 1)

            def exp(U, n):
                sc.wait_ge(shifted, U + 1)
                act.activation(prob[n % 2][:, :, :, :], prob[n % 2][:, :, :, :], ACT.Exp, scale=1.0 / HD ** 0.5)\
                    .then_inc(exp_done, 1)

            def router(s, idx):
                if s == "r":
                    sc.wait_ge(xb_ready, idx + 1)
                    act.activation(xn2T[:, :, :], ps_x[:, :].rearrange("p (c n) -> p c n", c=KC), ACT.Identity)\
                        .then_inc(xb_free, 1)

            for k, s in enumerate(PROJ):
                step(s, 0, 0, k)

            def pair(p, par, first, last):
                for n in range(4):
                    if not (first and n == 0):
                        prob_copy(p * 4 + n - 1)
                    for k, s in enumerate(steps(n, first, last)):
                        idx = before(p, n, k, first, last)
                        if s in "rl":
                            router(s, idx)
                        else:
                            step(s, p + 1, 1 - par, idx)
                    exp(p * 4 + n, n)

            each_pair(sc, pair)
            prob_copy(UNITS - 1)
            router("r", PAIR_STEPS_END)
            sc.wait_ge(gap_ready, 1)
            act.activation(ex[:, :], ex[:, :], ACT.Exp).then_inc(ex_ready, 1)

            def gelu(t, u, routed):
                half_w = (HR if routed else HS) // 2
                sc.wait_ge(up_ready[u], t + 1)
                if not (isinstance(t, int) and t == 0):
                    sc.wait_ge(hid_done[u], t)
                act.activation(gel[u][:, 0:half_w], ps_s[:, 2 * u + 1, 0:half_w], ACT.Gelu)\
                    .then_inc(gelu_done[u], 1)

            def hid_hi(t, u, routed):
                nch = (HR if routed else HS) // 2 // P
                sc.wait_ge(ht_ready[u], t + 1)
                if not (isinstance(t, int) and t == 0):
                    sc.wait_ge(y_ready, t)
                act.activation(hTh[u][:, 0:nch, :], ps_t[:, u, 0:nch * P].rearrange("p (c n) -> p c n", c=nch),
                               ACT.Identity).then_inc(ht_hi[u], 1)

            def x_hi(t):
                sc.wait_ge(xt_ready, t + 1)
                if not (isinstance(t, int) and t == 0):
                    sc.wait_ge(up_ready[1], t)
                act.activation(xTh[:, :, :], ps_x[:, 0:D].rearrange("p (c n) -> p c n", c=KC), ACT.Identity)\
                    .then_inc(xt_hi, 1)

            def pick_up(s):
                if not (isinstance(s, int) and s == 0):
                    sc.wait_ge(up_ready[1], s + TILES)
                act.activation(sel_up[:, :], sel_ind[:, bass.ds(s, 1)].broadcast_to([2 * ROWS, P]), ACT.Identity)\
                    .then_inc(sel_up_ready, 1)

            def pick_down(s):
                if not (isinstance(s, int) and s == 0):
                    sc.wait_ge(y_ready, s + TILES)
                act.activation(sel_down[:, :], sel_ind[:, bass.ds(s, 1)].broadcast_to([2 * ROWS, P]), ACT.Identity)\
                    .then_inc(sel_down_ready, 1)

            def tile(t, s, routed, first, last):
                gelu(t, 0, routed)
                if not first:
                    hid_hi(t - 1, 1, routed)
                gelu(t, 1, routed)
                if not last:
                    if routed:
                        pick_up(s + 1)
                    x_hi(t + 1)
                if routed:
                    pick_down(s)
                hid_hi(t, 0, routed)

            x_hi(0)
            tile(0, 0, False, True, False)
            with sc.Fori(1, TILES - 1) as s:
                tile(s, s, False, False, False)
            tile(TILES - 1, TILES - 1, False, False, True)
            hid_hi(TILES - 1, 1, False)
            sc.wait_ge(tables_ready, 1)
            pick_up(0)
            x_hi(TILES)
            tile(TILES, 0, True, True, False)
            with sc.Fori(1, SLOTS - 1) as s:
                tile(s + TILES, s, True, False, False)
            tile(TILES + SLOTS - 1, SLOTS - 1, True, False, True)
            hid_hi(TILES + SLOTS - 1, 1, True)

        @block.vector
        def _(ve):
            own_steps = [0]

            def chain(ins):
                own_steps[0] += 1
                ins.then_inc(vstep, 1)
                ve.wait_ge(vstep, own_steps[0])

            vec.memset(y_row[:, :], 0.0).then_inc(zero_ready, 1)
            vec.memset(half[:, :], -0.5)
            vec.memset(eps[:, :], EPS)
            vec.memset(ones_b[:, :], 1.0)
            for par in range(2):
                vec.memset(v_sb[par][:, :, :, HD:VW], 1.0)
            ve.wait_ge(const_in, 16)
            vec.tensor_copy(ident_b[:, :], const[:, C_ID:C_ID + P])
            vec.tensor_copy(upper_b[:, :], const[:, C_UP:C_UP + P])
            for t, row in ((sel_v, V_ROW), (sel_s, SHARED_ROW)):
                vec.tensor_scalar(t[:, :], const[0:2 * ROWS, C_ROW:C_ROW + 1].broadcast_to([2 * ROWS, P]), float(row), None,
                                  ALU.is_equal)
            ve.wait_ge(misc_in, 64)
            vec.tensor_scalar(bqc[:, :], bqs[:, :], const[:, C_LOQ:C_LOQ + 1], None, ALU.mult)\
                .then_inc(consts_ready, 1)
            ve.wait_ge(bias_in, 16)
            vec.tensor_scalar(bias_cut[:, :], bias_raw[:, :], const[0:2 * ROWS, C_LOB:C_LOB + 1], None, ALU.mult)\
                .then_inc(bias_cut_done, 1)
            ve.wait_ge(bias_cut_done, 1)
            vec.tensor_tensor(bias_tab[:, :], bias_raw[:, :], bias_cut[:, :].bitcast(f32), ALU.subtract)\
                .then_inc(bias_ready, 1)

            def ln1_stats(pp):
                for b in range(2):
                    vec.bn_stats(bn1[:, b, :], x_all[:, bass.ds((pp * 2 + b) * D, D)]).then_inc(ln1_bn, 1)
                ve.wait_ge(ln1_bn, pp * 2 + 2)
                vec.memset(tick[:, :], 0.0)
                for b in range(2):
                    last = vec.bn_aggr(mv1[:, b, :], bn1[:, b, :])
                last.then_inc(ln1_var, 1)

            def ln1_apply(pp):
                ve.wait_ge(ln1_rs, pp + 1)
                for b in range(2):
                    last = vec.tensor_scalar(xn1[:, b, :], x_all[:, bass.ds((pp * 2 + b) * D, D)], mv1[:, b, 0:1],
                                             rs1[:, b:b + 1], ALU.subtract, ALU.mult)
                last.then_inc(xn1_ready, 1)

            ve.wait_ge(x_in, 16)
            ln1_stats(0)
            for n, (lo, raw, hi) in enumerate(((wql, wq_raw, wqh), (wkl, wk_raw, wkh), (wvl, wv_raw, wvh))):
                ve.wait_ge(w_hi, n + 1)
                vec.tensor_tensor(lo[:, :, :], raw[:, :, :], hi[:, :, :].bitcast(f32), ALU.subtract).then_inc(w_ready, 1)
                if n == 0:
                    ln1_apply(0)

            def step(s, pp, par, idx, hi_idx):
                if s in HI:
                    ve.wait_ge(xb_hi, hi_idx + 1)
                if s in ("xT", "cT"):
                    a = int(s == "cT")
                    vec.tensor_tensor(aTl[a][:, :, :], ps_x[:, :].rearrange("p (c n) -> p c n", c=KC),
                                      aTh[a][:, :, :].bitcast(f32), ALU.subtract).then_inc(xb_free, 1)
                elif s[0] in "qk":
                    for gg in range(2):
                        g = 2 * int(s[1]) + gg
                        src = ps_x[:, gg * 256:(gg + 1) * 256]
                        if s[0] == "q":
                            last = vec.scalar_tensor_tensor(q_st[par][:, g, :], src, bqs[:, g:g + 1],
                                                            q_cut[:, gg, :].bitcast(f32), ALU.add, ALU.subtract)
                        else:
                            last = vec.scalar_tensor_tensor(k_lo[par][:, g, :], src, bks[:, g:g + 1],
                                                            k_hi[par][:, g, :].bitcast(f32), ALU.add, ALU.subtract)
                    last.then_inc(xb_free, 1)

            def router(s, q, idx):
                if s == "l":
                    ve.wait_ge(xb_ready, idx + 1)
                    vec.tensor_tensor(logits[:, bass.ds(q * 2, 2), :], ps_x[:, 0:2 * E].rearrange("p (t e) -> p t e", e=E),
                                      br[:, :].rearrange("p (o e) -> p o e", o=1).broadcast_to([P, 2, E]), ALU.add)\
                        .then_inc(xb_free, 1)

            for k, s in enumerate(PROJ):
                step(s, 0, 0, k, HI.index(s) if s in HI else 0)
                if s == "xT":
                    ln1_stats(1)
                    ve.wait_ge(xb_ready, 1)
                    ln1_apply(1)
            ve.wait_ge(mask_in, 32)
            vec.tensor_scalar(keep[:, :, :].rearrange("p b t -> p (b t)"), pad_b[:, :], 0.0, None, ALU.not_equal)\
                .then_inc(mstep, 1)
            vec.tensor_scalar(keep_s[:, :], sub_b[:, :], 0.0, None, ALU.not_equal).then_inc(mstep, 1)
            ve.wait_ge(mstep, 2)
            ve.wait_ge(bias_ready, 1)
            vec.tensor_tensor(keep[:, :, :], keep[:, :, :],
                              keep_s[:, :].rearrange("p (o t) -> p o t", o=1).broadcast_to([P, B, S]), ALU.mult)\
                .then_inc(mstep, 1)
            ve.wait_ge(mstep, 3)
            vec.tensor_scalar(mask_b[:, :, :], keep[:, :, :], -FILL, FILL, ALU.mult, ALU.add).then_inc(masks_ready, 1)
            ve.wait_ge(x_rest_in, 16)

            def softmax_shift(U, n):
                u = n % 2
                ve.wait_ge(scores_ready, U + 1)
                src = ps_s[:, 2 * u:2 * u + 2, :].rearrange("p j (g t) -> p j g t", g=4)
                if not (isinstance(U, int) and U == 0):
                    ve.wait_ge(shifted, U)
                vec.tensor_reduce(nmax[:, :, :], src, AX.X, ALU.max, negate=True).then_inc(maxed, 1)
                ve.wait_ge(maxed, U + 1)
                if not (isinstance(U, int) and U < 2):
                    ve.wait_ge(pt_ready, U - 1)
                vec.tensor_tensor(prob[n % 2][:, :, :, :], src,
                                  nmax[:, :, :].rearrange("p j (g o) -> p j g o", o=1).broadcast_to([P, 2, 4, P]), ALU.add)\
                    .then_inc(shifted, 1)

            def norm(p, b):
                ve.wait_ge(pv_done, p * 4 + 2 * b + 2)
                o = ps_o[:, 0:H * VW].rearrange("p (h d) -> p h d", d=VW)
                vec.reciprocal(rden[:, :], o[:, :, HD]).then_inc(nstep, 1)
                ve.wait_ge(nstep, (p * 2 + b) * 3 + 1)
                vec.tensor_tensor(att[:, :].rearrange("p (h d) -> p h d", d=HD), o[:, :, 0:HD],
                                  rden[:, :].rearrange("p (h o) -> p h o", o=1).broadcast_to([P, H, HD]), ALU.mult)\
                    .then_inc(nstep, 1)
                ve.wait_ge(nstep, (p * 2 + b) * 3 + 2)
                xs = x_all[:, bass.ds((p * 2 + b) * D, D)]
                vec.tensor_tensor(xs, xs, att[:, :], ALU.add).then_inc(normed, 1)
                ve.wait_ge(normed, p * 2 + b + 1)
                vec.memset(tick[:, :], 0.0)
                vec.bn_stats(bn2[:, b, :], xs).then_inc(nstep, 1)
                if b == 1:
                    ve.wait_ge(nstep, (p * 2 + b) * 3 + 3)
                    vec.memset(tick[:, :], 0.0)
                    for i in range(2):
                        last = vec.bn_aggr(mv2[:, i, :], bn2[:, i, :])
                    last.then_inc(ln2_var, 1)

            def ln2_apply(q):
                ve.wait_ge(ln2_rs, q + 1)
                if not (isinstance(q, int) and q == 0):
                    ve.wait_ge(xn2_saved, q * 32)
                for b in range(2):
                    last = vec.tensor_scalar(xn2p[:, b, :], x_all[:, bass.ds((q * 2 + b) * D, D)], mv2[:, b, 0:1],
                                             rs2[:, b:b + 1], ALU.subtract, ALU.mult)
                last.then_inc(xn2_ready, 1)

            def pair(p, par, first, last):
                for n in range(4):
                    softmax_shift(p * 4 + n, n)
                    for k, s in enumerate(steps(n, first, last)):
                        idx = before(p, n, k, first, last)
                        if s in "rl":
                            router(s, p - 1, idx)
                        else:
                            step(s, p + 1, 1 - par, idx, (p + 1) * 6 + (HI.index(s) if s in HI else 0))
                    if n == 0 and not first:
                        norm(p - 1, 1)
                    if n == 1 and not first:
                        ln2_apply(p - 1)
                    if n == 1 and not last and not (isinstance(p, int) and p + 2 >= PAIRS):
                        ln1_stats(p + 2)
                    if n == 2:
                        norm(p, 0)
                    if n == 3 and not last and not (isinstance(p, int) and p + 2 >= PAIRS):
                        ve.wait_ge(xb_ready, before(p, 0, 0, first, last) + 1)
                        ln1_apply(p + 2)

            each_pair(ve, pair)
            norm(PAIRS - 1, 1)
            ln2_apply(PAIRS - 1)
            router("l", PAIRS - 1, PAIR_STEPS_END + 1)

            base_steps = own_steps[0]
            three = [P, TILES, E]

            def over_experts(a):
                return a.rearrange("p (t o) -> p t o", o=1).broadcast_to(three)

            rank = const[:, C_RANK:C_RANK + E].rearrange("p (o e) -> p o e", o=1).broadcast_to(three)
            ve.wait_ge(xb_free, PAIR_STEPS_END + 2)
            chain(vec.tensor_scalar(lg[:, :, :], logits[:, :, :], 1.0 / TAU, None, ALU.mult))
            for k, pick in ((0, pick1), (1, pick2)):
                chain(vec.tensor_reduce(top[:, k, :], lg[:, :, :], AX.X, ALU.max))
                chain(vec.tensor_tensor(eq[:, :, :], lg[:, :, :], over_experts(top[:, k, :]), ALU.is_equal))
                chain(vec.tensor_tensor(eq[:, :, :], eq[:, :, :], rank, ALU.mult))
                chain(vec.tensor_reduce(best[:, :], eq[:, :, :], AX.X, ALU.max))
                chain(vec.tensor_tensor(pick[:, :, :], rank, over_experts(best[:, :]), ALU.is_equal))
                if k == 0:
                    chain(vec.scalar_tensor_tensor(lg[:, :, :], pick[:, :, :], FILL, lg[:, :, :], ALU.mult, ALU.add))
            vec.tensor_tensor(ex[:, :], top[:, 1, :], top[:, 0, :], ALU.subtract).then_inc(gap_ready, 1)
            vec.tensor_tensor(chosen[:, :, :], pick1[:, :, :], pick2[:, :, :], ALU.add).then_inc(chosen_ready, 1)
            ve.wait_ge(ranks_ready, 1)
            tot = ps_o[:, TILES * E:(TILES + 1) * E]
            vec.memset(ones_e[:, :], 1.0)
            chain(vec.tensor_scalar(cnt_i[:, :], tot, float(P - 1), None, ALU.add))
            chain(vec.tensor_scalar(cnt_s[:, :], cnt_i[:, :], 7, None, ALU.logical_shift_right))
            chain(vec.tensor_scalar(tiles_e[:, :], cnt_s[:, :], 1.0, None, ALU.max))
            chain(vec.tensor_tensor_scan(cum_e[:, :], ones_e[:, :], tiles_e[:, :], 0.0, ALU.mult, ALU.add))
            chain(vec.tensor_tensor(base_e[:, :], cum_e[:, :], tiles_e[:, :], ALU.subtract))
            chain(vec.tensor_scalar(base_e[:, :], base_e[:, :], float(P), None, ALU.mult))
            chain(vec.tensor_tensor(pos[:, :, :], ps_o[:, 0:TILES * E].rearrange("p (t e) -> p t e", e=E),
                                    base_e[:, :].rearrange("p (o e) -> p o e", o=1).broadcast_to(three), ALU.add))
            for k, pick in ((0, pick1), (1, pick2)):
                chain(vec.tensor_tensor(eq[:, :, :], pos[:, :, :], pick[:, :, :], ALU.mult))
                chain(vec.tensor_reduce(best[:, :], eq[:, :, :], AX.X, ALU.add))
                last = vec.tensor_copy(idx_top[:, k, :], best[:, :])
                if k == 0:
                    chain(last)
            last.then_inc(rows_ready, 1)
            wide = [P, SLOTS, E - 1]
            vec.tensor_scalar(tab_cum[:, :], cum_e[:, :], float(TILES), None, ALU.add)
            chain(vec.tensor_tensor(past[:, :, :],
                                    const[:, C_SLOT:C_SLOT + SLOTS].rearrange("p (s o) -> p s o", o=1).broadcast_to(wide),
                                    cum_e[:, 0:E - 1].rearrange("p (o e) -> p o e", o=1).broadcast_to(wide), ALU.is_ge))
            chain(vec.tensor_reduce(slot_e[:, :], past[:, :, :], AX.X, ALU.add))
            chain(vec.tensor_tensor(past2[:, :, :], past[:, :, :],
                                    const[:, C_STEP:C_STEP + E - 1].rearrange("p (o e) -> p o e", o=1).broadcast_to(wide),
                                    ALU.mult))
            chain(vec.tensor_reduce(slot_r[:, :], past2[:, :, :], AX.X, ALU.add))
            vec.tensor_copy(tab_ring[:, :], slot_r[:, :])
            vec.tensor_scalar(tab_need[:, :], slot_e[:, :], 2.0, None, ALU.add)
            vec.tensor_scalar(sel_ind[:, :], slot_e[0:2 * ROWS, :], const[0:2 * ROWS, C_ROW:C_ROW + 1], None, ALU.is_equal)\
                .then_inc(tables_ready, 1)
            ve.wait_ge(ex_ready, 1)
            chain(vec.tensor_scalar(top[:, 0, :], ex[:, :], 1.0, None, ALU.add))
            chain(vec.reciprocal(w_top[:, 0, :], top[:, 0, :]))
            chain(vec.tensor_tensor(w_top[:, 1, :], w_top[:, 0, :], ex[:, :], ALU.mult))

            def gate(t, u, routed):
                half_w = (HR if routed else HS) // 2
                ve.wait_ge(gelu_done[u], t + 1)
                if not (isinstance(t, int) and t == 0):
                    ve.wait_ge(ht_ready[u], t)
                vec.tensor_tensor(hid[u][:, 0:half_w], ps_s[:, 2 * u, 0:half_w], gel[u][:, 0:half_w], ALU.mult)\
                    .then_inc(hid_done[u], 1)

            def hid_lo(t, u, routed):
                nch = (HR if routed else HS) // 2 // P
                ve.wait_ge(ht_hi[u], t + 1)
                vec.tensor_tensor(hTl[u][:, 0:nch, :], ps_t[:, u, 0:nch * P].rearrange("p (c n) -> p c n", c=nch),
                                  hTh[u][:, 0:nch, :].bitcast(f32), ALU.subtract).then_inc(ht_lo[u], 1)

            def x_lo(t):
                ve.wait_ge(xt_hi, t + 1)
                vec.tensor_tensor(xTl[:, :, :], ps_x[:, 0:D].rearrange("p (c n) -> p c n", c=KC),
                                  xTh[:, :, :].bitcast(f32), ALU.subtract).then_inc(xt_lo, 1)

            def y_copy(t, s, routed):
                ve.wait_ge(y_ready, t + 1)
                if routed:
                    if not (isinstance(s, int) and s == 0):
                        ve.wait_ge(y_out, 16 * s)
                    vec.tensor_copy(y_row[:, :], ps_o[:, 0:D]).then_inc(y_done, 1)
                else:
                    a = x_all[:, bass.ds(s * D, D)]
                    vec.tensor_tensor(a, ps_o[:, 0:D], a, ALU.add).then_inc(y_done, 1)

            def tile(t, s, routed, first, last):
                gate(t, 0, routed)
                if not first:
                    hid_lo(t - 1, 1, routed)
                gate(t, 1, routed)
                if not last:
                    x_lo(t + 1)
                if not first:
                    y_copy(t - 1, s - 1, routed)
                hid_lo(t, 0, routed)

            x_lo(0)
            tile(0, 0, False, True, False)
            with ve.Fori(1, TILES - 1) as s:
                tile(s, s, False, False, False)
            tile(TILES - 1, TILES - 1, False, False, True)
            hid_lo(TILES - 1, 1, False)
            y_copy(TILES - 1, TILES - 1, False)
            x_lo(TILES)
            tile(TILES, 0, True, True, False)
            with ve.Fori(1, SLOTS - 1) as s:
                tile(s + TILES, s, True, False, False)
            tile(TILES + SLOTS - 1, SLOTS - 1, True, False, True)
            hid_lo(TILES + SLOTS - 1, 1, True)
            y_copy(TILES + SLOTS - 1, SLOTS - 1, True)

            for t in range(TILES):
                ve.wait_ge(gathered[t], 32)
                a = x_all[:, t * D:(t + 1) * D]
                for k in range(2):
                    vec.scalar_tensor_tensor(a, gath[:, t, k, :], w_top[:, k, t:t + 1], a, ALU.mult, ALU.add)\
                        .then_inc(combined, 1)
                    ve.wait_ge(combined, 2 * t + k + 1)

        @block.gpsimd
        def _(gp):
            def rstd(var_sem, out_sem, mv, ve_t, rs_t, q, step_sem):
                gp.wait_ge(var_sem, q + 1)
                pool.tensor_tensor(ve_t[:, :], mv[:, :, 1], eps[:, :], ALU.add).then_inc(step_sem, 1)
                gp.wait_ge(step_sem, q + 1)
                pool.tensor_tensor(rs_t[:, :], ve_t[:, :], half[:, :], ALU.pow).then_inc(out_sem, 1)

            def convert(src, hi_ap, lo_ap, count):
                pool.tensor_scalar(hi_ap, src, 1.0, 0.0, ALU.mult, ALU.add).then_inc(conv_hi, 1)
                gp.wait_ge(conv_hi, count)
                return pool.tensor_tensor(lo_ap, src, hi_ap.bitcast(f32), ALU.subtract)

            gp.wait_ge(consts_ready, 1)
            rstd(ln1_var, ln1_rs, mv1, ve1, rs1, 0, pstep)
            rstd(ln1_var, ln1_rs, mv1, ve1, rs1, 1, pstep)
            gp.wait_ge(shared_in, 32)
            SH = RING - 1
            convert(stage1[:, 0:W1S], ring[:, SH, 0:W1S], ring[:, SH, W1S:2 * W1S], 1)
            convert(stage2[:, 0:W2S], ring[:, SH, 2 * W1S:2 * W1S + W2S],
                    ring[:, SH, 2 * W1S + W2S:2 * W1S + 2 * W2S], 2).then_inc(converted, 1)

            def load_raw1(e):
                gp.dma_start(stage1[:, :].rearrange("p (c n) -> p c n", c=KC),
                             w1_d[e, :, :].rearrange("(c p) n -> p c n", p=P)).then_inc(raw1_in, 16)

            def load_raw2(e):
                gp.dma_start(stage2[:, :].rearrange("p (c n) -> p c n", n=D),
                             w2_d[e, :, :].rearrange("(c p) n -> p c n", p=P)).then_inc(raw2_in, 16)

            gp.wait_ge(converted, 1)
            load_raw1(0)
            load_raw2(0)

            def pair(p, par, first, last):
                if not first:
                    rstd(ln2_var, ln2_rs, mv2, ve2, rs2, p - 1, pstep2)
                if not last and not (isinstance(p, int) and p + 2 >= PAIRS):
                    rstd(ln1_var, ln1_rs, mv1, ve1, rs1, p + 2, pstep)

            each_pair(gp, pair)
            rstd(ln2_var, ln2_rs, mv2, ve2, rs2, PAIRS - 1, pstep2)

            def expert(e):
                r = e % RING
                gp.wait_ge(raw1_in, 16 * (e + 1))
                convert(stage1[:, :], ring[:, r, 0:W1R], ring[:, r, W1R:2 * W1R], 2 * e + 3).then_inc(pconv, 1)
                gp.wait_ge(pconv, e + 1)
                if e + 1 < E:
                    load_raw1(e + 1)
                gp.wait_ge(raw2_in, 16 * (e + 1))
                convert(stage2[:, :], ring[:, r, 2 * W1R:2 * W1R + W2R], ring[:, r, 2 * W1R + W2R:], 2 * e + 4)\
                    .then_inc(converted, 1)
                gp.wait_ge(converted, e + 2)
                if e + 1 < E:
                    load_raw2(e + 1)

            gp.wait_ge(pv_done, UNITS)
            gp.wait_ge(normed, B)
            gp.wait_ge(xb_free, PAIR_STEPS_END + 2)
            expert(0)
            gp.wait_ge(rows_ready, 1)
            gp.wait_ge(zero_out, 16)
            gp.wait_ge(xn2_saved, 32 * PAIRS)
            for t in range(TILES):
                for k in range(2):
                    gp.indirect_dma_start(
                        out=rows_in, out_offset=bass.IndirectOffsetOnAxis(ap=idx_top[:, k, t:t + 1], axis=0),
                        in_=xn2_all[:, t * D:(t + 1) * D], in_offset=None).then_inc(scattered, 16)
            expert(1)
            gp.wait_ge(tables_ready, 1)
            for e in range(2, E):
                if e == 2:
                    gp.wait_ge(y_done, TILES)
                else:
                    done = gp.value_load(tab_cum[0:1, e - RING:e - RING + 1], min_val=1, max_val=SLOTS + TILES)
                    gp.wait_ge(y_done, done)
                    pool.tensor_tensor(ptick[:, :], half[:, 0:1], half[:, 0:1], ALU.add)
                expert(e)
            gp.wait_ge(y_done, TILES + SLOTS)
            gp.wait_ge(y_out, 16 * SLOTS)
            for t in range(TILES):
                for k in range(2):
                    gp.indirect_dma_start(
                        out=gath[:, t, k, :], out_offset=None, in_=rows_out,
                        in_offset=bass.IndirectOffsetOnAxis(ap=idx_top[:, k, t:t + 1], axis=0))\
                        .then_inc(gathered[t], 16)


def kernel(**inputs):
    import numpy as np
    import concourse.bacc as bacc
    from concourse import mybir
    from concourse.bass_utils import run_bass_kernel_spmd

    def arr(name):
        return np.ascontiguousarray(inputs[name])

    def heads(w):
        v = w.reshape(w.shape[:-1] + (4, 4, 1, HD))
        return np.ascontiguousarray(np.broadcast_to(v, w.shape[:-1] + (4, 4, 2, HD)))

    wq = heads(arr("L0_xattn_Wq").T).reshape(D, 512)
    wk = heads(arr("L0_xattn_Wk").T).reshape(D, 512)
    bq = np.ascontiguousarray(heads(arr("L0_xattn_bq")).reshape(4, P).T)
    bk = np.ascontiguousarray(heads(arr("L0_xattn_bk")).reshape(4, P).T)
    wv = np.ascontiguousarray(arr("L0_xattn_Wv").T)
    bias = np.zeros((2, ROWS, BW), np.float32)
    bias[:, :E, :2 * HR] = arr("L0_ffn_be1")
    bias[:, :E, 2 * HR:] = arr("L0_ffn_be2")
    bias[:, SHARED_ROW, :2 * HS] = arr("L0_ffn_bs1")
    bias[:, SHARED_ROW, 2 * HS:2 * HS + D] = arr("L0_ffn_bs2")
    bias[:, V_ROW, :D] = arr("L0_xattn_bv")
    c = np.zeros((P, C_ALL), np.float32)
    c[:, C_ID:C_ID + P] = np.eye(P)
    c[:, C_UP:C_UP + P] = np.triu(np.ones((P, P)), 1)
    c[:, C_LOQ] = np.arange(P) % 32 >= HD
    c[:, C_LOB] = np.arange(P) >= ROWS
    c[:, C_ROW] = np.arange(P) % ROWS
    c[:, C_RANK:C_RANK + E] = E - np.arange(E)
    c[:, C_SLOT:C_SLOT + SLOTS] = np.arange(SLOTS)
    c[:, C_STEP:C_STEP + E - 1] = (np.arange(E - 1) + 1) % RING - np.arange(E - 1) % RING
    arrays = {
        "x": arr("x").reshape(N, D), "ctx": arr("ctx_1024").reshape(N, D),
        "pad": arr("mask_Bx1x1xS2_ik0").reshape(B * S).astype(np.int32),
        "sub": arr("mask_1x1xSxS2_ik0").reshape(S, S).astype(np.int32),
        "wq": wq, "wk": wk, "wv": wv, "bq": bq, "bk": bk, "bias": bias.reshape(2 * ROWS, BW),
        "ws1": arr("L0_ffn_Ws1"), "ws2": arr("L0_ffn_Ws2"), "w1": arr("L0_ffn_We1"), "w2": arr("L0_ffn_We2"),
        "wr": arr("L0_ffn_Wr"), "br": arr("L0_ffn_br"), "consts": c,
    }
    nc = bacc.Bacc("TRN2", target_bir_lowering=False, num_devices=1)
    args = [nc.dram_tensor(f"in_{n}", a.shape, mybir.dt.from_np(a.dtype), kind="ExternalInput").ap()
            for n, a in arrays.items()]
    out = nc.dram_tensor("out_0", (N, D), mybir.dt.float32, kind="ExternalOutput").ap()
    build(nc, *args, out)
    r = run_bass_kernel_spmd(nc, [{f"in_{n}": a for n, a in arrays.items()}], core_ids=[0])
    return r.results[0]["out_0"].reshape(B, S, D)
```

```python
import concourse.bass as bass
from concourse import mybir

P = 128
B, S, D = 16, 128, 256
H, HD = 16, 16
N = B * S
PAIRS = B // 2
E = 12
HR, HS = 3 * D, 2 * D
KC = D // P
TAU = 1.5
EPS = 1e-5
FILL = -1e30
TILES = N // P
SLOTS = (2 * N + (P - 1) * E + (E - 2)) // P
RING = 3
W1R, W2R = KC * 2 * HR, (HR // P) * D
W1S, W2S = KC * 2 * HS, (HS // P) * D
SLOT_W = 2 * (W1R + W2R)
VW = 2 * HD
ROWS = E + 2
BW = 2 * HR + D
SHARED_ROW, V_ROW = E, E + 1
C_ID, C_UP = 0, P
C_LOQ = 2 * P
C_LOB = C_LOQ + 1
C_ROW = C_LOB + 1
C_RANK = C_ROW + 1
C_SLOT = C_RANK + E
C_STEP = C_SLOT + SLOTS
C_ALL = C_STEP + E - 1


def build(nc, x_d, ctx_d, pad_d, sub_d, wq_d, wk_d, wv_d, bq_d, bk_d, bias_d, ws1_d, ws2_d, w1_d,
          w2_d, wr_d, br_d, const_d, out_d):
    f32, f32r = mybir.dt.float32, mybir.dt.float32r
    bf16, i32 = mybir.dt.bfloat16, mybir.dt.int32
    ALU, ACT, AX = mybir.AluOpType, mybir.ActivationFunctionType, mybir.AxisListType
    vec, act, pool, pe_ = nc.vector, nc.scalar, nc.gpsimd, nc.tensor

    xn2_dram = nc.dram_tensor("xn2_dram", (N, D), f32, kind="Internal").ap()
    rows_in = nc.dram_tensor("rows_in", (SLOTS * P, D), f32, kind="Internal").ap()
    rows_out = nc.dram_tensor("rows_out", (SLOTS * P, D), f32, kind="Internal").ap()

    at = [((nc.sbuf_base + 63) // 64) * 64]

    def size(shape, dt):
        n = 1
        for k in shape[1:]:
            n *= k
        return n * (2 if dt == bf16 else 4)

    offset_of = {}

    def put(name, shape, dt, where=at):
        t = nc.alloc_sbuf_tensor_at(name, shape, dt, offset=where[0])
        offset_of[name] = where[0]
        where[0] += (size(shape, dt) + 31) // 32 * 32
        return t

    x_all = put("x_all", [P, TILES * D], f32)
    xn2_all = put("xn2_all", [P, TILES * D], f32)
    const = put("const", [P, C_ALL], f32)
    bias_tab = put("bias_tab", [2 * ROWS, BW], f32r)
    ident_b = put("ident_b", [P, P], bf16)
    upper_b = put("upper_b", [P, P], bf16)
    ones_b = put("ones_b", [P, P], bf16)
    sel_v = put("sel_v", [2 * ROWS, P], f32r)
    sel_s = put("sel_s", [2 * ROWS, P], f32r)
    sel_up = put("sel_up", [2 * ROWS, P], f32r)
    sel_down = put("sel_down", [2 * ROWS, P], f32r)
    wr = put("wr", [P, KC, E], f32)
    br = put("br", [P, E], f32)
    logits = put("logits", [P, TILES, E], f32)
    xrow = put("xrow", [P, D], f32)
    half = put("half", [P, 2], f32)
    eps = put("eps", [P, 2], f32)
    tick = put("tick", [P, 1], f32)
    ptick = put("ptick", [P, 1], f32)
    bn1 = put("bn1", [P, 2, 6], f32)
    mv1 = put("mv1", [P, 2, 2], f32)
    ve1 = put("ve1", [P, 2], f32)
    rs1 = put("rs1", [P, 2], f32)
    bn2 = put("bn2", [P, 2, 6], f32)
    mv2 = put("mv2", [P, 2, 2], f32)
    ve2 = put("ve2", [P, 2], f32)
    rs2 = put("rs2", [P, 2], f32)
    w_top = put("w_top", [P, 2, TILES], f32)
    idx_top = put("idx_top", [P, 2, TILES], i32)
    tab_ring = put("tab_ring", [P, SLOTS], i32)
    tab_need = put("tab_need", [P, SLOTS], i32)
    tab_cum = put("tab_cum", [P, E], i32)
    sel_ind = put("sel_ind", [2 * ROWS, SLOTS], f32)
    stage1 = put("stage1", [P, W1R], f32)
    stage2 = put("stage2", [P, W2R], f32)
    ring = put("ring", [P, RING, SLOT_W], f32r)
    ring_at = at[0] - RING * SLOT_W * 4
    work_at = [at[0]]
    xTh = put("xTh", [P, KC, P], f32r)
    xTl = put("xTl", [P, KC, P], f32r)
    gel = [put(f"gel{u}", [P, HR // 2], f32) for u in range(2)]
    hid = [put(f"hid{u}", [P, HR // 2], f32) for u in range(2)]
    hTh = [put(f"hTh{u}", [P, 3, P], f32r) for u in range(2)]
    hTl = [put(f"hTl{u}", [P, 3, P], f32r) for u in range(2)]
    y_row = put("y_row", [P, D], f32)
    own = [at[0]]
    pad_b = put("pad_b", [P, B * S], i32, own)
    mask_b = put("mask_b", [P, B, S], bf16, own)
    xn2p = put("xn2p", [P, 2, D], f32, own)
    cbuf = put("cbuf", [P, 2, D], f32, own)
    assert own[0] <= nc.sbuf_top, own[0] - nc.sbuf_top
    low = [ring_at]
    wqh = put("wqh", [P, KC, 512], f32r, low)
    wql = put("wql", [P, KC, 512], f32r, low)
    wkh = put("wkh", [P, KC, 512], f32r, low)
    wkl = put("wkl", [P, KC, 512], f32r, low)
    wvh = put("wvh", [P, KC, D], f32r, low)
    wvl = put("wvl", [P, KC, D], f32r, low)
    aTh = [put(f"aTh{i}", [P, KC, 256], f32r, low) for i in range(2)]
    aTl = [put(f"aTl{i}", [P, KC, 256], f32r, low) for i in range(2)]
    q_st = [put(f"q_st{i}", [P, 4, 256], f32r, low) for i in range(2)]
    k_hi = [put(f"k_hi{i}", [P, 4, 256], f32r, low) for i in range(2)]
    k_lo = [put(f"k_lo{i}", [P, 4, 256], f32r, low) for i in range(2)]
    v_sb = [put(f"v_sb{i}", [P, 2, H, VW], f32, low) for i in range(2)]
    prob = [put(f"prob{i}", [P, 2, 4, P], f32, low) for i in range(2)]
    probT = put("probT", [P, 2, 4, P], f32, low)
    assert low[0] <= ring_at + 2 * SLOT_W * 4, low[0] - ring_at - 2 * SLOT_W * 4
    wk1 = [work_at[0]]
    xn1 = put("xn1", [P, 2, D], f32, wk1)
    att = put("att", [P, D], f32, wk1)
    rden = put("rden", [P, H], f32, wk1)
    nmax = put("nmax", [P, 2, 4], f32, wk1)
    bqs = put("bqs", [P, 4], f32, wk1)
    bqc = put("bqc", [P, 4], f32, wk1)
    bks = put("bks", [P, 4], f32, wk1)
    xn2T = put("xn2T", [P, KC, 256], f32, wk1)
    outT = put("outT", [P, 4 * P], f32, wk1)
    q_cut = put("q_cut", [P, 4, 256], f32r, wk1)
    sub_b = put("sub_b", [P, S], i32, wk1)
    keep_s = put("keep_s", [P, S], f32, wk1)
    assert wk1[0] <= at[0]
    pro = [offset_of["stage1"]]
    wq_raw = put("wq_raw", [P, KC, 512], f32, pro)
    wk_raw = put("wk_raw", [P, KC, 512], f32, pro)
    wv_raw = put("wv_raw", [P, KC, D], f32, pro)
    pr2 = [offset_of["prob0"]]
    bias_raw = put("bias_raw", [2 * ROWS, BW], f32, pr2)
    pr3 = [offset_of["xn2_all"]]
    bias_cut = put("bias_cut", [2 * ROWS, BW], f32r, pr3)
    keep = put("keep", [P, B, S], f32, pr3)
    rt = [offset_of["pad_b"]]
    lg = put("lg", [P, TILES, E], f32, rt)
    eq = put("eq", [P, TILES, E], f32, rt)
    pick1 = put("pick1", [P, TILES, E], f32, rt)
    pick2 = put("pick2", [P, TILES, E], f32, rt)
    chosen = put("chosen", [P, TILES, E], bf16, rt)
    pos = put("pos", [P, TILES, E], f32, rt)
    top = put("top", [P, 2, TILES], f32, rt)
    best = put("best", [P, TILES], f32, rt)
    ex = put("ex", [P, TILES], f32, rt)
    cnt_i = put("cnt_i", [P, E], i32, rt)
    cnt_s = put("cnt_s", [P, E], i32, rt)
    tiles_e = put("tiles_e", [P, E], f32, rt)
    cum_e = put("cum_e", [P, E], f32, rt)
    base_e = put("base_e", [P, E], f32, rt)
    ones_e = put("ones_e", [P, E], f32, rt)
    past = put("past", [P, SLOTS, E - 1], f32, rt)
    past2 = put("past2", [P, SLOTS, E - 1], f32, rt)
    slot_e = put("slot_e", [P, SLOTS], f32, rt)
    slot_r = put("slot_r", [P, SLOTS], f32, rt)
    assert rt[0] <= nc.sbuf_top
    ga = [ring_at]
    gath = put("gath", [P, TILES, 2, D], f32, ga)

    ident = const[:, C_ID:C_ID + P]

    ps_s = nc.alloc_psum_tensor("ps_s", [P, 4, 512], f32)
    ps_t = nc.alloc_psum_tensor("ps_t", [P, 2, 512], f32)
    ps_o = nc.alloc_psum_tensor("ps_o", [P, 512], f32)
    ps_x = nc.alloc_psum_tensor("ps_x", [P, 512], f32)

    step_bank = [ps_x[:, :], ps_t[:, 1, :]]
    assert len(step_bank) == 2

    def sem(name):
        return nc.alloc_semaphore(name)

    const_in, x_in, x_rest_in, ctx_in, wq_in, wk_in, wv_in = map(sem, (
        "const_in", "x_in", "x_rest_in", "ctx_in", "wq_in", "wk_in", "wv_in"))
    bias_in, mask_in, misc_in, zero_out, shared_in = map(sem, (
        "bias_in", "mask_in", "misc_in", "zero_out", "shared_in"))
    consts_ready, masks_ready, w_hi, w_ready, bias_cut_done, bias_ready = map(sem, (
        "consts_ready", "masks_ready", "w_hi", "w_ready", "bias_cut_done", "bias_ready"))
    scores_ready, shifted, maxed, exp_done, pt_ready, pt_copied, pv_done, normed = map(sem, (
        "scores_ready", "shifted", "maxed", "exp_done", "pt_ready", "pt_copied", "pv_done", "normed"))
    ot_copied, ot_ready = sem("ot_copied"), sem("ot_ready")
    xb_ready, xb_hi, xb_free, ln1_var, ln1_rs, ln2_var, ln2_rs, xn1_ready, xn2_ready, xn2_saved = map(sem, (
        "xb_ready", "xb_hi", "xb_free", "ln1_var", "ln1_rs", "ln2_var", "ln2_rs", "xn1_ready",
        "xn2_ready", "xn2_saved"))
    vstep, mstep, nstep, ln1_bn, pstep, pstep2, pconv = map(sem, (
        "vstep", "mstep", "nstep", "ln1_bn", "pstep", "pstep2", "pconv"))
    zero_ready = sem("zero_ready")
    chosen_ready, ranks_ready, tables_ready, rows_ready, scattered, ex_ready, gap_ready = map(sem, (
        "chosen_ready", "ranks_ready", "tables_ready", "rows_ready", "scattered", "ex_ready", "gap_ready"))
    xrow_in, xt_ready, xt_hi, xt_lo = map(sem, ("xrow_in", "xt_ready", "xt_hi", "xt_lo"))
    up_ready = [sem("up_ready0"), sem("up_ready1")]
    gelu_done = [sem("gelu_done0"), sem("gelu_done1")]
    hid_done = [sem("hid_done0"), sem("hid_done1")]
    ht_ready = [sem("ht_ready0"), sem("ht_ready1")]
    ht_hi = [sem("ht_hi0"), sem("ht_hi1")]
    ht_lo = [sem("ht_lo0"), sem("ht_lo1")]
    y_ready, y_done, y_out, sel_up_ready, sel_down_ready = map(sem, (
        "y_ready", "y_done", "y_out", "sel_up_ready", "sel_down_ready"))
    raw1_in, raw2_in, conv_hi, converted = map(sem, ("raw1_in", "raw2_in", "conv_hi", "converted"))
    gathered = [sem(f"gathered{t}") for t in range(TILES)]
    combined, stored = sem("combined"), sem("stored")

    PLAN = [["cT", "k0"], ["v", "xT"], ["r", "k1", "q0"], ["l", "q1"]]
    PROJ = [s for unit in PLAN for s in unit if s not in "rl"]
    HI = [s for s in PROJ if s != "v"]

    def steps(n, first, last):
        return [s for s in PLAN[n] if (s not in "rl" or not first) and (s in "rl" or not last)]

    def before(p, n, k, first, last):
        base = len(PROJ) if first else 9 * p + 5
        return base + sum(len(steps(m, first, last)) for m in range(n)) + k

    def index_of(s, p, first, last):
        n = [s in unit for unit in PLAN].index(True)
        return before(p, n, steps(n, first, last).index(s), first, last)

    def each_pair(eng, body):
        body(0, 0, True, False)
        with eng.Fori(0, (PAIRS - 4) // 2) as i:
            body(i * 2 + 1, 1, False, False)
            body(i * 2 + 2, 0, False, False)
        body(PAIRS - 3, 1, False, False)
        body(PAIRS - 2, 0, False, False)
        body(PAIRS - 1, 1, False, True)

    UNITS = 4 * PAIRS
    PAIR_STEPS_END = 9 * (PAIRS - 1) + 5 + 2

    block = nc.Block()
    with block:

        @block.sync
        def _(sp):
            sp.dma_start(const[:, :], const_d).then_inc(const_in, 16)
            sp.dma_start(x_all[:, 0:4 * D].rearrange("p (t d) -> p t d", d=D),
                         x_d[0:4 * P, :].rearrange("(t p) d -> p t d", p=P)).then_inc(x_in, 16)
            sp.dma_start(cbuf[:, :, :], ctx_d[0:2 * P, :].rearrange("(t p) d -> p t d", p=P)).then_inc(ctx_in, 16)
            sp.dma_start(wq_raw[:, :, :], wq_d.rearrange("(c p) n -> p c n", p=P)).then_inc(wq_in, 16)
            sp.dma_start(wk_raw[:, :, :], wk_d.rearrange("(c p) n -> p c n", p=P)).then_inc(wk_in, 16)
            sp.dma_start(wv_raw[:, :, :], wv_d.rearrange("(c p) n -> p c n", p=P)).then_inc(wv_in, 16)
            sp.dma_start(x_all[:, 4 * D:].rearrange("p (t d) -> p t d", d=D),
                         x_d[4 * P:, :].rearrange("(t p) d -> p t d", p=P)).then_inc(x_rest_in, 16)
            sp.wait_ge(w_ready, 3)
            sp.dma_start(stage1[:, 0:W1S].rearrange("p (c n) -> p c n", c=KC),
                         ws1_d.rearrange("(c p) n -> p c n", p=P)).then_inc(shared_in, 16)
            sp.dma_start(stage2[:, 0:W2S].rearrange("p (c n) -> p c n", n=D),
                         ws2_d.rearrange("(c p) n -> p c n", p=P)).then_inc(shared_in, 16)

            def load_ctx(pp):
                sp.dma_start(cbuf[:, :, :], ctx_d[bass.ds(pp * 2 * P, 2 * P), :]
                             .rearrange("(t p) d -> p t d", p=P)).then_inc(ctx_in, 16)

            sp.wait_ge(xb_ready, PROJ.index("cT") + 1)
            load_ctx(1)

            def save_xn2(q):
                sp.wait_ge(xn2_ready, q + 1)
                sp.dma_start(xn2_all[:, bass.ds(q * 2 * D, 2 * D)], xn2p[:, :, :].rearrange("p t d -> p (t d)")).then_inc(xn2_saved, 16)
                sp.dma_start(xn2_dram[bass.ds(q * 2 * P, 2 * P), :].rearrange("(t p) d -> p t d", p=P),
                             xn2p[:, :, :]).then_inc(xn2_saved, 16)

            def pair(p, par, first, last):
                if not last:
                    sp.wait_ge(xb_ready, index_of("cT", p, first, last) + 1)
                    load_ctx(p + 2)
                if not first:
                    save_xn2(p - 1)

            pair(0, 0, True, False)
            with sp.Fori(0, (PAIRS - 4) // 2) as i:
                pair(i * 2 + 1, 1, False, False)
                pair(i * 2 + 2, 0, False, False)
            pair(PAIRS - 3, 1, False, False)
            save_xn2(PAIRS - 3)
            save_xn2(PAIRS - 2)
            save_xn2(PAIRS - 1)

            def load_row(src, t, s):
                if not (isinstance(t, int) and t == 0):
                    sp.wait_ge(xt_ready, t)
                sp.dma_start(xrow[:, :], src[bass.ds(s * P, P), :]).then_inc(xrow_in, 16)

            sp.wait_ge(xn2_saved, 32 * PAIRS)
            load_row(xn2_dram, 0, 0)
            with sp.Fori(1, TILES) as s:
                load_row(xn2_dram, s, s)
            sp.wait_ge(scattered, 16 * 2 * TILES)
            def store_y(s):
                sp.wait_ge(y_done, TILES + s + 1)
                sp.dma_start(rows_out[bass.ds(s * P, P), :], y_row[:, :]).then_inc(y_out, 16)

            for s in range(3):
                load_row(rows_in, s + TILES, s)
            with sp.Fori(3, SLOTS) as s:
                store_y(s - 3)
                load_row(rows_in, s + TILES, s)
            for s in range(SLOTS - 3, SLOTS):
                store_y(s)
            for t in range(TILES):
                sp.wait_ge(combined, 2 * (t + 1))
                sp.dma_start(out_d[t * P:(t + 1) * P, :], x_all[:, t * D:(t + 1) * D]).then_inc(stored, 16)
            sp.wait_ge(stored, 16 * TILES)

        @block.tensor
        def _(pe):
            def transposes(dst, src, n):
                for c in range(KC):
                    for b in range(n):
                        last = pe_.transpose(dst[:, (c * n + b) * P:(c * n + b + 1) * P],
                                             src[:, b, c * P:(c + 1) * P], ident)
                return last

            def step(s, pp, par, idx, bank):
                before_it = idx - (0 if s == "k0" else 1)
                if not (isinstance(before_it, int) and before_it <= 0):
                    pe.wait_ge(xb_free, before_it)
                ps = step_bank[bank]
                if s == "xT":
                    pe.wait_ge(xn1_ready, pp + 1)
                    last = transposes(ps, xn1, 2)
                elif s == "cT":
                    pe.wait_ge(ctx_in, 16 * (pp + 1))
                    last = transposes(ps, cbuf, 2)
                elif s[0] in "qk":
                    wh, wl, a = (wqh, wql, 0) if s[0] == "q" else (wkh, wkl, 1)
                    for gg in range(2):
                        cols = slice((2 * int(s[1]) + gg) * P, (2 * int(s[1]) + gg + 1) * P)
                        n = 0
                        for w, t in ((wh, aTh), (wh, aTl), (wl, aTh)):
                            for c in range(KC):
                                last = pe_.matmul(ps[:, gg * 256:(gg + 1) * 256], w[:, c, cols], t[a][:, c, :],
                                                  start=n == 0, stop=n == 5)
                                n += 1
                else:
                    for b in range(2):
                        n = 0
                        for t, w in ((aTh, wvh), (aTh, wvl), (aTl, wvh)):
                            for c in range(KC):
                                pe_.matmul(ps[:, b * D:(b + 1) * D], t[1][:, c, b * P:(b + 1) * P], w[:, c, :],
                                           start=n == 0, stop=False)
                                n += 1
                        last = pe_.matmul(ps[:, b * D:(b + 1) * D], sel_v[:, :], bias_tab[:, 0:D],
                                          start=False, stop=True)
                last.then_inc(xb_ready, 1)

            def router(s, q, idx, bank):
                pe.wait_ge(xb_free, idx - (1 if s == "r" else 0))
                ps = step_bank[bank]
                if s == "r":
                    pe.wait_ge(xn2_ready, q + 1)
                    last = transposes(ps, xn2p, 2)
                else:
                    for b in range(2):
                        for c in range(KC):
                            last = pe_.matmul(ps[:, b * E:(b + 1) * E], xn2T[:, c, b * P:(b + 1) * P], wr[:, c, :],
                                              start=c == 0, stop=c == KC - 1)
                last.then_inc(xb_ready, 1)

            def scores(p, par, n):
                b, u = n // 2, n % 2
                U = p * 4 + n
                if not (isinstance(p, int) and p == 0 and n < 2):
                    pe.wait_ge(shifted, U - 1)
                for jj in range(2):
                    j = 2 * u + jj
                    pe_.matmul(ps_s[:, j, :].rearrange("p (g t) -> p g t", g=4), ident_b[:, :],
                               mask_b[:, bass.ds(p * 2 + b, 1), :].broadcast_to([P, 4, P]), start=True, stop=False)
                for jj in range(2):
                    j = 2 * u + jj
                    for g in range(4):
                        for k in (k_hi, k_lo):
                            last = pe_.matmul(ps_s[:, j, g * P:(g + 1) * P],
                                              q_st[par][32 * j:32 * j + 32, g, b * P:(b + 1) * P],
                                              k[par][32 * j:32 * j + 32, g, b * P:(b + 1) * P],
                                              start=False, stop=g == 3 and k is k_lo)
                last.then_inc(scores_ready, 1)

            def prob_transposes(U, n, jj):
                pe.wait_ge(exp_done, U + 1)
                if not (isinstance(U, int) and U == 0 and jj == 0):
                    pe.wait_ge(pt_copied, 2 * U + jj)
                for g in range(4):
                    last = pe_.transpose(ps_t[:, 0, g * P:(g + 1) * P], prob[n % 2][:, jj, g, :], ident)
                last.then_inc(pt_ready, 1)

            def values(U, n, par, batch, jj):
                b, u = n // 2, n % 2
                pe.wait_ge(pt_copied, 2 * U + jj + 1)
                if u == 0 and jj == 0 and not (isinstance(batch, int) and batch == 0):
                    pe.wait_ge(normed, batch)
                for g in range(4):
                    h = 4 * g + 2 * u + jj
                    j = 2 * u + jj
                    last = pe_.matmul(ps_o[32 * j:32 * j + VW, g * P:(g + 1) * P], v_sb[par][:, b, h, :],
                                      probT[:, jj, g, :], start=True, stop=True)
                last.then_inc(pv_done, 1)

            def out_transposes(batch):
                pe.wait_ge(ot_copied, batch + 1)
                for g in range(4):
                    last = pe_.transpose(ps_o[:, g * P:(g + 1) * P], outT[:, g * P:(g + 1) * P], ident)
                last.then_inc(ot_ready, 1)

            pe.wait_ge(consts_ready, 1)
            pe.wait_ge(w_ready, 3)
            pe.wait_ge(bias_ready, 1)
            for k, s in enumerate(PROJ):
                step(s, 0, 0, k, k % 2)
            pe.wait_ge(masks_ready, 1)
            pe.wait_ge(misc_in, 16 * 4)

            def pair(p, par, first, last):
                for n in range(4):
                    if n == 0:
                        pe.wait_ge(xb_free, before(p, 0, 0, first, last))
                    scores(p, par, n)
                    rest = list(enumerate(steps(n, first, last)))
                    prev = not (first and n == 0)
                    pn, ppar, pbatch = (n - 1) % 4, par if n else 1 - par, p * 2 + (n - 1) // 2

                    def next_step():
                        if rest:
                            k, st = rest.pop(0)
                            idx, bank = before(p, n, k, first, last), before(par, n, k, first, last) % 2
                            if st in ("r", "l"):
                                router(st, p - 1, idx, bank)
                            else:
                                step(st, p + 1, 1 - par, idx, bank)

                    if prev:
                        prob_transposes(p * 4 + n - 1, pn, 0)
                    next_step()
                    if prev:
                        prob_transposes(p * 4 + n - 1, pn, 1)
                        values(p * 4 + n - 1, pn, ppar, pbatch, 0)
                    next_step()
                    if prev:
                        values(p * 4 + n - 1, pn, ppar, pbatch, 1)
                    next_step()
                    if n % 2 == 0 and prev:
                        out_transposes(pbatch)

            each_pair(pe, pair)
            for jj in range(2):
                prob_transposes(UNITS - 1, 3, jj)
                values(UNITS - 1, 3, 1, B - 1, jj)
            out_transposes(B - 1)
            router("r", PAIRS - 1, PAIR_STEPS_END, PAIR_STEPS_END % 2)
            router("l", PAIRS - 1, PAIR_STEPS_END + 1, (PAIR_STEPS_END + 1) % 2)

            def up(t, s, u, routed, place):
                half_w = (HR if routed else HS) // 2
                w1 = W1R if routed else W1S
                full = 2 * (HR if routed else HS)
                if u == 0:
                    pe.wait_ge(xt_lo, t + 1)
                    if routed:
                        pe.wait_ge(sel_up_ready, s + 1)
                if not (isinstance(t, int) and t == 0):
                    pe.wait_ge(hid_done[u], t)
                for part in range(2):
                    out = ps_s[:, 2 * u + part, 0:half_w]
                    lo_col = part * (full // 2) + u * half_w
                    n = 0
                    for x, off in ((xTh, 0), (xTh, w1), (xTl, 0)):
                        for c in range(KC):
                            a = off + c * full + lo_col
                            pe_.matmul(out, x[:, c, :], weights(place, a, half_w), start=n == 0, stop=False)
                            n += 1
                    sel = sel_up if routed else sel_s
                    last = pe_.matmul(out, sel[:, :], bias_tab[:, lo_col:lo_col + half_w], start=False, stop=True)
                last.then_inc(up_ready[u], 1)

            def weights(place, a, width):
                return ring[:, bass.ds(place, 1), a:a + width].rearrange("p o n -> p (o n)")

            def hid_transposes(t, u, routed):
                nch = (HR if routed else HS) // 2 // P
                pe.wait_ge(hid_done[u], t + 1)
                if not (isinstance(t, int) and t == 0):
                    pe.wait_ge(ht_lo[u], t)
                for c in range(nch):
                    last = pe_.transpose(ps_t[:, u, c * P:(c + 1) * P], hid[u][:, c * P:(c + 1) * P], ident)
                last.then_inc(ht_ready[u], 1)

            def x_transposes(t):
                pe.wait_ge(xrow_in, (t + 1) * 16)
                if not (isinstance(t, int) and t == 0):
                    pe.wait_ge(xt_lo, t)
                for c in range(KC):
                    last = pe_.transpose(ps_x[:, c * P:(c + 1) * P], xrow[:, c * P:(c + 1) * P], ident)
                last.then_inc(xt_ready, 1)

            def down(t, s, routed, place):
                nch = (HR if routed else HS) // 2 // P
                w1 = W1R if routed else W1S
                w2 = W2R if routed else W2S
                pe.wait_ge(ht_lo[0], t + 1)
                pe.wait_ge(ht_lo[1], t + 1)
                if routed:
                    pe.wait_ge(sel_down_ready, s + 1)
                if not (isinstance(t, int) and t == 0):
                    pe.wait_ge(y_done, t)
                n = 0
                for u in range(2):
                    for c in range(nch):
                        for h, off in ((hTh, 2 * w1), (hTh, 2 * w1 + w2), (hTl, 2 * w1)):
                            a = off + (u * nch + c) * D
                            pe_.matmul(ps_o[:, 0:D], h[u][:, c, :], weights(place, a, D), start=n == 0, stop=False)
                            n += 1
                sel = sel_down if routed else sel_s
                lo_col = 2 * HR if routed else 2 * HS
                pe_.matmul(ps_o[:, 0:D], sel[:, :], bias_tab[:, lo_col:lo_col + D], start=False, stop=True)\
                    .then_inc(y_ready, 1)

            pe.wait_ge(chosen_ready, 1)
            pe_.matmul(ps_o[:, 0:TILES * E], upper_b[:, :], chosen[:, :, :].rearrange("p t e -> p (t e)"),
                       start=True, stop=False)
            for j in range(TILES - 1):
                k = TILES - 1 - j
                pe_.matmul(ps_o[:, (j + 1) * E:TILES * E].rearrange("p (t e) -> p t e", e=E), ones_b[:, :],
                           chosen[:, j:j + 1, :].broadcast_to([P, k, E]), start=False, stop=j == TILES - 2)
            for j in range(TILES):
                last = pe_.matmul(ps_o[:, TILES * E:(TILES + 1) * E], ones_b[:, :], chosen[:, j, :],
                                  start=j == 0, stop=j == TILES - 1)
            last.then_inc(ranks_ready, 1)
            pe.wait_ge(rows_ready, 1)

            pe.wait_ge(xb_free, PAIR_STEPS_END + 2)
            pe.wait_ge(conv_hi, 1)
            pe.wait_ge(converted, 1)
            x_transposes(0)

            def tile(t, s, routed, place, prev, prev_routed=None, last=False):
                if prev is not None:
                    hid_transposes(t - 1, 0, prev_routed)
                up(t, s, 0, routed, place)
                if prev is not None:
                    hid_transposes(t - 1, 1, prev_routed)
                up(t, s, 1, routed, place)
                if not last:
                    x_transposes(t + 1)
                if prev is not None:
                    down(t - 1, s - 1, prev_routed, prev)

            def ring_place(s):
                return pe.value_load(tab_ring[0:1, bass.ds(s, 1)], min_val=0, max_val=RING - 1)

            def expert_ready(s):
                need = pe.value_load(tab_need[0:1, bass.ds(s, 1)], min_val=2, max_val=E + 1)
                pe.wait_ge(converted, need)

            SH = RING - 1
            TURN = 3
            assert (TILES - 1) % TURN == 0
            tile(0, 0, False, SH, None)
            with pe.Fori(0, (TILES - 1) // TURN) as i:
                for k in range(TURN):
                    s = i * TURN + (k + 1)
                    tile(s, s, False, SH, SH, False)

            pe.wait_ge(tables_ready, 1)
            place = ring_place(0)
            expert_ready(0)
            tile(TILES, 0, True, place, SH, False)
            turns = (SLOTS - 2) // TURN
            with pe.Fori(0, turns) as i:
                prev = ring_place(i * TURN)
                for k in range(TURN):
                    s = i * TURN + (k + 1)
                    place = ring_place(s)
                    expert_ready(s)
                    tile(s + TILES, s, True, place, prev, True)
                    prev = place
            prev = ring_place(turns * TURN)
            for s in range(turns * TURN + 1, SLOTS):
                place = ring_place(s)
                expert_ready(s)
                tile(s + TILES, s, True, place, prev, True, s == SLOTS - 1)
                prev = place
            hid_transposes(TILES + SLOTS - 1, 0, True)
            hid_transposes(TILES + SLOTS - 1, 1, True)
            down(TILES + SLOTS - 1, SLOTS - 1, True, place)

        @block.scalar
        def _(sc):
            sc.dma_start(bias_raw[:, :], bias_d).then_inc(bias_in, 16)
            sc.dma_start(pad_b[:, :], pad_d.partition_broadcast(P)).then_inc(mask_in, 16)
            sc.dma_start(sub_b[:, :], sub_d).then_inc(mask_in, 16)
            sc.dma_start(bqs[:, :], bq_d).then_inc(misc_in, 16)
            sc.dma_start(bks[:, :], bk_d).then_inc(misc_in, 16)
            sc.dma_start(wr[:, :, :], wr_d.rearrange("(c p) n -> p c n", p=P)).then_inc(misc_in, 16)
            sc.dma_start(br[:, :], br_d.partition_broadcast(P)).then_inc(misc_in, 16)
            sc.wait_ge(zero_ready, 1)
            sc.dma_start(rows_in.rearrange("(s p) d -> p s d", p=P),
                         y_row[:, :].rearrange("p (o d) -> p o d", o=1).broadcast_to([P, SLOTS, D])).then_inc(zero_out, 16)
            sc.wait_ge(wq_in, 16)
            act.activation(wqh[:, :, :], wq_raw[:, :, :], ACT.Identity).then_inc(w_hi, 1)
            sc.wait_ge(wk_in, 16)
            act.activation(wkh[:, :, :], wk_raw[:, :, :], ACT.Identity).then_inc(w_hi, 1)
            sc.wait_ge(wv_in, 16)
            act.activation(wvh[:, :, :], wv_raw[:, :, :], ACT.Identity).then_inc(w_hi, 1)
            sc.wait_ge(consts_ready, 1)
            sc.wait_ge(misc_in, 64)

            def step(s, pp, par, idx, bank):
                ps = step_bank[bank]
                sc.wait_ge(xb_ready, idx + 1)
                if s in ("xT", "cT"):
                    act.activation(aTh[s == "cT"][:, :, :], ps[:, :].rearrange("p (c n) -> p c n", c=KC),
                                   ACT.Identity).then_inc(xb_hi, 1)
                elif s[0] in "qk":
                    for gg in range(2):
                        g = 2 * int(s[1]) + gg
                        src = ps[:, gg * 256:(gg + 1) * 256]
                        if s[0] == "q":
                            last = act.activation(q_cut[:, g, :], src, ACT.Identity, bias=bqc[:, g:g + 1],
                                                  scale=const[:, C_LOQ:C_LOQ + 1])
                        else:
                            last = act.activation(k_hi[par][:, g, :], src, ACT.Identity, bias=bks[:, g:g + 1])
                    last.then_inc(xb_hi, 1)
                else:
                    sc.wait_ge(xb_free, idx)
                    act.activation(v_sb[par][:, :, :, 0:HD],
                                   ps[:, :].rearrange("p (b h d) -> p b h d", b=2, h=H), ACT.Identity)\
                        .then_inc(xb_free, 1)

            EXP_AT = 1

            def prob_copy(U, jj):
                sc.wait_ge(pt_ready, 2 * U + jj + 1)
                if not (isinstance(U, int) and U == 0):
                    sc.wait_ge(pv_done, 2 * U + jj - 1)
                act.activation(probT[:, jj, :, :], ps_t[:, 0, :].rearrange("p (g t) -> p g t", g=4),
                               ACT.Identity).then_inc(pt_copied, 1)

            def out_copy(batch):
                sc.wait_ge(pv_done, batch * 4 + 4)
                act.activation(outT[:, :], ps_o[:, :], ACT.Identity).then_inc(ot_copied, 1)

            def exp(U, n):
                sc.wait_ge(shifted, U + 1)
                act.activation(prob[n % 2][:, :, :, :], prob[n % 2][:, :, :, :], ACT.Exp, scale=1.0 / HD ** 0.5)\
                    .then_inc(exp_done, 1)

            def router(s, idx, bank):
                if s == "r":
                    ps = step_bank[bank]
                    sc.wait_ge(xb_ready, idx + 1)
                    sc.wait_ge(xb_free, idx)
                    act.activation(xn2T[:, :, :], ps[:, :].rearrange("p (c n) -> p c n", c=KC), ACT.Identity)\
                        .then_inc(xb_free, 1)

            for k, s in enumerate(PROJ):
                step(s, 0, 0, k, k % 2)

            def pair(p, par, first, last):
                for n in range(4):
                    U = p * 4 + n - 1
                    rest = list(enumerate(steps(n, first, last)))
                    prev = not (first and n == 0)

                    def next_step():
                        if rest:
                            k, st = rest.pop(0)
                            idx, bank = before(p, n, k, first, last), before(par, n, k, first, last) % 2
                            if st in "rl":
                                router(st, idx, bank)
                            else:
                                step(st, p + 1, 1 - par, idx, bank)

                    if prev:
                        prob_copy(U, 0)
                    next_step()
                    if prev:
                        prob_copy(U, 1)
                    if EXP_AT == 1:
                        exp(p * 4 + n, n)
                    next_step()
                    if EXP_AT == 2:
                        exp(p * 4 + n, n)
                    if n % 2 == 0 and prev:
                        out_copy(p * 2 + (n - 1) // 2)
                    next_step()

            each_pair(sc, pair)
            for jj in range(2):
                prob_copy(UNITS - 1, jj)
            out_copy(B - 1)
            router("r", PAIR_STEPS_END, PAIR_STEPS_END % 2)
            sc.wait_ge(gap_ready, 1)
            act.activation(ex[:, :], ex[:, :], ACT.Exp).then_inc(ex_ready, 1)

            def gelu(t, u, routed):
                half_w = (HR if routed else HS) // 2
                sc.wait_ge(up_ready[u], t + 1)
                if not (isinstance(t, int) and t == 0):
                    sc.wait_ge(hid_done[u], t)
                act.activation(gel[u][:, 0:half_w], ps_s[:, 2 * u + 1, 0:half_w], ACT.Gelu)\
                    .then_inc(gelu_done[u], 1)

            def hid_hi(t, u, routed):
                nch = (HR if routed else HS) // 2 // P
                sc.wait_ge(ht_ready[u], t + 1)
                if not (isinstance(t, int) and t == 0):
                    sc.wait_ge(y_ready, t)
                act.activation(hTh[u][:, 0:nch, :], ps_t[:, u, 0:nch * P].rearrange("p (c n) -> p c n", c=nch),
                               ACT.Identity).then_inc(ht_hi[u], 1)

            def x_hi(t):
                sc.wait_ge(xt_ready, t + 1)
                if not (isinstance(t, int) and t == 0):
                    sc.wait_ge(up_ready[1], t)
                act.activation(xTh[:, :, :], ps_x[:, 0:D].rearrange("p (c n) -> p c n", c=KC), ACT.Identity)\
                    .then_inc(xt_hi, 1)

            def pick_up(s):
                if not (isinstance(s, int) and s == 0):
                    sc.wait_ge(up_ready[1], s + TILES)
                act.activation(sel_up[:, :], sel_ind[:, bass.ds(s, 1)].broadcast_to([2 * ROWS, P]), ACT.Identity)\
                    .then_inc(sel_up_ready, 1)

            def pick_down(s):
                if not (isinstance(s, int) and s == 0):
                    sc.wait_ge(y_ready, s + TILES)
                act.activation(sel_down[:, :], sel_ind[:, bass.ds(s, 1)].broadcast_to([2 * ROWS, P]), ACT.Identity)\
                    .then_inc(sel_down_ready, 1)

            def tile(t, s, routed, prev_routed=None, last=False):
                if prev_routed is not None:
                    hid_hi(t - 1, 0, prev_routed)
                gelu(t, 0, routed)
                if prev_routed is not None:
                    hid_hi(t - 1, 1, prev_routed)
                    if prev_routed:
                        pick_down(s - 1)
                gelu(t, 1, routed)
                if not last:
                    x_hi(t + 1)
                    if routed:
                        pick_up(s + 1)

            x_hi(0)
            tile(0, 0, False)
            with sc.Fori(1, TILES) as s:
                tile(s, s, False, False)
            sc.wait_ge(tables_ready, 1)
            pick_up(0)
            tile(TILES, 0, True, False)
            with sc.Fori(1, SLOTS - 1) as s:
                tile(s + TILES, s, True, True)
            tile(TILES + SLOTS - 1, SLOTS - 1, True, True, True)
            hid_hi(TILES + SLOTS - 1, 0, True)
            hid_hi(TILES + SLOTS - 1, 1, True)
            pick_down(SLOTS - 1)

        @block.vector
        def _(ve):
            own_steps = [0]

            def chain(ins):
                own_steps[0] += 1
                ins.then_inc(vstep, 1)
                ve.wait_ge(vstep, own_steps[0])

            vec.memset(y_row[:, :], 0.0).then_inc(zero_ready, 1)
            vec.memset(half[:, :], -0.5)
            vec.memset(eps[:, :], EPS)
            vec.memset(ones_b[:, :], 1.0)
            for par in range(2):
                vec.memset(v_sb[par][:, :, :, HD:VW], 0.0).then_inc(mstep, 1)
            ve.wait_ge(mstep, 2)
            for par in range(2):
                vec.memset(v_sb[par][:, :, :, HD:HD + 1], 1.0)
            ve.wait_ge(const_in, 16)
            vec.tensor_copy(ident_b[:, :], const[:, C_ID:C_ID + P])
            vec.tensor_copy(upper_b[:, :], const[:, C_UP:C_UP + P])
            for t, row in ((sel_v, V_ROW), (sel_s, SHARED_ROW)):
                vec.tensor_scalar(t[:, :], const[0:2 * ROWS, C_ROW:C_ROW + 1].broadcast_to([2 * ROWS, P]), float(row), None,
                                  ALU.is_equal)
            ve.wait_ge(misc_in, 64)
            vec.tensor_scalar(bqc[:, :], bqs[:, :], const[:, C_LOQ:C_LOQ + 1], None, ALU.mult)\
                .then_inc(consts_ready, 1)
            ve.wait_ge(bias_in, 16)
            vec.tensor_scalar(bias_cut[:, :], bias_raw[:, :], const[0:2 * ROWS, C_LOB:C_LOB + 1], None, ALU.mult)\
                .then_inc(bias_cut_done, 1)
            ve.wait_ge(bias_cut_done, 1)
            vec.tensor_tensor(bias_tab[:, :], bias_raw[:, :], bias_cut[:, :].bitcast(f32), ALU.subtract)\
                .then_inc(bias_ready, 1)

            def ln1_stats(pp):
                for b in range(2):
                    vec.bn_stats(bn1[:, b, :], x_all[:, bass.ds((pp * 2 + b) * D, D)]).then_inc(ln1_bn, 1)
                ve.wait_ge(ln1_bn, pp * 2 + 2)
                vec.memset(tick[:, :], 0.0)
                for b in range(2):
                    last = vec.bn_aggr(mv1[:, b, :], bn1[:, b, :])
                last.then_inc(ln1_var, 1)

            def ln1_apply(pp):
                ve.wait_ge(ln1_rs, pp + 1)
                for b in range(2):
                    last = vec.tensor_scalar(xn1[:, b, :], x_all[:, bass.ds((pp * 2 + b) * D, D)], mv1[:, b, 0:1],
                                             rs1[:, b:b + 1], ALU.subtract, ALU.mult)
                last.then_inc(xn1_ready, 1)

            ve.wait_ge(x_in, 16)
            ln1_stats(0)
            for n, (lo, raw, hi) in enumerate(((wql, wq_raw, wqh), (wkl, wk_raw, wkh), (wvl, wv_raw, wvh))):
                ve.wait_ge(w_hi, n + 1)
                vec.tensor_tensor(lo[:, :, :], raw[:, :, :], hi[:, :, :].bitcast(f32), ALU.subtract).then_inc(w_ready, 1)
                if n == 0:
                    ln1_apply(0)

            def step(s, pp, par, idx, hi_idx, bank):
                ps = step_bank[bank]
                if s in HI:
                    ve.wait_ge(xb_hi, hi_idx + 1)
                if s in ("xT", "cT"):
                    a = int(s == "cT")
                    vec.tensor_tensor(aTl[a][:, :, :], ps[:, :].rearrange("p (c n) -> p c n", c=KC),
                                      aTh[a][:, :, :].bitcast(f32), ALU.subtract).then_inc(xb_free, 1)
                elif s[0] in "qk":
                    for gg in range(2):
                        g = 2 * int(s[1]) + gg
                        src = ps[:, gg * 256:(gg + 1) * 256]
                        if s[0] == "q":
                            last = vec.scalar_tensor_tensor(q_st[par][:, g, :], src, bqs[:, g:g + 1],
                                                            q_cut[:, g, :].bitcast(f32), ALU.add, ALU.subtract)
                        else:
                            last = vec.scalar_tensor_tensor(k_lo[par][:, g, :], src, bks[:, g:g + 1],
                                                            k_hi[par][:, g, :].bitcast(f32), ALU.add, ALU.subtract)
                    last.then_inc(xb_free, 1)

            def router(s, q, idx, bank):
                ps = step_bank[bank]
                if s == "l":
                    ve.wait_ge(xb_ready, idx + 1)
                    vec.tensor_tensor(logits[:, bass.ds(q * 2, 2), :], ps[:, 0:2 * E].rearrange("p (t e) -> p t e", e=E),
                                      br[:, :].rearrange("p (o e) -> p o e", o=1).broadcast_to([P, 2, E]), ALU.add)\
                        .then_inc(xb_free, 1)

            for k, s in enumerate(PROJ):
                step(s, 0, 0, k, HI.index(s) if s in HI else 0, k % 2)
                if s == "xT":
                    ln1_stats(1)
                    ve.wait_ge(xb_ready, k + 1)
                    ln1_apply(1)
            ve.wait_ge(mask_in, 32)
            vec.tensor_scalar(keep[:, :, :].rearrange("p b t -> p (b t)"), pad_b[:, :], 0.0, None, ALU.not_equal)\
                .then_inc(mstep, 1)
            vec.tensor_scalar(keep_s[:, :], sub_b[:, :], 0.0, None, ALU.not_equal).then_inc(mstep, 1)
            ve.wait_ge(mstep, 4)
            ve.wait_ge(bias_ready, 1)
            vec.tensor_tensor(keep[:, :, :], keep[:, :, :],
                              keep_s[:, :].rearrange("p (o t) -> p o t", o=1).broadcast_to([P, B, S]), ALU.mult)\
                .then_inc(mstep, 1)
            ve.wait_ge(mstep, 5)
            vec.tensor_scalar(mask_b[:, :, :], keep[:, :, :], -FILL, FILL, ALU.mult, ALU.add).then_inc(masks_ready, 1)
            ve.wait_ge(x_rest_in, 16)

            def softmax_shift(U, n):
                u = n % 2
                ve.wait_ge(scores_ready, U + 1)
                src = ps_s[:, 2 * u:2 * u + 2, :].rearrange("p j (g t) -> p j g t", g=4)
                if not (isinstance(U, int) and U == 0):
                    ve.wait_ge(shifted, U)
                vec.tensor_reduce(nmax[:, :, :], src, AX.X, ALU.max, negate=True).then_inc(maxed, 1)
                ve.wait_ge(maxed, U + 1)
                if not (isinstance(U, int) and U < 2):
                    ve.wait_ge(pt_ready, 2 * (U - 1))
                vec.tensor_tensor(prob[n % 2][:, :, :, :], src,
                                  nmax[:, :, :].rearrange("p j (g o) -> p j g o", o=1).broadcast_to([P, 2, 4, P]), ALU.add)\
                    .then_inc(shifted, 1)

            def norm(p, b):
                ve.wait_ge(ot_ready, p * 2 + b + 1)
                o = ps_o[:, :].rearrange("p (h d) -> p h d", d=VW)
                vec.reciprocal(rden[:, :], o[:, :, HD]).then_inc(nstep, 1)
                ve.wait_ge(nstep, (p * 2 + b) * 3 + 1)
                vec.tensor_tensor(att[:, :].rearrange("p (h d) -> p h d", d=HD), o[:, :, 0:HD],
                                  rden[:, :].rearrange("p (h o) -> p h o", o=1).broadcast_to([P, H, HD]), ALU.mult)\
                    .then_inc(nstep, 1)
                ve.wait_ge(nstep, (p * 2 + b) * 3 + 2)
                xs = x_all[:, bass.ds((p * 2 + b) * D, D)]
                vec.tensor_tensor(xs, xs, att[:, :], ALU.add).then_inc(normed, 1)
                ve.wait_ge(normed, p * 2 + b + 1)
                vec.memset(tick[:, :], 0.0)
                vec.bn_stats(bn2[:, b, :], xs).then_inc(nstep, 1)
                if b == 1:
                    ve.wait_ge(nstep, (p * 2 + b) * 3 + 3)
                    vec.memset(tick[:, :], 0.0)
                    for i in range(2):
                        last = vec.bn_aggr(mv2[:, i, :], bn2[:, i, :])
                    last.then_inc(ln2_var, 1)

            def ln2_apply(q):
                ve.wait_ge(ln2_rs, q + 1)
                if not (isinstance(q, int) and q == 0):
                    ve.wait_ge(xn2_saved, q * 32)
                for b in range(2):
                    last = vec.tensor_scalar(xn2p[:, b, :], x_all[:, bass.ds((q * 2 + b) * D, D)], mv2[:, b, 0:1],
                                             rs2[:, b:b + 1], ALU.subtract, ALU.mult)
                last.then_inc(xn2_ready, 1)

            def pair(p, par, first, last):
                for n in range(4):
                    softmax_shift(p * 4 + n, n)
                    for k, st in enumerate(steps(n, first, last) or [None]):
                        idx = before(p, n, k, first, last)
                        bank = before(par, n, k, first, last) % 2
                        if st in ("r", "l"):
                            router(st, p - 1, idx, bank)
                        elif st:
                            step(st, p + 1, 1 - par, idx, (p + 1) * len(HI) + (HI.index(st) if st in HI else 0), bank)
                    if n == 0 and not first:
                        norm(p - 1, 1)
                    if n == 1 and not first:
                        ln2_apply(p - 1)
                    if n == 1 and not last and not (isinstance(p, int) and p + 2 >= PAIRS):
                        ln1_stats(p + 2)
                    if n == 2:
                        norm(p, 0)
                    if n == 3 and not last and not (isinstance(p, int) and p + 2 >= PAIRS):
                        ve.wait_ge(xb_ready, index_of("xT", p, first, last) + 1)
                        ln1_apply(p + 2)

            each_pair(ve, pair)
            norm(PAIRS - 1, 1)
            ln2_apply(PAIRS - 1)
            router("l", PAIRS - 1, PAIR_STEPS_END + 1, (PAIR_STEPS_END + 1) % 2)

            base_steps = own_steps[0]
            three = [P, TILES, E]

            def over_experts(a):
                return a.rearrange("p (t o) -> p t o", o=1).broadcast_to(three)

            rank = const[:, C_RANK:C_RANK + E].rearrange("p (o e) -> p o e", o=1).broadcast_to(three)
            ve.wait_ge(xb_free, PAIR_STEPS_END + 2)
            chain(vec.tensor_scalar(lg[:, :, :], logits[:, :, :], 1.0 / TAU, None, ALU.mult))
            for k, pick in ((0, pick1), (1, pick2)):
                chain(vec.tensor_reduce(top[:, k, :], lg[:, :, :], AX.X, ALU.max))
                chain(vec.tensor_tensor(eq[:, :, :], lg[:, :, :], over_experts(top[:, k, :]), ALU.is_equal))
                chain(vec.tensor_tensor(eq[:, :, :], eq[:, :, :], rank, ALU.mult))
                chain(vec.tensor_reduce(best[:, :], eq[:, :, :], AX.X, ALU.max))
                chain(vec.tensor_tensor(pick[:, :, :], rank, over_experts(best[:, :]), ALU.is_equal))
                if k == 0:
                    chain(vec.scalar_tensor_tensor(lg[:, :, :], pick[:, :, :], FILL, lg[:, :, :], ALU.mult, ALU.add))
            vec.tensor_tensor(ex[:, :], top[:, 1, :], top[:, 0, :], ALU.subtract).then_inc(gap_ready, 1)
            vec.tensor_tensor(chosen[:, :, :], pick1[:, :, :], pick2[:, :, :], ALU.add).then_inc(chosen_ready, 1)
            ve.wait_ge(ranks_ready, 1)
            tot = ps_o[:, TILES * E:(TILES + 1) * E]
            vec.memset(ones_e[:, :], 1.0)
            chain(vec.tensor_scalar(cnt_i[:, :], tot, float(P - 1), None, ALU.add))
            chain(vec.tensor_scalar(cnt_s[:, :], cnt_i[:, :], 7, None, ALU.logical_shift_right))
            chain(vec.tensor_scalar(tiles_e[:, :], cnt_s[:, :], 1.0, None, ALU.max))
            chain(vec.tensor_tensor_scan(cum_e[:, :], ones_e[:, :], tiles_e[:, :], 0.0, ALU.mult, ALU.add))
            chain(vec.tensor_tensor(base_e[:, :], cum_e[:, :], tiles_e[:, :], ALU.subtract))
            chain(vec.tensor_scalar(base_e[:, :], base_e[:, :], float(P), None, ALU.mult))
            chain(vec.tensor_tensor(pos[:, :, :], ps_o[:, 0:TILES * E].rearrange("p (t e) -> p t e", e=E),
                                    base_e[:, :].rearrange("p (o e) -> p o e", o=1).broadcast_to(three), ALU.add))
            for k, pick in ((0, pick1), (1, pick2)):
                chain(vec.tensor_tensor(eq[:, :, :], pos[:, :, :], pick[:, :, :], ALU.mult))
                chain(vec.tensor_reduce(best[:, :], eq[:, :, :], AX.X, ALU.add))
                last = vec.tensor_copy(idx_top[:, k, :], best[:, :])
                if k == 0:
                    chain(last)
            last.then_inc(rows_ready, 1)
            wide = [P, SLOTS, E - 1]
            vec.tensor_scalar(tab_cum[:, :], cum_e[:, :], float(TILES), None, ALU.add)
            chain(vec.tensor_tensor(past[:, :, :],
                                    const[:, C_SLOT:C_SLOT + SLOTS].rearrange("p (s o) -> p s o", o=1).broadcast_to(wide),
                                    cum_e[:, 0:E - 1].rearrange("p (o e) -> p o e", o=1).broadcast_to(wide), ALU.is_ge))
            chain(vec.tensor_reduce(slot_e[:, :], past[:, :, :], AX.X, ALU.add))
            chain(vec.tensor_tensor(past2[:, :, :], past[:, :, :],
                                    const[:, C_STEP:C_STEP + E - 1].rearrange("p (o e) -> p o e", o=1).broadcast_to(wide),
                                    ALU.mult))
            chain(vec.tensor_reduce(slot_r[:, :], past2[:, :, :], AX.X, ALU.add))
            vec.tensor_copy(tab_ring[:, :], slot_r[:, :])
            vec.tensor_scalar(tab_need[:, :], slot_e[:, :], 2.0, None, ALU.add)
            vec.tensor_scalar(sel_ind[:, :], slot_e[0:2 * ROWS, :], const[0:2 * ROWS, C_ROW:C_ROW + 1], None, ALU.is_equal)\
                .then_inc(tables_ready, 1)
            ve.wait_ge(ex_ready, 1)
            chain(vec.tensor_scalar(top[:, 0, :], ex[:, :], 1.0, None, ALU.add))
            chain(vec.reciprocal(w_top[:, 0, :], top[:, 0, :]))
            chain(vec.tensor_tensor(w_top[:, 1, :], w_top[:, 0, :], ex[:, :], ALU.mult))

            def gate(t, u, routed):
                half_w = (HR if routed else HS) // 2
                ve.wait_ge(gelu_done[u], t + 1)
                if not (isinstance(t, int) and t == 0):
                    ve.wait_ge(ht_ready[u], t)
                vec.tensor_tensor(hid[u][:, 0:half_w], ps_s[:, 2 * u, 0:half_w], gel[u][:, 0:half_w], ALU.mult)\
                    .then_inc(hid_done[u], 1)

            def hid_lo(t, u, routed):
                nch = (HR if routed else HS) // 2 // P
                ve.wait_ge(ht_hi[u], t + 1)
                vec.tensor_tensor(hTl[u][:, 0:nch, :], ps_t[:, u, 0:nch * P].rearrange("p (c n) -> p c n", c=nch),
                                  hTh[u][:, 0:nch, :].bitcast(f32), ALU.subtract).then_inc(ht_lo[u], 1)

            def x_lo(t):
                ve.wait_ge(xt_hi, t + 1)
                vec.tensor_tensor(xTl[:, :, :], ps_x[:, 0:D].rearrange("p (c n) -> p c n", c=KC),
                                  xTh[:, :, :].bitcast(f32), ALU.subtract).then_inc(xt_lo, 1)

            def y_copy(t, s, routed):
                ve.wait_ge(y_ready, t + 1)
                if routed:
                    if not (isinstance(s, int) and s == 0):
                        ve.wait_ge(y_out, 16 * s)
                    vec.tensor_copy(y_row[:, :], ps_o[:, 0:D]).then_inc(y_done, 1)
                else:
                    a = x_all[:, bass.ds(s * D, D)]
                    vec.tensor_tensor(a, ps_o[:, 0:D], a, ALU.add).then_inc(y_done, 1)

            def tile(t, s, routed, prev_routed=None, last=False):
                if prev_routed is not None:
                    hid_lo(t - 1, 0, prev_routed)
                gate(t, 0, routed)
                if prev_routed is not None:
                    hid_lo(t - 1, 1, prev_routed)
                gate(t, 1, routed)
                if not last:
                    x_lo(t + 1)
                if prev_routed is not None:
                    y_copy(t - 1, s - 1 if routed == prev_routed else TILES - 1, prev_routed)

            x_lo(0)
            tile(0, 0, False)
            with ve.Fori(1, TILES) as s:
                tile(s, s, False, False)
            tile(TILES, 0, True, False)
            with ve.Fori(1, SLOTS - 1) as s:
                tile(s + TILES, s, True, True)
            tile(TILES + SLOTS - 1, SLOTS - 1, True, True, True)
            hid_lo(TILES + SLOTS - 1, 0, True)
            hid_lo(TILES + SLOTS - 1, 1, True)
            y_copy(TILES + SLOTS - 1, SLOTS - 1, True)

            for t in range(TILES):
                ve.wait_ge(gathered[t], 32)
                a = x_all[:, t * D:(t + 1) * D]
                for k in range(2):
                    vec.scalar_tensor_tensor(a, gath[:, t, k, :], w_top[:, k, t:t + 1], a, ALU.mult, ALU.add)\
                        .then_inc(combined, 1)
                    ve.wait_ge(combined, 2 * t + k + 1)

        @block.gpsimd
        def _(gp):
            def rstd(var_sem, out_sem, mv, ve_t, rs_t, q, step_sem):
                gp.wait_ge(var_sem, q + 1)
                pool.tensor_tensor(ve_t[:, :], mv[:, :, 1], eps[:, :], ALU.add).then_inc(step_sem, 1)
                gp.wait_ge(step_sem, q + 1)
                pool.tensor_tensor(rs_t[:, :], ve_t[:, :], half[:, :], ALU.pow).then_inc(out_sem, 1)

            def convert(src, hi_ap, lo_ap, count):
                pool.tensor_scalar(hi_ap, src, 1.0, 0.0, ALU.mult, ALU.add).then_inc(conv_hi, 1)
                gp.wait_ge(conv_hi, count)
                return pool.tensor_tensor(lo_ap, src, hi_ap.bitcast(f32), ALU.subtract)

            gp.wait_ge(consts_ready, 1)
            rstd(ln1_var, ln1_rs, mv1, ve1, rs1, 0, pstep)
            rstd(ln1_var, ln1_rs, mv1, ve1, rs1, 1, pstep)
            gp.wait_ge(shared_in, 32)
            SH = RING - 1
            convert(stage1[:, 0:W1S], ring[:, SH, 0:W1S], ring[:, SH, W1S:2 * W1S], 1)
            convert(stage2[:, 0:W2S], ring[:, SH, 2 * W1S:2 * W1S + W2S],
                    ring[:, SH, 2 * W1S + W2S:2 * W1S + 2 * W2S], 2).then_inc(converted, 1)

            def load_raw1(e):
                gp.dma_start(stage1[:, :].rearrange("p (c n) -> p c n", c=KC),
                             w1_d[e, :, :].rearrange("(c p) n -> p c n", p=P)).then_inc(raw1_in, 16)

            def load_raw2(e):
                gp.dma_start(stage2[:, :].rearrange("p (c n) -> p c n", n=D),
                             w2_d[e, :, :].rearrange("(c p) n -> p c n", p=P)).then_inc(raw2_in, 16)

            gp.wait_ge(converted, 1)
            load_raw1(0)
            load_raw2(0)

            def pair(p, par, first, last):
                if not first:
                    rstd(ln2_var, ln2_rs, mv2, ve2, rs2, p - 1, pstep2)
                if not last and not (isinstance(p, int) and p + 2 >= PAIRS):
                    rstd(ln1_var, ln1_rs, mv1, ve1, rs1, p + 2, pstep)

            each_pair(gp, pair)
            rstd(ln2_var, ln2_rs, mv2, ve2, rs2, PAIRS - 1, pstep2)

            def expert(e):
                r = e % RING
                gp.wait_ge(raw1_in, 16 * (e + 1))
                convert(stage1[:, :], ring[:, r, 0:W1R], ring[:, r, W1R:2 * W1R], 2 * e + 3).then_inc(pconv, 1)
                gp.wait_ge(pconv, e + 1)
                if e + 1 < E:
                    load_raw1(e + 1)
                gp.wait_ge(raw2_in, 16 * (e + 1))
                convert(stage2[:, :], ring[:, r, 2 * W1R:2 * W1R + W2R], ring[:, r, 2 * W1R + W2R:], 2 * e + 4)\
                    .then_inc(converted, 1)
                gp.wait_ge(converted, e + 2)
                if e + 1 < E:
                    load_raw2(e + 1)

            gp.wait_ge(pv_done, 2 * UNITS)
            gp.wait_ge(normed, B)
            gp.wait_ge(xb_free, PAIR_STEPS_END + 2)
            expert(0)
            gp.wait_ge(rows_ready, 1)
            gp.wait_ge(zero_out, 16)
            gp.wait_ge(xn2_saved, 32 * PAIRS)
            for t in range(TILES):
                for k in range(2):
                    gp.indirect_dma_start(
                        out=rows_in, out_offset=bass.IndirectOffsetOnAxis(ap=idx_top[:, k, t:t + 1], axis=0),
                        in_=xn2_all[:, t * D:(t + 1) * D], in_offset=None).then_inc(scattered, 16)
            expert(1)
            gp.wait_ge(tables_ready, 1)
            for e in range(2, E):
                if e == 2:
                    gp.wait_ge(y_done, TILES)
                else:
                    done = gp.value_load(tab_cum[0:1, e - RING:e - RING + 1], min_val=1, max_val=SLOTS + TILES)
                    gp.wait_ge(y_done, done)
                    pool.tensor_tensor(ptick[:, :], half[:, 0:1], half[:, 0:1], ALU.add)
                expert(e)
            gp.wait_ge(y_done, TILES + SLOTS)
            gp.wait_ge(y_out, 16 * SLOTS)
            for t in range(TILES):
                for k in range(2):
                    gp.indirect_dma_start(
                        out=gath[:, t, k, :], out_offset=None, in_=rows_out,
                        in_offset=bass.IndirectOffsetOnAxis(ap=idx_top[:, k, t:t + 1], axis=0))\
                        .then_inc(gathered[t], 16)


def kernel(**inputs):
    import numpy as np
    import concourse.bacc as bacc
    from concourse import mybir
    from concourse.bass_utils import run_bass_kernel_spmd

    def arr(name):
        return np.ascontiguousarray(inputs[name])

    def heads(w):
        v = w.reshape(w.shape[:-1] + (4, 4, 1, HD))
        return np.ascontiguousarray(np.broadcast_to(v, w.shape[:-1] + (4, 4, 2, HD)))

    wq = heads(arr("L0_xattn_Wq").T).reshape(D, 512)
    wk = heads(arr("L0_xattn_Wk").T).reshape(D, 512)
    bq = np.ascontiguousarray(heads(arr("L0_xattn_bq")).reshape(4, P).T)
    bk = np.ascontiguousarray(heads(arr("L0_xattn_bk")).reshape(4, P).T)
    wv = np.ascontiguousarray(arr("L0_xattn_Wv").T)
    bias = np.zeros((2, ROWS, BW), np.float32)
    bias[:, :E, :2 * HR] = arr("L0_ffn_be1")
    bias[:, :E, 2 * HR:] = arr("L0_ffn_be2")
    bias[:, SHARED_ROW, :2 * HS] = arr("L0_ffn_bs1")
    bias[:, SHARED_ROW, 2 * HS:2 * HS + D] = arr("L0_ffn_bs2")
    bias[:, V_ROW, :D] = arr("L0_xattn_bv")
    c = np.zeros((P, C_ALL), np.float32)
    c[:, C_ID:C_ID + P] = np.eye(P)
    c[:, C_UP:C_UP + P] = np.triu(np.ones((P, P)), 1)
    c[:, C_LOQ] = np.arange(P) % 32 >= HD
    c[:, C_LOB] = np.arange(P) >= ROWS
    c[:, C_ROW] = np.arange(P) % ROWS
    c[:, C_RANK:C_RANK + E] = E - np.arange(E)
    c[:, C_SLOT:C_SLOT + SLOTS] = np.arange(SLOTS)
    c[:, C_STEP:C_STEP + E - 1] = (np.arange(E - 1) + 1) % RING - np.arange(E - 1) % RING
    arrays = {
        "x": arr("x").reshape(N, D), "ctx": arr("ctx_1024").reshape(N, D),
        "pad": arr("mask_Bx1x1xS2_ik0").reshape(B * S).astype(np.int32),
        "sub": arr("mask_1x1xSxS2_ik0").reshape(S, S).astype(np.int32),
        "wq": wq, "wk": wk, "wv": wv, "bq": bq, "bk": bk, "bias": bias.reshape(2 * ROWS, BW),
        "ws1": arr("L0_ffn_Ws1"), "ws2": arr("L0_ffn_Ws2"), "w1": arr("L0_ffn_We1"), "w2": arr("L0_ffn_We2"),
        "wr": arr("L0_ffn_Wr"), "br": arr("L0_ffn_br"), "consts": c,
    }
    nc = bacc.Bacc("TRN2", target_bir_lowering=False, num_devices=1)
    args = [nc.dram_tensor(f"in_{n}", a.shape, mybir.dt.from_np(a.dtype), kind="ExternalInput").ap()
            for n, a in arrays.items()]
    out = nc.dram_tensor("out_0", (N, D), mybir.dt.float32, kind="ExternalOutput").ap()
    build(nc, *args, out)
    r = run_bass_kernel_spmd(nc, [{f"in_{n}": a for n, a in arrays.items()}], core_ids=[0])
    return r.results[0]["out_0"].reshape(B, S, D)
```

```python
import concourse.bass as bass
from concourse import mybir

P = 128
B, S, D = 16, 128, 256
H, HD = 16, 16
N = B * S
PAIRS = B // 2
E = 12
HR, HS = 3 * D, 2 * D
KC = D // P
TAU = 1.5
EPS = 1e-5
FILL = -1e30
TILES = N // P
SLOTS = (2 * N + (P - 1) * E + (E - 2)) // P
RING = 3
W1R, W2R = KC * 2 * HR, (HR // P) * D
W1S, W2S = KC * 2 * HS, (HS // P) * D
SLOT_W = 2 * (W1R + W2R)
VW = 2 * HD
ROWS = E + 2
BW = 2 * HR + D
SHARED_ROW, V_ROW = E, E + 1
C_ID, C_UP = 0, P
C_LOQ = 2 * P
C_LOB = C_LOQ + 1
C_ROW = C_LOB + 1
C_RANK = C_ROW + 1
C_SLOT = C_RANK + E
C_STEP = C_SLOT + SLOTS
C_ALL = C_STEP + E - 1


def build(nc, x_d, ctx_d, pad_d, sub_d, wq_d, wk_d, wv_d, bq_d, bk_d, bias_d, ws1_d, ws2_d, w1_d,
          w2_d, wr_d, br_d, const_d, out_d):
    f32, f32r = mybir.dt.float32, mybir.dt.float32r
    bf16, i32 = mybir.dt.bfloat16, mybir.dt.int32
    ALU, ACT, AX = mybir.AluOpType, mybir.ActivationFunctionType, mybir.AxisListType
    vec, act, pool, pe_ = nc.vector, nc.scalar, nc.gpsimd, nc.tensor

    xn2_dram = nc.dram_tensor("xn2_dram", (N, D), f32, kind="Internal").ap()
    rows_in = nc.dram_tensor("rows_in", (SLOTS * P, D), f32, kind="Internal").ap()
    rows_out = nc.dram_tensor("rows_out", (SLOTS * P, D), f32, kind="Internal").ap()

    at = [((nc.sbuf_base + 63) // 64) * 64]

    def size(shape, dt):
        n = 1
        for k in shape[1:]:
            n *= k
        return n * (2 if dt == bf16 else 4)

    offset_of = {}

    def put(name, shape, dt, where=at):
        t = nc.alloc_sbuf_tensor_at(name, shape, dt, offset=where[0])
        offset_of[name] = where[0]
        where[0] += (size(shape, dt) + 31) // 32 * 32
        return t

    x_all = put("x_all", [P, TILES * D], f32)
    xn2_all = put("xn2_all", [P, TILES * D], f32)
    const = put("const", [P, C_ALL], f32)
    bias_tab = put("bias_tab", [2 * ROWS, BW], f32r)
    ident_b = put("ident_b", [P, P], bf16)
    upper_b = put("upper_b", [P, P], bf16)
    ones_b = put("ones_b", [P, P], bf16)
    sel_v = put("sel_v", [2 * ROWS, P], f32r)
    sel_s = put("sel_s", [2 * ROWS, P], f32r)
    sel_down = put("sel_down", [2 * ROWS, P], f32r)
    wr = put("wr", [P, KC, E], f32)
    br = put("br", [P, E], f32)
    logits = put("logits", [P, TILES, E], f32)
    xrow = put("xrow", [P, D], f32)
    half = put("half", [P, 2], f32)
    eps = put("eps", [P, 2], f32)
    tick = put("tick", [P, 1], f32)
    ptick = put("ptick", [P, 1], f32)
    bn1 = put("bn1", [P, 2, 6], f32)
    mv1 = put("mv1", [P, 2, 2], f32)
    ve1 = put("ve1", [P, 2], f32)
    rs1 = put("rs1", [P, 2], f32)
    bn2 = put("bn2", [P, 2, 6], f32)
    mv2 = put("mv2", [P, 2, 2], f32)
    ve2 = put("ve2", [P, 2], f32)
    rs2 = put("rs2", [P, 2], f32)
    w_top = put("w_top", [P, 2, TILES], f32)
    idx_top = put("idx_top", [P, 2, TILES], i32)
    top = put("top", [P, 2, TILES], f32)
    ex = put("ex", [P, TILES], f32)
    tab_ring = put("tab_ring", [P, SLOTS], i32)
    tab_need = put("tab_need", [P, SLOTS], i32)
    tab_cum = put("tab_cum", [P, E], i32)
    sel_ind = put("sel_ind", [2 * ROWS, SLOTS], f32)
    stage1 = put("stage1", [P, W1R], f32)
    stage2 = put("stage2", [P, W2R], f32)
    ring = put("ring", [P, RING, SLOT_W], f32r)
    ring_at = at[0] - RING * SLOT_W * 4
    work_at = [at[0]]
    xTh = put("xTh", [P, KC, P], f32r)
    xTl = put("xTl", [P, KC, P], f32r)
    ag = [put(f"ag{u}", [P, 2, HR // 2], f32) for u in range(2)]
    hTh = [put(f"hTh{u}", [P, 3, P], f32r) for u in range(2)]
    hTl = [put(f"hTl{u}", [P, 3, P], f32r) for u in range(2)]
    y_row = put("y_row", [P, D], f32)
    own = [at[0]]
    pad_b = put("pad_b", [P, B * S], i32, own)
    mask_b = put("mask_b", [P, B, S], bf16, own)
    xn2p = put("xn2p", [P, 2, D], f32, own)
    cbuf = put("cbuf", [P, 2, D], f32, own)
    up_bias_s = put("up_bias_s", [P, 2, HS], f32, own)
    assert own[0] <= nc.sbuf_top, own[0] - nc.sbuf_top
    low = [ring_at]
    wqh = put("wqh", [P, KC, 512], f32r, low)
    wql = put("wql", [P, KC, 512], f32r, low)
    wkh = put("wkh", [P, KC, 512], f32r, low)
    wkl = put("wkl", [P, KC, 512], f32r, low)
    wvh = put("wvh", [P, KC, D], f32r, low)
    wvl = put("wvl", [P, KC, D], f32r, low)
    aTh = [put(f"aTh{i}", [P, KC, 256], f32r, low) for i in range(2)]
    aTl = [put(f"aTl{i}", [P, KC, 256], f32r, low) for i in range(2)]
    q_st = [put(f"q_st{i}", [P, 4, 256], f32r, low) for i in range(2)]
    k_hi = [put(f"k_hi{i}", [P, 4, 256], f32r, low) for i in range(2)]
    k_lo = [put(f"k_lo{i}", [P, 4, 256], f32r, low) for i in range(2)]
    v_sb = [put(f"v_sb{i}", [P, 2, H, VW], f32, low) for i in range(2)]
    prob = [put(f"prob{i}", [P, 2, 4, P], f32, low) for i in range(2)]
    probT = put("probT", [P, 2, 4, P], f32, low)
    assert low[0] <= ring_at + 2 * SLOT_W * 4, low[0] - ring_at - 2 * SLOT_W * 4
    wk1 = [work_at[0]]
    xn1 = put("xn1", [P, 2, D], f32, wk1)
    q_cut = put("q_cut", [P, 4, 256], f32r, wk1)
    bqs = put("bqs", [P, 4], f32, wk1)
    bqc = put("bqc", [P, 4], f32, wk1)
    bks = put("bks", [P, 4], f32, wk1)
    sub_b = put("sub_b", [P, S], i32, wk1)
    keep_s = put("keep_s", [P, S], f32, wk1)
    assert wk1[0] <= offset_of["hTh0"]
    wk1 = [offset_of["hTh0"]]
    att = put("att", [P, D], f32, wk1)
    rden = put("rden", [P, H], f32, wk1)
    nmax = put("nmax", [P, 2, 4], f32, wk1)
    xn2T = put("xn2T", [P, KC, 256], f32, wk1)
    outT = put("outT", [P, 4 * P], f32, wk1)
    assert wk1[0] <= offset_of["y_row"]
    assert wk1[0] <= at[0]
    pro = [offset_of["stage1"]]
    wq_raw = put("wq_raw", [P, KC, 512], f32, pro)
    wk_raw = put("wk_raw", [P, KC, 512], f32, pro)
    wv_raw = put("wv_raw", [P, KC, D], f32, pro)
    pr2 = [offset_of["prob0"]]
    bias_raw = put("bias_raw", [2 * ROWS, BW], f32, pr2)
    pr3 = [offset_of["xn2_all"]]
    bias_cut = put("bias_cut", [2 * ROWS, BW], f32r, pr3)
    keep = put("keep", [P, B, S], f32, pr3)
    rt = [offset_of["pad_b"]]
    lg = put("lg", [P, TILES, E], f32, rt)
    eq = put("eq", [P, TILES, E], f32, rt)
    pick1 = put("pick1", [P, TILES, E], f32, rt)
    pick2 = put("pick2", [P, TILES, E], f32, rt)
    chosen = put("chosen", [P, TILES, E], bf16, rt)
    pos = put("pos", [P, TILES, E], f32, rt)
    best = put("best", [P, TILES], f32, rt)
    cnt_i = put("cnt_i", [P, E], i32, rt)
    cnt_s = put("cnt_s", [P, E], i32, rt)
    tiles_e = put("tiles_e", [P, E], f32, rt)
    cum_e = put("cum_e", [P, E], f32, rt)
    base_e = put("base_e", [P, E], f32, rt)
    rank_sb = put("rank_sb", [P, (TILES + 1) * E], f32, rt)
    ones_e = put("ones_e", [P, E], f32, rt)
    past = put("past", [P, SLOTS, E - 1], f32, rt)
    past2 = put("past2", [P, SLOTS, E - 1], f32, rt)
    slot_e = put("slot_e", [P, SLOTS], f32, rt)
    slot_r = put("slot_r", [P, SLOTS], f32, rt)
    assert rt[0] <= nc.sbuf_top
    assert rt[0] <= offset_of["up_bias_s"]
    ub = [offset_of["pad_b"]]
    up_bias = put("up_bias", [P, RING, 2, HR], f32, ub)
    assert ub[0] <= nc.sbuf_top and offset_of["up_bias_s"] >= offset_of["up_bias"] + 2 * 2 * HR * 4
    ga = [ring_at + SLOT_W * 4]
    gath = put("gath", [P, TILES, 2, D], f32, ga)

    ident = const[:, C_ID:C_ID + P]

    ps_s = nc.alloc_psum_tensor("ps_s", [P, 4, 512], f32)
    ps_t = nc.alloc_psum_tensor("ps_t", [P, 2, 512], f32)
    ps_o = nc.alloc_psum_tensor("ps_o", [P, 512], f32)
    ps_x = nc.alloc_psum_tensor("ps_x", [P, 512], f32)

    step_bank = [ps_x[:, :], ps_t[:, 1, :]]

    def sem(name):
        return nc.alloc_semaphore(name)

    const_in, x_in, x_rest_in, ctx_in, wq_in, wk_in, wv_in = map(sem, (
        "const_in", "x_in", "x_rest_in", "ctx_in", "wq_in", "wk_in", "wv_in"))
    bias_in, mask_in, misc_in, zero_out, shared_in = map(sem, (
        "bias_in", "mask_in", "misc_in", "zero_out", "shared_in"))
    consts_ready, masks_ready, w_hi, w_ready, bias_cut_done, bias_ready = map(sem, (
        "consts_ready", "masks_ready", "w_hi", "w_ready", "bias_cut_done", "bias_ready"))
    scores_ready, shifted, maxed, exp_done, pt_ready, pt_copied, pv_done, normed = map(sem, (
        "scores_ready", "shifted", "maxed", "exp_done", "pt_ready", "pt_copied", "pv_done", "normed"))
    ot_copied, ot_ready = sem("ot_copied"), sem("ot_ready")
    added, idents_ready, setup_ready = sem("added"), sem("idents_ready"), sem("setup_ready")
    ranks_copied = sem("ranks_copied")
    router_in = sem("router_in")
    v_ones = sem("v_ones")
    xb_ready, xb_hi, xb_free, ln1_var, ln1_rs, ln2_var, ln2_rs, xn1_ready, xn2_ready, xn2_saved = map(sem, (
        "xb_ready", "xb_hi", "xb_free", "ln1_var", "ln1_rs", "ln2_var", "ln2_rs", "xn1_ready",
        "xn2_ready", "xn2_saved"))
    vstep, mstep, nstep, ln1_bn, pstep, pstep2, pconv = map(sem, (
        "vstep", "mstep", "nstep", "ln1_bn", "pstep", "pstep2", "pconv"))
    zero_ready = sem("zero_ready")
    chosen_ready, ranks_ready, tables_ready, rows_ready, scattered, ex_ready, gap_ready = map(sem, (
        "chosen_ready", "ranks_ready", "tables_ready", "rows_ready", "scattered", "ex_ready", "gap_ready"))
    xrow_in, xt_ready, xt_hi, xt_lo = map(sem, ("xrow_in", "xt_ready", "xt_hi", "xt_lo"))
    up_ready = [sem("up_ready0"), sem("up_ready1")]
    up_copied = [sem("up_copied0"), sem("up_copied1")]
    first_bias_in, up_bias_in = sem("first_bias_in"), sem("up_bias_in")
    gelu_done = [sem("gelu_done0"), sem("gelu_done1")]
    hid_done = [sem("hid_done0"), sem("hid_done1")]
    ht_ready = [sem("ht_ready0"), sem("ht_ready1")]
    ht_hi = [sem("ht_hi0"), sem("ht_hi1")]
    ht_lo = [sem("ht_lo0"), sem("ht_lo1")]
    y_ready, y_done, y_out, shared_bias_in, sel_down_ready = map(sem, (
        "y_ready", "y_done", "y_out", "shared_bias_in", "sel_down_ready"))
    raw1_in, raw2_in, conv_hi, converted = map(sem, ("raw1_in", "raw2_in", "conv_hi", "converted"))
    gathered = [sem(f"gathered{t}") for t in range(TILES)]
    combined, stored = sem("combined"), sem("stored")

    PLAN = [["cT", "xT", "k0"], ["v", "k1"], ["r", "q0"], ["q1", "l"]]
    PROJ = [s for unit in PLAN for s in unit if s not in "rl"]
    HI = [s for s in PROJ if s != "v"]

    def steps(n, first, last):
        return [s for s in PLAN[n] if (s not in "rl" or not first) and (s in "rl" or not last)]

    def before(p, n, k, first, last):
        base = len(PROJ) if first else 9 * p + 5
        return base + sum(len(steps(m, first, last)) for m in range(n)) + k

    def index_of(s, p, first, last):
        n = [s in unit for unit in PLAN].index(True)
        return before(p, n, steps(n, first, last).index(s), first, last)

    def each_pair(eng, body):
        body(0, 0, True, False)
        with eng.Fori(0, (PAIRS - 4) // 2) as i:
            body(i * 2 + 1, 1, False, False)
            body(i * 2 + 2, 0, False, False)
        body(PAIRS - 3, 1, False, False)
        body(PAIRS - 2, 0, False, False)
        body(PAIRS - 1, 1, False, True)

    UNITS = 4 * PAIRS
    BACK = 5
    FRONT = TILES - BACK
    B0 = FRONT + SLOTS
    BACK_PLACE = E % RING
    ROUTED_IN = 2
    RANKS_AT = 256
    PAIR_STEPS_END = 9 * (PAIRS - 1) + 5 + 2

    block = nc.Block()
    with block:

        @block.sync
        def _(sp):
            sp.dma_start(x_all[:, 0:2 * D].rearrange("p (t d) -> p t d", d=D),
                         x_d[0:2 * P, :].rearrange("(t p) d -> p t d", p=P)).then_inc(x_in, 16)
            sp.dma_start(cbuf[:, :, :], ctx_d[0:2 * P, :].rearrange("(t p) d -> p t d", p=P)).then_inc(ctx_in, 16)
            sp.dma_start(wk_raw[:, :, :], wk_d.rearrange("(c p) n -> p c n", p=P)).then_inc(wk_in, 16)
            sp.dma_start(wv_raw[:, :, :], wv_d.rearrange("(c p) n -> p c n", p=P)).then_inc(wv_in, 16)
            sp.dma_start(wq_raw[:, :, :], wq_d.rearrange("(c p) n -> p c n", p=P)).then_inc(wq_in, 16)
            sp.dma_start(sub_b[:, :], sub_d).then_inc(mask_in, 16)
            sp.dma_start(pad_b[:, :], pad_d.partition_broadcast(P)).then_inc(mask_in, 16)
            sp.dma_start(x_all[:, 2 * D:].rearrange("p (t d) -> p t d", d=D),
                         x_d[2 * P:, :].rearrange("(t p) d -> p t d", p=P)).then_inc(x_rest_in, 16)
            sp.dma_start(wr[:, :, :], wr_d.rearrange("(c p) n -> p c n", p=P)).then_inc(router_in, 16)
            sp.dma_start(br[:, :], br_d.partition_broadcast(P)).then_inc(router_in, 16)
            def load_ctx(pp):
                sp.dma_start(cbuf[:, :, :], ctx_d[bass.ds(pp * 2 * P, 2 * P), :]
                             .rearrange("(t p) d -> p t d", p=P)).then_inc(ctx_in, 16)

            sp.wait_ge(xb_ready, PROJ.index("cT") + 1)
            load_ctx(1)

            sp.wait_ge(w_ready, 3)
            sp.dma_start(stage1[:, 0:W1S].rearrange("p (c n) -> p c n", c=KC),
                         ws1_d.rearrange("(c p) n -> p c n", p=P)).then_inc(shared_in, 16)
            sp.dma_start(stage2[:, 0:W2S].rearrange("p (c n) -> p c n", n=D),
                         ws2_d.rearrange("(c p) n -> p c n", p=P)).then_inc(shared_in, 16)

            sp.dma_start(up_bias_s[:, :, :].rearrange("p a n -> p (a n)"),
                         bias_d[SHARED_ROW, 0:2 * HS].partition_broadcast(P)).then_inc(shared_bias_in, 16)
            sp.wait_ge(zero_ready, 1)
            sp.dma_start(rows_in.rearrange("(s p) d -> p s d", p=P),
                         y_row[:, :].rearrange("p (o d) -> p o d", o=1).broadcast_to([P, SLOTS, D])).then_inc(zero_out, 16)
            def save_xn2(q):
                sp.wait_ge(xn2_ready, q + 1)
                sp.dma_start(xn2_all[:, bass.ds(q * 2 * D, 2 * D)], xn2p[:, :, :].rearrange("p t d -> p (t d)")).then_inc(xn2_saved, 16)
                sp.dma_start(xn2_dram[bass.ds(q * 2 * P, 2 * P), :].rearrange("(t p) d -> p t d", p=P),
                             xn2p[:, :, :]).then_inc(xn2_saved, 16)

            def load_row(src, t, s):
                if not (isinstance(t, int) and t == 0):
                    sp.wait_ge(xt_ready, t)
                sp.dma_start(xrow[:, :], src[bass.ds(s * P, P), :]).then_inc(xrow_in, 16)

            def pair(p, par, first, last):
                if not last:
                    sp.wait_ge(xb_ready, index_of("cT", p, first, last) + 1)
                    load_ctx(p + 2)
                if not first:
                    save_xn2(p - 1)

            pair(0, 0, True, False)
            with sp.Fori(0, (PAIRS - 4) // 2) as i:
                pair(i * 2 + 1, 1, False, False)
                pair(i * 2 + 2, 0, False, False)
            pair(PAIRS - 3, 1, False, False)
            save_xn2(PAIRS - 3)
            save_xn2(PAIRS - 2)
            sp.wait_ge(xn2_saved, 32)
            load_row(xn2_dram, 0, 0)
            load_row(xn2_dram, 1, 1)
            save_xn2(PAIRS - 1)

            sp.wait_ge(xn2_saved, 32 * PAIRS)
            with sp.Fori(2, FRONT) as s:
                load_row(xn2_dram, s, s)
            sp.wait_ge(scattered, 16 * 2 * TILES)
            def store_y(s):
                sp.wait_ge(y_done, FRONT + s + 1)
                sp.dma_start(rows_out[bass.ds(s * P, P), :], y_row[:, :]).then_inc(y_out, 16)

            for s in range(3):
                load_row(rows_in, s + FRONT, s)
            with sp.Fori(3, SLOTS) as s:
                store_y(s - 3)
                load_row(rows_in, s + FRONT, s)
            for i in range(BACK):
                if i < 3:
                    store_y(SLOTS - 3 + i)
                load_row(xn2_dram, B0 + i, FRONT + i)
            for t in range(TILES):
                sp.wait_ge(combined, 2 * (t + 1))
                sp.dma_start(out_d[t * P:(t + 1) * P, :], x_all[:, t * D:(t + 1) * D]).then_inc(stored, 16)
            sp.wait_ge(stored, 16 * TILES)

        @block.tensor
        def _(pe):
            def transposes(dst, src, n):
                for c in range(KC):
                    for b in range(n):
                        last = pe_.transpose(dst[:, (c * n + b) * P:(c * n + b + 1) * P],
                                             src[:, b, c * P:(c + 1) * P], ident)
                return last

            def step(s, pp, par, idx, bank):
                if not (isinstance(idx, int) and idx < 2):
                    pe.wait_ge(xb_free, idx - 1)
                ps = step_bank[bank]
                if s == "xT":
                    pe.wait_ge(xn1_ready, pp + 1)
                    last = transposes(ps, xn1, 2)
                elif s == "cT":
                    pe.wait_ge(ctx_in, 16 * (pp + 1))
                    last = transposes(ps, cbuf, 2)
                elif s[0] in "qk":
                    wh, wl, a = (wqh, wql, 0) if s[0] == "q" else (wkh, wkl, 1)
                    for gg in range(2):
                        cols = slice((2 * int(s[1]) + gg) * P, (2 * int(s[1]) + gg + 1) * P)
                        n = 0
                        for w, t in ((wh, aTh), (wh, aTl), (wl, aTh)):
                            for c in range(KC):
                                last = pe_.matmul(ps[:, gg * 256:(gg + 1) * 256], w[:, c, cols], t[a][:, c, :],
                                                  start=n == 0, stop=n == 5)
                                n += 1
                else:
                    for b in range(2):
                        n = 0
                        for t, w in ((aTh, wvh), (aTh, wvl), (aTl, wvh)):
                            for c in range(KC):
                                pe_.matmul(ps[:, b * D:(b + 1) * D], t[1][:, c, b * P:(b + 1) * P], w[:, c, :],
                                           start=n == 0, stop=False)
                                n += 1
                        last = pe_.matmul(ps[:, b * D:(b + 1) * D], sel_v[:, :], bias_tab[:, 0:D],
                                          start=False, stop=True)
                last.then_inc(xb_ready, 1)

            def router(s, q, idx, bank):
                pe.wait_ge(xb_free, idx - (0 if isinstance(idx, int) and idx == PAIR_STEPS_END + 1 else 1))
                ps = step_bank[bank]
                if s == "r":
                    pe.wait_ge(xn2_ready, q + 1)
                    last = transposes(ps, xn2p, 2)
                else:
                    for b in range(2):
                        for c in range(KC):
                            last = pe_.matmul(ps[:, b * E:(b + 1) * E], xn2T[:, c, b * P:(b + 1) * P], wr[:, c, :],
                                              start=c == 0, stop=c == KC - 1)
                last.then_inc(xb_ready, 1)

            def scores(p, par, n):
                b, u = n // 2, n % 2
                U = p * 4 + n
                if not (isinstance(p, int) and p == 0 and n < 2):
                    pe.wait_ge(shifted, U - 1)
                for jj in range(2):
                    j = 2 * u + jj
                    pe_.matmul(ps_s[:, j, :].rearrange("p (g t) -> p g t", g=4), ident_b[:, :],
                               mask_b[:, bass.ds(p * 2 + b, 1), :].broadcast_to([P, 4, P]), start=True, stop=False)
                for jj in range(2):
                    j = 2 * u + jj
                    for g in range(4):
                        for k in (k_hi, k_lo):
                            last = pe_.matmul(ps_s[:, j, g * P:(g + 1) * P],
                                              q_st[par][32 * j:32 * j + 32, g, b * P:(b + 1) * P],
                                              k[par][32 * j:32 * j + 32, g, b * P:(b + 1) * P],
                                              start=False, stop=g == 3 and k is k_lo)
                last.then_inc(scores_ready, 1)

            def prob_transposes(U, n, jj):
                pe.wait_ge(exp_done, U + 1)
                if not (isinstance(U, int) and U == 0 and jj == 0):
                    pe.wait_ge(pt_copied, 2 * U + jj)
                for g in range(4):
                    last = pe_.transpose(ps_t[:, 0, g * P:(g + 1) * P], prob[n % 2][:, jj, g, :], ident)
                last.then_inc(pt_ready, 1)

            def values(U, n, par, batch, jj):
                b, u = n // 2, n % 2
                pe.wait_ge(pt_copied, 2 * U + jj + 1)
                if u == 0 and jj == 0 and not (isinstance(batch, int) and batch == 0):
                    pe.wait_ge(normed, batch)
                for g in range(4):
                    h = 4 * g + 2 * u + jj
                    j = 2 * u + jj
                    last = pe_.matmul(ps_o[32 * j:32 * j + VW, g * P:(g + 1) * P], v_sb[par][:, b, h, :],
                                      probT[:, jj, g, :], start=True, stop=True)
                last.then_inc(pv_done, 1)

            def out_transposes(batch):
                pe.wait_ge(ot_copied, batch + 1)
                for g in range(4):
                    last = pe_.transpose(ps_o[:, g * P:(g + 1) * P], outT[:, g * P:(g + 1) * P], ident)
                last.then_inc(ot_ready, 1)

            pe.wait_ge(const_in, 16)
            for k, s in enumerate(PROJ):
                if s == "xT":
                    pe.wait_ge(idents_ready, 1)
                if s == "k0":
                    pe.wait_ge(w_ready, 1)
                if s == "v":
                    pe.wait_ge(w_ready, 2)
                    pe.wait_ge(bias_ready, 1)
                if s == "q0":
                    pe.wait_ge(w_ready, 3)
                step(s, 0, 0, k, k % 2)
            pe.wait_ge(masks_ready, 1)
            pe.wait_ge(v_ones, 2)
            pe.wait_ge(router_in, 32)

            def pair(p, par, first, last):
                for n in range(4):
                    if n == 0:
                        pe.wait_ge(xb_free, before(p, 0, 0, first, last))
                    scores(p, par, n)
                    rest = list(enumerate(steps(n, first, last)))
                    prev = not (first and n == 0)
                    pn, ppar, pbatch = (n - 1) % 4, par if n else 1 - par, p * 2 + (n - 1) // 2

                    def next_step():
                        if rest:
                            k, st = rest.pop(0)
                            idx, bank = before(p, n, k, first, last), before(par, n, k, first, last) % 2
                            if st in ("r", "l"):
                                router(st, p - 1, idx, bank)
                            else:
                                step(st, p + 1, 1 - par, idx, bank)

                    if prev:
                        prob_transposes(p * 4 + n - 1, pn, 0)
                    next_step()
                    if prev:
                        prob_transposes(p * 4 + n - 1, pn, 1)
                        values(p * 4 + n - 1, pn, ppar, pbatch, 0)
                    next_step()
                    if prev:
                        values(p * 4 + n - 1, pn, ppar, pbatch, 1)
                    next_step()
                    if n % 2 == 0 and prev:
                        out_transposes(pbatch)

            each_pair(pe, pair)

            def up(t, s, u, routed, place):
                half_w = (HR if routed else HS) // 2
                w1 = W1R if routed else W1S
                full = 2 * (HR if routed else HS)
                if u == 0:
                    pe.wait_ge(xt_lo, t + 1)
                if not (isinstance(t, int) and t == 0):
                    pe.wait_ge(up_copied[u], t)
                for part in range(2):
                    out = ps_s[:, 2 * u + part, 0:half_w]
                    lo_col = part * (full // 2) + u * half_w
                    n = 0
                    for x, off in ((xTh, 0), (xTh, w1), (xTl, 0)):
                        for c in range(KC):
                            a = off + c * full + lo_col
                            last = pe_.matmul(out, x[:, c, :], weights(place, a, half_w), start=n == 0, stop=n == 5)
                            n += 1
                last.then_inc(up_ready[u], 1)

            def weights(place, a, width):
                return ring[:, bass.ds(place, 1), a:a + width].rearrange("p o n -> p (o n)")

            def hid_transposes(t, u, routed):
                nch = (HR if routed else HS) // 2 // P
                pe.wait_ge(hid_done[u], t + 1)
                if not (isinstance(t, int) and t == 0):
                    pe.wait_ge(ht_lo[u], t)
                for c in range(nch):
                    last = pe_.transpose(ps_t[:, u, c * P:(c + 1) * P], ag[u][:, 0, c * P:(c + 1) * P], ident)
                last.then_inc(ht_ready[u], 1)

            def x_transposes(t):
                pe.wait_ge(xrow_in, (t + 1) * 16)
                if not (isinstance(t, int) and t == 0):
                    pe.wait_ge(xt_lo, t)
                for c in range(KC):
                    last = pe_.transpose(ps_x[:, c * P:(c + 1) * P], xrow[:, c * P:(c + 1) * P], ident)
                last.then_inc(xt_ready, 1)

            def down(t, s, routed, place):
                nch = (HR if routed else HS) // 2 // P
                w1 = W1R if routed else W1S
                w2 = W2R if routed else W2S
                pe.wait_ge(ht_lo[0], t + 1)
                pe.wait_ge(ht_lo[1], t + 1)
                if routed:
                    pe.wait_ge(sel_down_ready, s + 1)
                if not (isinstance(t, int) and t == 0):
                    pe.wait_ge(y_done, t)
                n = 0
                for u in range(2):
                    for c in range(nch):
                        for h, off in ((hTh, 2 * w1), (hTh, 2 * w1 + w2), (hTl, 2 * w1)):
                            a = off + (u * nch + c) * D
                            pe_.matmul(ps_o[:, 0:D], h[u][:, c, :], weights(place, a, D), start=n == 0, stop=False)
                            n += 1
                sel = sel_down if routed else sel_s
                lo_col = 2 * HR if routed else 2 * HS
                pe_.matmul(ps_o[:, 0:D], sel[:, :], bias_tab[:, lo_col:lo_col + D], start=False, stop=True)\
                    .then_inc(y_ready, 1)

            def ranks():
                out = ps_x[:, RANKS_AT:RANKS_AT + (TILES + 1) * E]
                pe.wait_ge(chosen_ready, 1)
                pe.wait_ge(xt_lo, ROUTED_IN + 2)
                pe_.matmul(out[:, 0:TILES * E], upper_b[:, :], chosen[:, :, :].rearrange("p t e -> p (t e)"),
                           start=True, stop=False)
                for j in range(TILES - 1):
                    k = TILES - 1 - j
                    pe_.matmul(out[:, (j + 1) * E:TILES * E].rearrange("p (t e) -> p t e", e=E), ones_b[:, :],
                               chosen[:, j:j + 1, :].broadcast_to([P, k, E]), start=False, stop=j == TILES - 2)
                for j in range(TILES):
                    last = pe_.matmul(out[:, TILES * E:(TILES + 1) * E], ones_b[:, :], chosen[:, j, :],
                                      start=j == 0, stop=j == TILES - 1)
                last.then_inc(ranks_ready, 1)

            def tile(t, s, routed, place, prev, prev_routed=None, last=False):
                if prev is not None:
                    hid_transposes(t - 1, 0, prev_routed)
                up(t, s, 0, routed, place)
                if prev is not None:
                    hid_transposes(t - 1, 1, prev_routed)
                up(t, s, 1, routed, place)
                if not last:
                    x_transposes(t + 1)
                if prev is not None:
                    down(t - 1, s - 1, prev_routed, prev)

            def ring_place(s):
                return pe.value_load(tab_ring[0:1, bass.ds(s, 1)], min_val=0, max_val=RING - 1)

            def expert_ready(s):
                need = pe.value_load(tab_need[0:1, bass.ds(s, 1)], min_val=2, max_val=E + 1)
                pe.wait_ge(converted, need)

            SH = RING - 1
            TURN_S, TURN = 4, 5
            assert PAIR_STEPS_END % 2 == 0
            prob_transposes(UNITS - 1, 3, 0)
            pe.wait_ge(xb_free, PAIR_STEPS_END - 1)
            x_transposes(0)
            prob_transposes(UNITS - 1, 3, 1)
            for jj in range(2):
                values(UNITS - 1, 3, 1, B - 1, jj)
            pe.wait_ge(converted, 1)
            pe.wait_ge(shifted, UNITS)
            up(0, 0, 0, False, SH)
            out_transposes(B - 1)
            up(0, 0, 1, False, SH)
            router("r", PAIRS - 1, PAIR_STEPS_END, 0)
            router("l", PAIRS - 1, PAIR_STEPS_END + 1, 1)
            x_transposes(1)
            pe.wait_ge(xb_free, PAIR_STEPS_END + 2)
            for s in range(1, ROUTED_IN + 1):
                tile(s, s, False, SH, SH, False)
            ranks()
            pe.wait_ge(ranks_copied, 1)
            assert (FRONT - 1 - ROUTED_IN) % TURN_S == 0
            with pe.Fori(0, (FRONT - 1 - ROUTED_IN) // TURN_S) as i:
                for k in range(TURN_S):
                    s = i * TURN_S + (k + 1 + ROUTED_IN)
                    tile(s, s, False, SH, SH, False)

            pe.wait_ge(tables_ready, 1)
            pe.wait_ge(first_bias_in, 16)
            place = ring_place(0)
            expert_ready(0)
            tile(FRONT, 0, True, place, SH, False)
            turns = (SLOTS - 2) // TURN
            with pe.Fori(0, turns) as i:
                prev = ring_place(i * TURN)
                for k in range(TURN):
                    s = i * TURN + (k + 1)
                    place = ring_place(s)
                    expert_ready(s)
                    tile(s + FRONT, s, True, place, prev, True)
                    prev = place
            prev = ring_place(turns * TURN)
            for s in range(turns * TURN + 1, SLOTS):
                place = ring_place(s)
                expert_ready(s)
                tile(s + FRONT, s, True, place, prev, True)
                prev = place
            pe.wait_ge(converted, E + 2)
            tile(B0, SLOTS, False, BACK_PLACE, prev, True)
            for i in range(1, BACK):
                tile(B0 + i, 0, False, BACK_PLACE, BACK_PLACE, False, i == BACK - 1)
            hid_transposes(B0 + BACK - 1, 0, False)
            hid_transposes(B0 + BACK - 1, 1, False)
            down(B0 + BACK - 1, 0, False, BACK_PLACE)

        @block.scalar
        def _(sc):
            sc.dma_start(const[:, :], const_d).then_inc(const_in, 16)
            sc.dma_start(bias_raw[:, :], bias_d).then_inc(bias_in, 16)
            sc.dma_start(bks[:, :], bk_d).then_inc(misc_in, 16)
            sc.dma_start(bqs[:, :], bq_d).then_inc(misc_in, 16)
            sc.wait_ge(const_in, 16)
            act.activation(ident_b[:, :], ident, ACT.Identity)
            act.activation(upper_b[:, :], const[:, C_UP:C_UP + P], ACT.Identity).then_inc(idents_ready, 1)

            def weights_hi(hi, raw, loaded):
                sc.wait_ge(loaded, 16)
                act.activation(hi[:, :, :], raw[:, :, :], ACT.Identity).then_inc(w_hi, 1)

            def step(s, pp, par, idx, bank):
                ps = step_bank[bank]
                sc.wait_ge(xb_ready, idx + 1)
                if s in ("xT", "cT"):
                    act.activation(aTh[s == "cT"][:, :, :], ps[:, :].rearrange("p (c n) -> p c n", c=KC),
                                   ACT.Identity).then_inc(xb_hi, 1)
                elif s[0] in "qk":
                    for gg in range(2):
                        g = 2 * int(s[1]) + gg
                        src = ps[:, gg * 256:(gg + 1) * 256]
                        if s[0] == "q":
                            last = act.activation(q_cut[:, g, :], src, ACT.Identity, bias=bqc[:, g:g + 1],
                                                  scale=const[:, C_LOQ:C_LOQ + 1])
                        else:
                            last = act.activation(k_hi[par][:, g, :], src, ACT.Identity, bias=bks[:, g:g + 1])
                    last.then_inc(xb_hi, 1)
                else:
                    sc.wait_ge(xb_free, idx)
                    act.activation(v_sb[par][:, :, :, 0:HD],
                                   ps[:, :].rearrange("p (b h d) -> p b h d", b=2, h=H), ACT.Identity)\
                        .then_inc(xb_free, 1)

            def prob_copy(U, jj):
                sc.wait_ge(pt_ready, 2 * U + jj + 1)
                if not (isinstance(U, int) and U == 0):
                    sc.wait_ge(pv_done, 2 * U + jj - 1)
                act.activation(probT[:, jj, :, :], ps_t[:, 0, :].rearrange("p (g t) -> p g t", g=4),
                               ACT.Identity).then_inc(pt_copied, 1)

            def out_copy(batch):
                sc.wait_ge(pv_done, batch * 4 + 4)
                act.activation(outT[:, :], ps_o[:, :], ACT.Identity).then_inc(ot_copied, 1)

            def exp(U, n):
                sc.wait_ge(shifted, U + 1)
                act.activation(prob[n % 2][:, :, :, :], prob[n % 2][:, :, :, :], ACT.Exp, scale=1.0 / HD ** 0.5)\
                    .then_inc(exp_done, 1)

            def router(s, idx, bank):
                if s == "r":
                    ps = step_bank[bank]
                    sc.wait_ge(xb_ready, idx + 1)
                    sc.wait_ge(xb_free, idx)
                    act.activation(xn2T[:, :, :], ps[:, :].rearrange("p (c n) -> p c n", c=KC), ACT.Identity)\
                        .then_inc(xb_free, 1)

            for k, s in enumerate(PROJ):
                if k == 1:
                    weights_hi(wkh, wk_raw, wk_in)
                if s == "v":
                    weights_hi(wvh, wv_raw, wv_in)
                    weights_hi(wqh, wq_raw, wq_in)
                if s == "k0":
                    sc.wait_ge(misc_in, 32)
                if s == "q0":
                    sc.wait_ge(consts_ready, 1)
                step(s, 0, 0, k, k % 2)

            def pair(p, par, first, last):
                for n in range(4):
                    U = p * 4 + n - 1
                    rest = list(enumerate(steps(n, first, last)))
                    prev = not (first and n == 0)

                    def next_step():
                        if rest:
                            k, st = rest.pop(0)
                            idx, bank = before(p, n, k, first, last), before(par, n, k, first, last) % 2
                            if st in "rl":
                                router(st, idx, bank)
                            else:
                                step(st, p + 1, 1 - par, idx, bank)

                    if prev:
                        prob_copy(U, 0)
                    next_step()
                    if prev:
                        prob_copy(U, 1)
                    if n == 0:
                        next_step()
                    if n % 2 == 0 and prev:
                        out_copy(p * 2 + (n - 1) // 2)
                    exp(p * 4 + n, n)
                    next_step()
                    next_step()

            each_pair(sc, pair)
            def gelu(t, u, routed):
                half_w = (HR if routed else HS) // 2
                sc.wait_ge(up_copied[u], t + 1)
                act.activation(ag[u][:, 1, 0:half_w], ag[u][:, 1, 0:half_w], ACT.Gelu).then_inc(gelu_done[u], 1)

            def hid_hi(t, u, routed):
                nch = (HR if routed else HS) // 2 // P
                sc.wait_ge(ht_ready[u], t + 1)
                if not (isinstance(t, int) and t == 0):
                    sc.wait_ge(y_ready, t)
                act.activation(hTh[u][:, 0:nch, :], ps_t[:, u, 0:nch * P].rearrange("p (c n) -> p c n", c=nch),
                               ACT.Identity).then_inc(ht_hi[u], 1)

            def x_hi(t):
                sc.wait_ge(xt_ready, t + 1)
                if not (isinstance(t, int) and t == 0):
                    sc.wait_ge(up_ready[1], t)
                act.activation(xTh[:, :, :], ps_x[:, 0:D].rearrange("p (c n) -> p c n", c=KC), ACT.Identity)\
                    .then_inc(xt_hi, 1)

            def pick_down(s):
                if not (isinstance(s, int) and s == 0):
                    sc.wait_ge(y_ready, s + FRONT)
                act.activation(sel_down[:, :], sel_ind[:, bass.ds(s, 1)].broadcast_to([2 * ROWS, P]), ACT.Identity)\
                    .then_inc(sel_down_ready, 1)

            def tile(t, s, routed, prev_routed=None, last=False):
                if prev_routed is not None:
                    hid_hi(t - 1, 0, prev_routed)
                    hid_hi(t - 1, 1, prev_routed)
                    if prev_routed:
                        pick_down(s - 1)
                gelu(t, 0, routed)
                if not last:
                    x_hi(t + 1)
                gelu(t, 1, routed)

            prob_copy(UNITS - 1, 0)
            x_hi(0)
            prob_copy(UNITS - 1, 1)
            out_copy(B - 1)
            gelu(0, 0, False)
            router("r", PAIR_STEPS_END, 0)
            gelu(0, 1, False)
            x_hi(1)
            with sc.Fori(1, FRONT) as s:
                tile(s, s, False, False)
            sc.wait_ge(gap_ready, 1)
            act.activation(ex[:, :], ex[:, :], ACT.Exp).then_inc(ex_ready, 1)
            tile(FRONT, 0, True, False)
            sc.wait_ge(tables_ready, 1)
            with sc.Fori(1, SLOTS) as s:
                tile(s + FRONT, s, True, True)
            tile(B0, SLOTS, False, True)
            for i in range(1, BACK):
                tile(B0 + i, 0, False, False, i == BACK - 1)
            hid_hi(B0 + BACK - 1, 0, False)
            hid_hi(B0 + BACK - 1, 1, False)

        @block.vector
        def _(ve):
            own_steps = [0]

            def chain(ins):
                own_steps[0] += 1
                ins.then_inc(vstep, 1)
                ve.wait_ge(vstep, own_steps[0])

            def ln1_stats(pp):
                for b in range(2):
                    vec.bn_stats(bn1[:, b, :], x_all[:, bass.ds((pp * 2 + b) * D, D)]).then_inc(ln1_bn, 1)
                ve.wait_ge(ln1_bn, pp * 2 + 2)
                vec.memset(tick[:, :], 0.0)
                for b in range(2):
                    last = vec.bn_aggr(mv1[:, b, :], bn1[:, b, :])
                last.then_inc(ln1_var, 1)

            def ln1_apply(pp):
                ve.wait_ge(ln1_rs, pp + 1)
                for b in range(2):
                    last = vec.tensor_scalar(xn1[:, b, :], x_all[:, bass.ds((pp * 2 + b) * D, D)], mv1[:, b, 0:1],
                                             rs1[:, b:b + 1], ALU.subtract, ALU.mult)
                last.then_inc(xn1_ready, 1)

            vec.memset(half[:, :], -0.5)
            vec.memset(eps[:, :], EPS).then_inc(setup_ready, 1)
            vec.memset(y_row[:, :], 0.0).then_inc(zero_ready, 1)
            ve.wait_ge(x_in, 16)
            ln1_stats(0)
            vec.memset(ones_b[:, :], 1.0)
            ve.wait_ge(const_in, 16)
            for t, row in ((sel_v, V_ROW), (sel_s, SHARED_ROW)):
                vec.tensor_scalar(t[:, :], const[0:2 * ROWS, C_ROW:C_ROW + 1].broadcast_to([2 * ROWS, P]), float(row), None,
                                  ALU.is_equal)
            ve.wait_ge(bias_in, 16)
            vec.tensor_scalar(bias_cut[:, :], bias_raw[:, :], const[0:2 * ROWS, C_LOB:C_LOB + 1], None, ALU.mult)\
                .then_inc(bias_cut_done, 1)
            ln1_apply(0)
            ve.wait_ge(bias_cut_done, 1)
            vec.tensor_tensor(bias_tab[:, :], bias_raw[:, :], bias_cut[:, :].bitcast(f32), ALU.subtract)\
                .then_inc(bias_ready, 1)

            def weights_lo(lo, raw, hi, n):
                ve.wait_ge(w_hi, n + 1)
                vec.tensor_tensor(lo[:, :, :], raw[:, :, :], hi[:, :, :].bitcast(f32), ALU.subtract).then_inc(w_ready, 1)

            def step(s, pp, par, idx, hi_idx, bank):
                ps = step_bank[bank]
                if s in HI:
                    ve.wait_ge(xb_hi, hi_idx + 1)
                if s in ("xT", "cT"):
                    a = int(s == "cT")
                    vec.tensor_tensor(aTl[a][:, :, :], ps[:, :].rearrange("p (c n) -> p c n", c=KC),
                                      aTh[a][:, :, :].bitcast(f32), ALU.subtract).then_inc(xb_free, 1)
                elif s[0] in "qk":
                    for gg in range(2):
                        g = 2 * int(s[1]) + gg
                        src = ps[:, gg * 256:(gg + 1) * 256]
                        if s[0] == "q":
                            last = vec.scalar_tensor_tensor(q_st[par][:, g, :], src, bqs[:, g:g + 1],
                                                            q_cut[:, g, :].bitcast(f32), ALU.add, ALU.subtract)
                        else:
                            last = vec.scalar_tensor_tensor(k_lo[par][:, g, :], src, bks[:, g:g + 1],
                                                            k_hi[par][:, g, :].bitcast(f32), ALU.add, ALU.subtract)
                    last.then_inc(xb_free, 1)

            def router(s, q, idx, bank):
                ps = step_bank[bank]
                if s == "l":
                    ve.wait_ge(xb_ready, idx + 1)
                    vec.tensor_tensor(logits[:, bass.ds(q * 2, 2), :], ps[:, 0:2 * E].rearrange("p (t e) -> p t e", e=E),
                                      br[:, :].rearrange("p (o e) -> p o e", o=1).broadcast_to([P, 2, E]), ALU.add)\
                        .then_inc(xb_free, 1)

            for k, s in enumerate(PROJ):
                if s == "xT":
                    weights_lo(wkl, wk_raw, wkh, 0)
                if s == "k0":
                    ve.wait_ge(misc_in, 32)
                if s == "v":
                    weights_lo(wvl, wv_raw, wvh, 1)
                    weights_lo(wql, wq_raw, wqh, 2)
                    vec.tensor_scalar(bqc[:, :], bqs[:, :], const[:, C_LOQ:C_LOQ + 1], None, ALU.mult)\
                        .then_inc(consts_ready, 1)
                step(s, 0, 0, k, HI.index(s) if s in HI else 0, k % 2)
                if s == "v":
                    ve.wait_ge(mask_in, 32)
                    ve.wait_ge(router_in, 32)
                    vec.tensor_scalar(keep[:, :, :].rearrange("p b t -> p (b t)"), pad_b[:, :], 0.0, None, ALU.not_equal)\
                        .then_inc(mstep, 1)
                    vec.tensor_scalar(keep_s[:, :], sub_b[:, :], 0.0, None, ALU.not_equal).then_inc(mstep, 1)
                    ve.wait_ge(mstep, 2)
                    vec.tensor_tensor(keep[:, :, :], keep[:, :, :],
                                      keep_s[:, :].rearrange("p (o t) -> p o t", o=1).broadcast_to([P, B, S]), ALU.mult)\
                        .then_inc(mstep, 1)
                    ve.wait_ge(mstep, 3)
                    vec.tensor_scalar(mask_b[:, :, :], keep[:, :, :], -FILL, FILL, ALU.mult, ALU.add).then_inc(masks_ready, 1)
                if s == "k1":
                    for par in range(2):
                        vec.memset(v_sb[par][:, :, :, HD + 1:VW], 0.0)
                        vec.memset(v_sb[par][:, :, :, HD:HD + 1], 1.0).then_inc(v_ones, 1)
                    ve.wait_ge(x_rest_in, 16)
                    ln1_stats(1)
                    ln1_apply(1)

            def softmax_shift(U, n, between=None):
                u = n % 2
                ve.wait_ge(scores_ready, U + 1)
                src = ps_s[:, 2 * u:2 * u + 2, :].rearrange("p j (g t) -> p j g t", g=4)
                if not (isinstance(U, int) and U == 0):
                    ve.wait_ge(shifted, U)
                vec.tensor_reduce(nmax[:, :, :], src, AX.X, ALU.max, negate=True).then_inc(maxed, 1)
                if between:
                    between()
                ve.wait_ge(maxed, U + 1)
                if not (isinstance(U, int) and U < 2):
                    ve.wait_ge(pt_ready, 2 * (U - 1))
                vec.tensor_tensor(prob[n % 2][:, :, :, :], src,
                                  nmax[:, :, :].rearrange("p j (g o) -> p j g o", o=1).broadcast_to([P, 2, 4, P]), ALU.add)\
                    .then_inc(shifted, 1)

            def norm(p, b):
                ve.wait_ge(ot_ready, p * 2 + b + 1)
                o = ps_o[:, :].rearrange("p (h d) -> p h d", d=VW)
                vec.reciprocal(rden[:, :], o[:, :, HD]).then_inc(nstep, 1)
                ve.wait_ge(nstep, (p * 2 + b) * 2 + 1)
                vec.tensor_tensor(att[:, :].rearrange("p (h d) -> p h d", d=HD), o[:, :, 0:HD],
                                  rden[:, :].rearrange("p (h o) -> p h o", o=1).broadcast_to([P, H, HD]), ALU.mult)\
                    .then_inc(normed, 1)

            def residual(p, b):
                ve.wait_ge(normed, p * 2 + b + 1)
                xs = x_all[:, bass.ds((p * 2 + b) * D, D)]
                vec.tensor_tensor(xs, xs, att[:, :], ALU.add).then_inc(added, 1)
                ve.wait_ge(added, p * 2 + b + 1)
                vec.memset(tick[:, :], 0.0)
                vec.bn_stats(bn2[:, b, :], xs).then_inc(nstep, 1)
                if b == 1:
                    ve.wait_ge(nstep, (p * 2 + b) * 2 + 2)
                    vec.memset(tick[:, :], 0.0)
                    for i in range(2):
                        last = vec.bn_aggr(mv2[:, i, :], bn2[:, i, :])
                    last.then_inc(ln2_var, 1)

            def ln2_apply(q):
                ve.wait_ge(ln2_rs, q + 1)
                if not (isinstance(q, int) and q == 0):
                    ve.wait_ge(xn2_saved, q * 32)
                for b in range(2):
                    last = vec.tensor_scalar(xn2p[:, b, :], x_all[:, bass.ds((q * 2 + b) * D, D)], mv2[:, b, 0:1],
                                             rs2[:, b:b + 1], ALU.subtract, ALU.mult)
                last.then_inc(xn2_ready, 1)

            def pair(p, par, first, last):
                for n in range(4):
                    todo = list(enumerate(steps(n, first, last)))

                    def next_step():
                        k, st = todo.pop(0)
                        idx = before(p, n, k, first, last)
                        bank = before(par, n, k, first, last) % 2
                        if st in ("r", "l"):
                            router(st, p - 1, idx, bank)
                        else:
                            step(st, p + 1, 1 - par, idx, (p + 1) * len(HI) + (HI.index(st) if st in HI else 0), bank)

                    softmax_shift(p * 4 + n, n, next_step if n == 0 and todo else None)
                    if n == 3:
                        residual(p, 0)
                    if n == 1 and not first:
                        residual(p - 1, 1)
                    further = not last and not (isinstance(p, int) and p + 2 >= PAIRS)
                    if n == 1 and not first:
                        ln2_apply(p - 1)
                    if n == 2 and further:
                        ln1_stats(p + 2)
                    if n == 2:
                        norm(p, 0)
                    while todo:
                        next_step()
                    if n == 0 and not first:
                        norm(p - 1, 1)
                    if n == 3 and further:
                        ve.wait_ge(xb_ready, index_of("xT", p, first, last) + 1)
                        ln1_apply(p + 2)

            each_pair(ve, pair)
            three, wide = [P, TILES, E], [P, SLOTS, E - 1]

            def over_experts(a):
                return a.rearrange("p (t o) -> p t o", o=1).broadcast_to(three)

            def over_tiles(a):
                return a.rearrange("p (o e) -> p o e", o=1).broadcast_to(wide)

            rank = const[:, C_RANK:C_RANK + E].rearrange("p (o e) -> p o e", o=1).broadcast_to(three)

            def choose(k, pick):
                if k == 0:
                    chain(vec.tensor_scalar(lg[:, :, :], logits[:, :, :], 1.0 / TAU, None, ALU.mult))
                chain(vec.tensor_reduce(top[:, k, :], lg[:, :, :], AX.X, ALU.max))
                chain(vec.tensor_tensor(eq[:, :, :], lg[:, :, :], over_experts(top[:, k, :]), ALU.is_equal))
                chain(vec.tensor_tensor(eq[:, :, :], eq[:, :, :], rank, ALU.mult))
                chain(vec.tensor_reduce(best[:, :], eq[:, :, :], AX.X, ALU.max))
                chain(vec.tensor_tensor(pick[:, :, :], rank, over_experts(best[:, :]), ALU.is_equal))
                if k == 0:
                    chain(vec.scalar_tensor_tensor(lg[:, :, :], pick[:, :, :], FILL, lg[:, :, :], ALU.mult, ALU.add))
                else:
                    vec.tensor_tensor(ex[:, :], top[:, 1, :], top[:, 0, :], ALU.subtract).then_inc(gap_ready, 1)
                    vec.tensor_tensor(chosen[:, :, :], pick1[:, :, :], pick2[:, :, :], ALU.add).then_inc(chosen_ready, 1)

            def first_rows():
                ve.wait_ge(ranks_ready, 1)
                vec.tensor_copy(rank_sb[:, :], ps_x[:, RANKS_AT:RANKS_AT + (TILES + 1) * E]).then_inc(ranks_copied, 1)
                vec.memset(ones_e[:, :], 1.0)
                ve.wait_ge(ranks_copied, 1)
                chain(vec.tensor_scalar(cnt_i[:, :], rank_sb[:, TILES * E:], float(P - 1), None, ALU.add))
                chain(vec.tensor_scalar(cnt_s[:, :], cnt_i[:, :], 7, None, ALU.logical_shift_right))
                chain(vec.tensor_scalar(tiles_e[:, :], cnt_s[:, :], 1.0, None, ALU.max))
                chain(vec.tensor_tensor_scan(cum_e[:, :], ones_e[:, :], tiles_e[:, :], 0.0, ALU.mult, ALU.add))
                chain(vec.tensor_tensor(base_e[:, :], cum_e[:, :], tiles_e[:, :], ALU.subtract))
                chain(vec.tensor_scalar(base_e[:, :], base_e[:, :], float(P), None, ALU.mult))

            def row_numbers(k, pick):
                if k == 0:
                    chain(vec.tensor_tensor(pos[:, :, :], rank_sb[:, 0:TILES * E].rearrange("p (t e) -> p t e", e=E),
                                            base_e[:, :].rearrange("p (o e) -> p o e", o=1).broadcast_to(three), ALU.add))
                chain(vec.tensor_tensor(eq[:, :, :], pos[:, :, :], pick[:, :, :], ALU.mult))
                chain(vec.tensor_reduce(best[:, :], eq[:, :, :], AX.X, ALU.add))
                last = vec.tensor_copy(idx_top[:, k, :], best[:, :])
                if k == 0:
                    chain(last)
                else:
                    last.then_inc(rows_ready, 1)

            def tile_tables():
                vec.tensor_scalar(tab_cum[:, :], cum_e[:, :], float(FRONT), None, ALU.add)
                chain(vec.tensor_tensor(past[:, :, :],
                                        const[:, C_SLOT:C_SLOT + SLOTS].rearrange("p (s o) -> p s o", o=1).broadcast_to(wide),
                                        over_tiles(cum_e[:, 0:E - 1]), ALU.is_ge))
                chain(vec.tensor_reduce(slot_e[:, :], past[:, :, :], AX.X, ALU.add))
                chain(vec.tensor_tensor(past2[:, :, :], past[:, :, :], over_tiles(const[:, C_STEP:C_STEP + E - 1]), ALU.mult))
                chain(vec.tensor_reduce(slot_r[:, :], past2[:, :, :], AX.X, ALU.add))
                vec.tensor_copy(tab_ring[:, :], slot_r[:, :])
                vec.tensor_scalar(tab_need[:, :], slot_e[:, :], 2.0, None, ALU.add)
                vec.tensor_scalar(sel_ind[:, :], slot_e[0:2 * ROWS, :], const[0:2 * ROWS, C_ROW:C_ROW + 1], None,
                                  ALU.is_equal).then_inc(tables_ready, 1)

            def choice_weights():
                ve.wait_ge(ex_ready, 1)
                chain(vec.tensor_scalar(top[:, 0, :], ex[:, :], 1.0, None, ALU.add))
                chain(vec.reciprocal(w_top[:, 0, :], top[:, 0, :]))
                chain(vec.tensor_tensor(w_top[:, 1, :], w_top[:, 0, :], ex[:, :], ALU.mult))

            def add_bias(t, u, routed, place):
                half_w = (HR if routed else HS) // 2
                cols = slice(u * half_w, (u + 1) * half_w)
                if routed:
                    bias = up_bias[:, bass.ds(place, 1), :, cols].rearrange("p o a n -> p (o a) n")
                elif place is not None:
                    bias = up_bias[:, place, :, cols]
                else:
                    bias = up_bias_s[:, :, cols]
                ve.wait_ge(up_ready[u], t + 1)
                if not (isinstance(t, int) and t == 0):
                    ve.wait_ge(ht_ready[u], t)
                vec.tensor_tensor(ag[u][:, :, 0:half_w], ps_s[:, 2 * u:2 * u + 2, 0:half_w], bias, ALU.add)\
                    .then_inc(up_copied[u], 1)

            def gate(t, u, routed):
                half_w = (HR if routed else HS) // 2
                ve.wait_ge(gelu_done[u], t + 1)
                vec.tensor_tensor(ag[u][:, 0, 0:half_w], ag[u][:, 0, 0:half_w], ag[u][:, 1, 0:half_w], ALU.mult)\
                    .then_inc(hid_done[u], 1)

            def hid_lo(t, u, routed):
                nch = (HR if routed else HS) // 2 // P
                ve.wait_ge(ht_hi[u], t + 1)
                vec.tensor_tensor(hTl[u][:, 0:nch, :], ps_t[:, u, 0:nch * P].rearrange("p (c n) -> p c n", c=nch),
                                  hTh[u][:, 0:nch, :].bitcast(f32), ALU.subtract).then_inc(ht_lo[u], 1)

            def x_lo(t):
                ve.wait_ge(xt_hi, t + 1)
                vec.tensor_tensor(xTl[:, :, :], ps_x[:, 0:D].rearrange("p (c n) -> p c n", c=KC),
                                  xTh[:, :, :].bitcast(f32), ALU.subtract).then_inc(xt_lo, 1)

            def y_copy(t, s, routed):
                ve.wait_ge(y_ready, t + 1)
                if routed:
                    if not (isinstance(s, int) and s == 0):
                        ve.wait_ge(y_out, 16 * s)
                    vec.tensor_copy(y_row[:, :], ps_o[:, 0:D]).then_inc(y_done, 1)
                else:
                    a = x_all[:, bass.ds(s * D, D)]
                    vec.tensor_tensor(a, ps_o[:, 0:D], a, ALU.add).then_inc(y_done, 1)

            def tile(t, s, routed, prev_routed=None, last=False, place=None, prev_s=None):
                if routed:
                    place = ve.value_load(tab_ring[0:1, bass.ds(s, 1)], min_val=0, max_val=RING - 1)
                if prev_routed is not None:
                    hid_lo(t - 1, 0, prev_routed)
                add_bias(t, 0, routed, place)
                if prev_routed is not None:
                    hid_lo(t - 1, 1, prev_routed)
                gate(t, 0, routed)
                if not last:
                    x_lo(t + 1)
                add_bias(t, 1, routed, place)
                gate(t, 1, routed)
                if prev_routed is not None:
                    y_copy(t - 1, s - 1 if prev_s is None else prev_s, prev_routed)

            x_lo(0)
            ve.wait_ge(shared_bias_in, 16)
            add_bias(0, 0, False, None)
            norm(PAIRS - 1, 1)
            residual(PAIRS - 1, 1)
            add_bias(0, 1, False, None)
            ln2_apply(PAIRS - 1)
            gate(0, 0, False)
            router("l", PAIRS - 1, PAIR_STEPS_END + 1, 1)
            gate(0, 1, False)
            x_lo(1)
            ve.wait_ge(xb_free, PAIR_STEPS_END + 2)
            choose(0, pick1)
            tile(1, 1, False, False)
            choose(1, pick2)
            for s in range(2, ROUTED_IN + 1):
                tile(s, s, False, False)
            first_rows()
            row_numbers(0, pick1)
            row_numbers(1, pick2)
            tile(ROUTED_IN + 1, ROUTED_IN + 1, False, False)
            tile_tables()
            with ve.Fori(ROUTED_IN + 2, FRONT) as s:
                tile(s, s, False, False)
            ve.wait_ge(tables_ready, 1)
            tile(FRONT, 0, True, False, prev_s=FRONT - 1)
            choice_weights()
            with ve.Fori(1, SLOTS) as s:
                tile(s + FRONT, s, True, True)

            def combine(t):
                ve.wait_ge(gathered[t], 32)
                if t >= FRONT:
                    ve.wait_ge(y_done, B0 + t - FRONT + 1)
                a = x_all[:, t * D:(t + 1) * D]
                for k in range(2):
                    vec.scalar_tensor_tensor(a, gath[:, t, k, :], w_top[:, k, t:t + 1], a, ALU.mult, ALU.add)\
                        .then_inc(combined, 1)
                    ve.wait_ge(combined, 2 * t + k + 1)

            for i in range(BACK):
                tile(B0 + i, FRONT + i, False, i == 0, i == BACK - 1, place=BACK_PLACE,
                     prev_s=SLOTS - 1 if i == 0 else FRONT + i - 1)
                if i >= 2:
                    for t in range(2 * (i - 2), 2 * (i - 1)):
                        combine(t)
            hid_lo(B0 + BACK - 1, 0, False)
            hid_lo(B0 + BACK - 1, 1, False)
            y_copy(B0 + BACK - 1, TILES - 1, False)
            for t in range(2 * (BACK - 2), TILES):
                combine(t)

        @block.gpsimd
        def _(gp):
            def rstd(var_sem, out_sem, mv, ve_t, rs_t, q, step_sem):
                gp.wait_ge(var_sem, q + 1)
                pool.tensor_tensor(ve_t[:, :], mv[:, :, 1], eps[:, :], ALU.add).then_inc(step_sem, 1)
                gp.wait_ge(step_sem, q + 1)
                pool.tensor_tensor(rs_t[:, :], ve_t[:, :], half[:, :], ALU.pow).then_inc(out_sem, 1)

            def convert(src, hi_ap, lo_ap, count):
                pool.tensor_scalar(hi_ap, src, 1.0, 0.0, ALU.mult, ALU.add).then_inc(conv_hi, 1)
                gp.wait_ge(conv_hi, count)
                return pool.tensor_tensor(lo_ap, src, hi_ap.bitcast(f32), ALU.subtract)

            gp.wait_ge(setup_ready, 1)
            rstd(ln1_var, ln1_rs, mv1, ve1, rs1, 0, pstep)
            rstd(ln1_var, ln1_rs, mv1, ve1, rs1, 1, pstep)
            gp.wait_ge(shared_in, 32)
            SH = RING - 1
            convert(stage1[:, 0:W1S], ring[:, SH, 0:W1S], ring[:, SH, W1S:2 * W1S], 1)
            convert(stage2[:, 0:W2S], ring[:, SH, 2 * W1S:2 * W1S + W2S],
                    ring[:, SH, 2 * W1S + W2S:2 * W1S + 2 * W2S], 2).then_inc(converted, 1)

            def load_raw1(e):
                gp.dma_start(stage1[:, :].rearrange("p (c n) -> p c n", c=KC),
                             w1_d[e, :, :].rearrange("(c p) n -> p c n", p=P)).then_inc(raw1_in, 16)

            def load_raw2(e):
                gp.dma_start(stage2[:, :].rearrange("p (c n) -> p c n", n=D),
                             w2_d[e, :, :].rearrange("(c p) n -> p c n", p=P)).then_inc(raw2_in, 16)

            gp.wait_ge(converted, 1)
            load_raw1(0)
            load_raw2(0)

            def pair(p, par, first, last):
                if not first:
                    rstd(ln2_var, ln2_rs, mv2, ve2, rs2, p - 1, pstep2)
                if not last and not (isinstance(p, int) and p + 2 >= PAIRS):
                    rstd(ln1_var, ln1_rs, mv1, ve1, rs1, p + 2, pstep)

            each_pair(gp, pair)
            rstd(ln2_var, ln2_rs, mv2, ve2, rs2, PAIRS - 1, pstep2)

            def load_up_bias(e):
                gp.dma_start(up_bias[:, e % RING, :, :].rearrange("p a n -> p (a n)"),
                             bias_d[e, 0:2 * HR].partition_broadcast(P))\
                    .then_inc(up_bias_in if e else first_bias_in, 16)

            def expert(e):
                r = e % RING
                if e > 0:
                    load_up_bias(e)
                gp.wait_ge(raw1_in, 16 * (e + 1))
                convert(stage1[:, :], ring[:, r, 0:W1R], ring[:, r, W1R:2 * W1R], 2 * e + 3).then_inc(pconv, 1)
                gp.wait_ge(pconv, e + 1)
                if e + 1 < E:
                    load_raw1(e + 1)
                else:
                    gp.dma_start(stage1[:, 0:W1S].rearrange("p (c n) -> p c n", c=KC),
                                 ws1_d.rearrange("(c p) n -> p c n", p=P)).then_inc(raw1_in, 16)
                gp.wait_ge(raw2_in, 16 * (e + 1))
                if e > 0:
                    gp.wait_ge(up_bias_in, 16 * e)
                convert(stage2[:, :], ring[:, r, 2 * W1R:2 * W1R + W2R], ring[:, r, 2 * W1R + W2R:], 2 * e + 4)\
                    .then_inc(converted, 1)
                gp.wait_ge(converted, e + 2)
                if e + 1 < E:
                    load_raw2(e + 1)
                else:
                    gp.dma_start(stage2[:, 0:W2S].rearrange("p (c n) -> p c n", n=D),
                                 ws2_d.rearrange("(c p) n -> p c n", p=P)).then_inc(raw2_in, 16)

            gp.wait_ge(pv_done, 2 * UNITS)
            gp.wait_ge(normed, B)
            gp.wait_ge(xb_free, PAIR_STEPS_END + 2)
            expert(0)
            gp.wait_ge(rows_ready, 1)
            gp.wait_ge(zero_out, 16)
            gp.wait_ge(xn2_saved, 32 * PAIRS)
            for t in range(TILES):
                for k in range(2):
                    gp.indirect_dma_start(
                        out=rows_in, out_offset=bass.IndirectOffsetOnAxis(ap=idx_top[:, k, t:t + 1], axis=0),
                        in_=xn2_all[:, t * D:(t + 1) * D], in_offset=None).then_inc(scattered, 16)
            gp.wait_ge(tables_ready, 1)
            load_up_bias(0)
            expert(1)
            for e in range(2, E):
                if e == 2:
                    gp.wait_ge(y_done, FRONT)
                else:
                    done = gp.value_load(tab_cum[0:1, e - RING:e - RING + 1], min_val=1, max_val=SLOTS + FRONT)
                    gp.wait_ge(y_done, done)
                    pool.tensor_tensor(ptick[:, :], half[:, 0:1], half[:, 0:1], ALU.add)
                expert(e)
            done = gp.value_load(tab_cum[0:1, E - RING:E - RING + 1], min_val=1, max_val=SLOTS + FRONT)
            gp.wait_ge(y_done, done)
            pool.tensor_tensor(ptick[:, :], half[:, 0:1], half[:, 0:1], ALU.add)
            gp.dma_start(up_bias[:, BACK_PLACE, :, 0:HS],
                         bias_d[SHARED_ROW, 0:2 * HS].rearrange("(a n) -> a n", a=2).partition_broadcast(P))\
                .then_inc(up_bias_in, 16)
            gp.wait_ge(raw1_in, 16 * (E + 1))
            convert(stage1[:, 0:W1S], ring[:, BACK_PLACE, 0:W1S], ring[:, BACK_PLACE, W1S:2 * W1S], 2 * E + 3)
            gp.wait_ge(raw2_in, 16 * (E + 1))
            gp.wait_ge(up_bias_in, 16 * E)
            convert(stage2[:, 0:W2S], ring[:, BACK_PLACE, 2 * W1S:2 * W1S + W2S],
                    ring[:, BACK_PLACE, 2 * W1S + W2S:2 * W1S + 2 * W2S], 2 * E + 4).then_inc(converted, 1)
            gp.wait_ge(y_done, FRONT + SLOTS)
            gp.wait_ge(y_out, 16 * SLOTS)
            for t in range(TILES):
                for k in range(2):
                    gp.indirect_dma_start(
                        out=gath[:, t, k, :], out_offset=None, in_=rows_out,
                        in_offset=bass.IndirectOffsetOnAxis(ap=idx_top[:, k, t:t + 1], axis=0))\
                        .then_inc(gathered[t], 16)


def kernel(**inputs):
    import numpy as np
    import concourse.bacc as bacc
    from concourse import mybir
    from concourse.bass_utils import run_bass_kernel_spmd

    def arr(name):
        return np.ascontiguousarray(inputs[name])

    def heads(w):
        v = w.reshape(w.shape[:-1] + (4, 4, 1, HD))
        return np.ascontiguousarray(np.broadcast_to(v, w.shape[:-1] + (4, 4, 2, HD)))

    wq = heads(arr("L0_xattn_Wq").T).reshape(D, 512)
    wk = heads(arr("L0_xattn_Wk").T).reshape(D, 512)
    bq = np.ascontiguousarray(heads(arr("L0_xattn_bq")).reshape(4, P).T)
    bk = np.ascontiguousarray(heads(arr("L0_xattn_bk")).reshape(4, P).T)
    wv = np.ascontiguousarray(arr("L0_xattn_Wv").T)
    bias = np.zeros((2, ROWS, BW), np.float32)
    bias[:, :E, :2 * HR] = arr("L0_ffn_be1")
    bias[:, :E, 2 * HR:] = arr("L0_ffn_be2")
    bias[:, SHARED_ROW, :2 * HS] = arr("L0_ffn_bs1")
    bias[:, SHARED_ROW, 2 * HS:2 * HS + D] = arr("L0_ffn_bs2")
    bias[:, V_ROW, :D] = arr("L0_xattn_bv")
    c = np.zeros((P, C_ALL), np.float32)
    c[:, C_ID:C_ID + P] = np.eye(P)
    c[:, C_UP:C_UP + P] = np.triu(np.ones((P, P)), 1)
    c[:, C_LOQ] = np.arange(P) % 32 >= HD
    c[:, C_LOB] = np.arange(P) >= ROWS
    c[:, C_ROW] = np.arange(P) % ROWS
    c[:, C_RANK:C_RANK + E] = E - np.arange(E)
    c[:, C_SLOT:C_SLOT + SLOTS] = np.arange(SLOTS)
    c[:, C_STEP:C_STEP + E - 1] = (np.arange(E - 1) + 1) % RING - np.arange(E - 1) % RING
    arrays = {
        "x": arr("x").reshape(N, D), "ctx": arr("ctx_1024").reshape(N, D),
        "pad": arr("mask_Bx1x1xS2_ik0").reshape(B * S).astype(np.int32),
        "sub": arr("mask_1x1xSxS2_ik0").reshape(S, S).astype(np.int32),
        "wq": wq, "wk": wk, "wv": wv, "bq": bq, "bk": bk, "bias": bias.reshape(2 * ROWS, BW),
        "ws1": arr("L0_ffn_Ws1"), "ws2": arr("L0_ffn_Ws2"), "w1": arr("L0_ffn_We1"), "w2": arr("L0_ffn_We2"),
        "wr": arr("L0_ffn_Wr"), "br": arr("L0_ffn_br"), "consts": c,
    }
    nc = bacc.Bacc("TRN2", target_bir_lowering=False, num_devices=1)
    args = [nc.dram_tensor(f"in_{n}", a.shape, mybir.dt.from_np(a.dtype), kind="ExternalInput").ap()
            for n, a in arrays.items()]
    out = nc.dram_tensor("out_0", (N, D), mybir.dt.float32, kind="ExternalOutput").ap()
    build(nc, *args, out)
    r = run_bass_kernel_spmd(nc, [{f"in_{n}": a for n, a in arrays.items()}], core_ids=[0])
    return r.results[0]["out_0"].reshape(B, S, D)
```
